# Optimizing a Trainium2 kernel written in Bass

```python
import numpy as np
import jax
import jax.numpy as jnp

def _softmax(x, axis=-1):
    return jax.nn.softmax(x, axis=axis)

def _gelu(x):
    return jax.nn.gelu(x, approximate=True)

def _silu(x):
    return jax.nn.silu(x)

def _sigmoid(x):
    return jax.nn.sigmoid(x)

def _layernorm(x, axis=-1, eps=1e-05):
    m = jnp.mean(x, axis=axis, keepdims=True)
    v = jnp.var(x, axis=axis, keepdims=True)
    return (x - m) / jnp.sqrt(v + eps)

def _scatter_add(tgt, idx, src, axis=0):
    return tgt.at[idx].add(src)

def _segment_sum(src, seg, n):
    return jax.ops.segment_sum(src, seg, n)
kernel_name = 'mk_seq_preln_d2_jaxref_r4_f58955'

def setup_inputs(seed: int=0):
    np.random.seed(seed)
    _w = jnp.asarray

    def _L0_attn_setup():
        import jax, jax.numpy as jnp
        import numpy as np
        from jax.scipy.linalg import solve_triangular
        B, T, D = (2, 1024, 256)
        HEAD_DIM = 128
        CHUNK = 64

        def _forward(out, W_write, W_read, W_alpha, W_beta, A_log, dt_bias):
            Bs, Ts, Ds = out.shape
            d, C = (HEAD_DIM, CHUNK)
            H = Ds // d
            x = out.astype(jnp.float32)
            rk = x.reshape(Bs, Ts, H, d)
            rk = rk / jnp.maximum(jnp.linalg.norm(rk, axis=-1, keepdims=True), 1e-12)
            rk = jnp.swapaxes(rk, 1, 2)
            wk = jnp.pad(rk[:, :, :-1], ((0, 0), (0, 0), (1, 0), (0, 0)))
            v = jnp.einsum('btd,ed->bte', x, W_write).reshape(Bs, Ts, H, d)
            v = jnp.swapaxes(v, 1, 2)
            beta = jax.nn.sigmoid(jnp.einsum('btd,hd->bth', x, W_beta))
            beta = jnp.swapaxes(beta, 1, 2)[..., None]
            log_decay = -jnp.exp(A_log)[None, None, :] * jax.nn.softplus(jnp.einsum('btd,hd->bth', x, W_alpha) + dt_bias)
            log_decay = jnp.swapaxes(log_decay, 1, 2)
            v_scaled = v * beta
            wk_scaled = wk * beta
            pad = -Ts % C
            if pad:
                p4 = ((0, 0), (0, 0), (0, pad), (0, 0))
                rk = jnp.pad(rk, p4)
                wk = jnp.pad(wk, p4)
                v_scaled = jnp.pad(v_scaled, p4)
                wk_scaled = jnp.pad(wk_scaled, p4)
                log_decay = jnp.pad(log_decay, ((0, 0), (0, 0), (0, pad)))
            Tp = Ts + pad
            N = Tp // C
            chunk = lambda a: a.reshape(Bs, H, N, C, d)
            rk, wk, v_scaled, wk_scaled = map(chunk, (rk, wk, v_scaled, wk_scaled))
            log_decay = log_decay.reshape(Bs, H, N, C)
            cum = jnp.cumsum(log_decay, -1)
            L_mask = jnp.tril(jnp.exp(jnp.tril(cum[..., :, None] - cum[..., None, :])))
            decay_exp = jnp.exp(cum)[..., None]
            chunk_end_decay = jnp.exp(cum[..., -1])
            M = jnp.tril(-(wk_scaled @ jnp.swapaxes(wk, -1, -2)) * L_mask, -1)
            eye = jnp.eye(C, dtype=x.dtype)
            A = solve_triangular(eye - M, jnp.broadcast_to(eye, M.shape), lower=True, unit_diagonal=True)
            intra = jnp.tril(rk @ jnp.swapaxes(wk, -1, -2) * L_mask, -1)
            rk_decay = rk * decay_exp
            tail_decay = jnp.exp(cum[..., -1:] - cum)[..., None]
            wk_pos = jnp.swapaxes(wk * tail_decay, -1, -2)
            wk_scaled_dec = wk_scaled * decay_exp
            toN = lambda a: jnp.moveaxis(a, 2, 0)

            def step(S, inp):
                A_i, vsc_i, wkd_i, rkd_i, intra_i, wkp_i, ced_i = inp
                v_new = A_i @ vsc_i - A_i @ wkd_i @ S
                o_i = rkd_i @ S + intra_i @ v_new
                S = ced_i[..., None, None] * S + wkp_i @ v_new
                return (S, o_i)
            S0 = jnp.zeros((Bs, H, d, d), x.dtype)
            _, o = jax.lax.scan(step, S0, (toN(A), toN(v_scaled), toN(wk_scaled_dec), toN(rk_decay), toN(intra), toN(wk_pos), jnp.moveaxis(chunk_end_decay, 2, 0)))
            o = jnp.moveaxis(o, 0, 2).reshape(Bs, H, Tp, d)
            o = jnp.swapaxes(o, 1, 2).reshape(Bs, Tp, Ds)[:, :Ts]
            return out + jnp.einsum('btd,ed->bte', o, W_read).astype(out.dtype)
        key = jax.random.key(seed)
        ks = jax.random.split(key, 7)
        H = D // HEAD_DIM
        out = jax.random.normal(ks[0], (B, T, D), dtype=jnp.float32)
        scale = D ** (-0.5)
        W_write = jax.random.normal(ks[1], (D, D), jnp.float32) * scale
        W_read = jax.random.normal(ks[2], (D, D), jnp.float32) * scale
        W_alpha = jax.random.normal(ks[3], (H, D), jnp.float32) * scale
        W_beta = jax.random.normal(ks[4], (H, D), jnp.float32) * scale
        A_log = jnp.log(jax.random.uniform(ks[5], (H,), jnp.float32, 0.05, 16.0))
        dt_bias = jnp.ones((H,), jnp.float32)
        return {'out': out, 'W_write': W_write, 'W_read': W_read, 'W_alpha': W_alpha, 'W_beta': W_beta, 'A_log': A_log, 'dt_bias': dt_bias}
    _L0_attn_in = _L0_attn_setup()

    def _L0_ffn_setup():
        import jax, jax.numpy as jnp
        import numpy as np
        GROUP = 16
        EPS = 1e-05

        def _dequant(q, scale):
            w = q.astype(jnp.float32) / 7.5 - 1.0
            return w * jnp.repeat(scale, GROUP, axis=1)

        def _qlora_linear(x, q, scale, bias, la, lb):
            w = _dequant(q, scale)
            base = jnp.einsum('btd,od->bto', x, w) + bias
            lora = jnp.einsum('btr,or->bto', jnp.einsum('btd,rd->btr', x, la), lb)
            return base + lora

        def _layernorm(x, g, b):
            mu = jnp.mean(x, axis=-1, keepdims=True)
            var = jnp.mean(jnp.square(x - mu), axis=-1, keepdims=True)
            return (x - mu) * jax.lax.rsqrt(var + EPS) * g + b
        key = jax.random.key(seed)
        ks = jax.random.split(key, 6)
        D, R, B, T = (256, 32, 8, 1024)
        x = jax.random.normal(ks[0], (B, T, D), dtype=jnp.float32)
        qweights = jax.random.randint(ks[1], (6, D, D), 0, 16, dtype=jnp.int32)
        scales = jax.random.uniform(ks[2], (6, D, D // GROUP), dtype=jnp.float32)
        biases = jax.random.normal(ks[3], (6, D), dtype=jnp.float32) * 0.02
        lora_a = jax.random.normal(ks[4], (6, R, D), dtype=jnp.float32) * 0.02
        lora_b = jax.random.normal(ks[5], (6, D, R), dtype=jnp.float32) * 0.02
        ln_gamma = jnp.ones((3, D), dtype=jnp.float32)
        ln_beta = jnp.zeros((3, D), dtype=jnp.float32)
        return {'x': x, 'qweights': qweights, 'scales': scales, 'biases': biases, 'lora_a': lora_a, 'lora_b': lora_b, 'ln_gamma': ln_gamma, 'ln_beta': ln_beta}
    _L0_ffn_in = _L0_ffn_setup()

    def _L1_attn_setup():
        import jax, jax.numpy as jnp
        import numpy as np
        B, S, D = (2, 512, 256)
        NH, KVH = (16, 4)
        HD = D // NH
        ROPE_BASE = 10000.0

        def rotate_half(x):
            half = x.shape[-1] // 2
            x1, x2 = (x[..., :half], x[..., half:])
            return jnp.concatenate((-x2, x1), axis=-1)

        def rope_cache(seq_len, head_dim, base, dtype):
            half = head_dim // 2
            inv_freq = 1.0 / base ** (jnp.arange(half, dtype=jnp.float32) / max(1, half))
            t = jnp.arange(seq_len, dtype=jnp.float32)
            freqs = jnp.einsum('i,j->ij', t, inv_freq)
            emb = jnp.concatenate((freqs, freqs), axis=-1)
            cos = jnp.cos(emb)[None, None].astype(dtype)
            sin = jnp.sin(emb)[None, None].astype(dtype)
            return (sin, cos)
        key = jax.random.key(seed)
        ks = jax.random.split(key, 5)
        s = 0.02
        return {'x': jax.random.normal(ks[0], (B, S, D), dtype=jnp.float32), 'Wq': jax.random.normal(ks[1], (D, D), dtype=jnp.float32) * s, 'Wk': jax.random.normal(ks[2], (D, KVH * HD), dtype=jnp.float32) * s, 'Wv': jax.random.normal(ks[3], (D, KVH * HD), dtype=jnp.float32) * s, 'Wo': jax.random.normal(ks[4], (D, D), dtype=jnp.float32) * s}
    _L1_attn_in = _L1_attn_setup()

    def _L1_ffn_setup():
        import jax, jax.numpy as jnp
        import numpy as np
        B, S, H = (2, 1024, 256)
        E, K, I = (8, 2, 352)
        key = jax.random.key(seed)
        ks = jax.random.split(key, 9)
        sc = 0.02
        return {'hidden_states': jax.random.normal(ks[0], (B, S, H), jnp.float32), 'gate_w': jax.random.normal(ks[1], (E, H), jnp.float32) * sc, 'w_gate': jax.random.normal(ks[2], (E, H, I), jnp.float32) * sc, 'w_up': jax.random.normal(ks[3], (E, H, I), jnp.float32) * sc, 'w_down': jax.random.normal(ks[4], (E, I, H), jnp.float32) * sc, 'sw_gate': jax.random.normal(ks[5], (H, I), jnp.float32) * sc, 'sw_up': jax.random.normal(ks[6], (H, I), jnp.float32) * sc, 'sw_down': jax.random.normal(ks[7], (I, H), jnp.float32) * sc, 'shared_gate_w': jax.random.normal(ks[8], (1, H), jnp.float32) * sc}
    _L1_ffn_in = _L1_ffn_setup()
    _d = {'L0_attn_out': _L0_attn_in['out'], 'L0_attn_W_write': _L0_attn_in['W_write'], 'L0_attn_W_read': _L0_attn_in['W_read'], 'L0_attn_W_alpha': _L0_attn_in['W_alpha'], 'L0_attn_W_beta': _L0_attn_in['W_beta'], 'L0_attn_A_log': _L0_attn_in['A_log'], 'L0_attn_dt_bias': _L0_attn_in['dt_bias'], 'L0_ffn_qweights': _L0_ffn_in['qweights'], 'L0_ffn_scales': _L0_ffn_in['scales'], 'L0_ffn_biases': _L0_ffn_in['biases'], 'L0_ffn_lora_a': _L0_ffn_in['lora_a'], 'L0_ffn_lora_b': _L0_ffn_in['lora_b'], 'L0_ffn_ln_gamma': _L0_ffn_in['ln_gamma'], 'L0_ffn_ln_beta': _L0_ffn_in['ln_beta'], 'L1_attn_Wq': _L1_attn_in['Wq'], 'L1_attn_Wk': _L1_attn_in['Wk'], 'L1_attn_Wv': _L1_attn_in['Wv'], 'L1_attn_Wo': _L1_attn_in['Wo'], 'L1_ffn_gate_w': _L1_ffn_in['gate_w'], 'L1_ffn_w_gate': _L1_ffn_in['w_gate'], 'L1_ffn_w_up': _L1_ffn_in['w_up'], 'L1_ffn_w_down': _L1_ffn_in['w_down'], 'L1_ffn_sw_gate': _L1_ffn_in['sw_gate'], 'L1_ffn_sw_up': _L1_ffn_in['sw_up'], 'L1_ffn_sw_down': _L1_ffn_in['sw_down'], 'L1_ffn_shared_gate_w': _L1_ffn_in['shared_gate_w']}
    _x0 = _d['L0_attn_out']
    _d['L0_attn_out'] = jax.random.normal(jax.random.fold_in(jax.random.key(seed), 1), (8, 1024, 256), dtype=_x0.dtype)
    del _x0
    return _d

def reference(L0_attn_out, L0_attn_W_write, L0_attn_W_read, L0_attn_W_alpha, L0_attn_W_beta, L0_attn_A_log, L0_attn_dt_bias, L0_ffn_qweights, L0_ffn_scales, L0_ffn_biases, L0_ffn_lora_a, L0_ffn_lora_b, L0_ffn_ln_gamma, L0_ffn_ln_beta, L1_attn_Wq, L1_attn_Wk, L1_attn_Wv, L1_attn_Wo, L1_ffn_gate_w, L1_ffn_w_gate, L1_ffn_w_up, L1_ffn_w_down, L1_ffn_sw_gate, L1_ffn_sw_up, L1_ffn_sw_down, L1_ffn_shared_gate_w):

    def _L0_attn_ref(out, W_write, W_read, W_alpha, W_beta, A_log, dt_bias):
        import jax, jax.numpy as jnp
        import numpy as np
        from jax.scipy.linalg import solve_triangular
        B, T, D = (2, 1024, 256)
        HEAD_DIM = 128
        CHUNK = 64

        def _forward(out, W_write, W_read, W_alpha, W_beta, A_log, dt_bias):
            Bs, Ts, Ds = out.shape
            d, C = (HEAD_DIM, CHUNK)
            H = Ds // d
            x = out.astype(jnp.float32)
            rk = x.reshape(Bs, Ts, H, d)
            rk = rk / jnp.maximum(jnp.linalg.norm(rk, axis=-1, keepdims=True), 1e-12)
            rk = jnp.swapaxes(rk, 1, 2)
            wk = jnp.pad(rk[:, :, :-1], ((0, 0), (0, 0), (1, 0), (0, 0)))
            v = jnp.einsum('btd,ed->bte', x, W_write).reshape(Bs, Ts, H, d)
            v = jnp.swapaxes(v, 1, 2)
            beta = jax.nn.sigmoid(jnp.einsum('btd,hd->bth', x, W_beta))
            beta = jnp.swapaxes(beta, 1, 2)[..., None]
            log_decay = -jnp.exp(A_log)[None, None, :] * jax.nn.softplus(jnp.einsum('btd,hd->bth', x, W_alpha) + dt_bias)
            log_decay = jnp.swapaxes(log_decay, 1, 2)
            v_scaled = v * beta
            wk_scaled = wk * beta
            pad = -Ts % C
            if pad:
                p4 = ((0, 0), (0, 0), (0, pad), (0, 0))
                rk = jnp.pad(rk, p4)
                wk = jnp.pad(wk, p4)
                v_scaled = jnp.pad(v_scaled, p4)
                wk_scaled = jnp.pad(wk_scaled, p4)
                log_decay = jnp.pad(log_decay, ((0, 0), (0, 0), (0, pad)))
            Tp = Ts + pad
            N = Tp // C
            chunk = lambda a: a.reshape(Bs, H, N, C, d)
            rk, wk, v_scaled, wk_scaled = map(chunk, (rk, wk, v_scaled, wk_scaled))
            log_decay = log_decay.reshape(Bs, H, N, C)
            cum = jnp.cumsum(log_decay, -1)
            L_mask = jnp.tril(jnp.exp(jnp.tril(cum[..., :, None] - cum[..., None, :])))
            decay_exp = jnp.exp(cum)[..., None]
            chunk_end_decay = jnp.exp(cum[..., -1])
            M = jnp.tril(-(wk_scaled @ jnp.swapaxes(wk, -1, -2)) * L_mask, -1)
            eye = jnp.eye(C, dtype=x.dtype)
            A = solve_triangular(eye - M, jnp.broadcast_to(eye, M.shape), lower=True, unit_diagonal=True)
            intra = jnp.tril(rk @ jnp.swapaxes(wk, -1, -2) * L_mask, -1)
            rk_decay = rk * decay_exp
            tail_decay = jnp.exp(cum[..., -1:] - cum)[..., None]
            wk_pos = jnp.swapaxes(wk * tail_decay, -1, -2)
            wk_scaled_dec = wk_scaled * decay_exp
            toN = lambda a: jnp.moveaxis(a, 2, 0)

            def step(S, inp):
                A_i, vsc_i, wkd_i, rkd_i, intra_i, wkp_i, ced_i = inp
                v_new = A_i @ vsc_i - A_i @ wkd_i @ S
                o_i = rkd_i @ S + intra_i @ v_new
                S = ced_i[..., None, None] * S + wkp_i @ v_new
                return (S, o_i)
            S0 = jnp.zeros((Bs, H, d, d), x.dtype)
            _, o = jax.lax.scan(step, S0, (toN(A), toN(v_scaled), toN(wk_scaled_dec), toN(rk_decay), toN(intra), toN(wk_pos), jnp.moveaxis(chunk_end_decay, 2, 0)))
            o = jnp.moveaxis(o, 0, 2).reshape(Bs, H, Tp, d)
            o = jnp.swapaxes(o, 1, 2).reshape(Bs, Tp, Ds)[:, :Ts]
            return out + jnp.einsum('btd,ed->bte', o, W_read).astype(out.dtype)
        return _forward(out, W_write, W_read, W_alpha, W_beta, A_log, dt_bias)

    def _L0_ffn_ref(x, qweights, scales, biases, lora_a, lora_b, ln_gamma, ln_beta):
        import jax, jax.numpy as jnp
        import numpy as np
        GROUP = 16
        EPS = 1e-05

        def _dequant(q, scale):
            w = q.astype(jnp.float32) / 7.5 - 1.0
            return w * jnp.repeat(scale, GROUP, axis=1)

        def _qlora_linear(x, q, scale, bias, la, lb):
            w = _dequant(q, scale)
            base = jnp.einsum('btd,od->bto', x, w) + bias
            lora = jnp.einsum('btr,or->bto', jnp.einsum('btd,rd->btr', x, la), lb)
            return base + lora

        def _layernorm(x, g, b):
            mu = jnp.mean(x, axis=-1, keepdims=True)
            var = jnp.mean(jnp.square(x - mu), axis=-1, keepdims=True)
            return (x - mu) * jax.lax.rsqrt(var + EPS) * g + b
        h = x
        for blk in range(3):
            i0, i1 = (2 * blk, 2 * blk + 1)
            y = _qlora_linear(h, qweights[i0], scales[i0], biases[i0], lora_a[i0], lora_b[i0])
            y = _layernorm(y, ln_gamma[blk], ln_beta[blk])
            y = jax.nn.gelu(y, approximate=False)
            y = _qlora_linear(y, qweights[i1], scales[i1], biases[i1], lora_a[i1], lora_b[i1])
            h = y + h
        return h

    def _L1_attn_ref(x, Wq, Wk, Wv, Wo):
        import jax, jax.numpy as jnp
        import numpy as np
        B, S, D = (2, 512, 256)
        NH, KVH = (16, 4)
        HD = D // NH
        ROPE_BASE = 10000.0

        def rotate_half(x):
            half = x.shape[-1] // 2
            x1, x2 = (x[..., :half], x[..., half:])
            return jnp.concatenate((-x2, x1), axis=-1)

        def rope_cache(seq_len, head_dim, base, dtype):
            half = head_dim // 2
            inv_freq = 1.0 / base ** (jnp.arange(half, dtype=jnp.float32) / max(1, half))
            t = jnp.arange(seq_len, dtype=jnp.float32)
            freqs = jnp.einsum('i,j->ij', t, inv_freq)
            emb = jnp.concatenate((freqs, freqs), axis=-1)
            cos = jnp.cos(emb)[None, None].astype(dtype)
            sin = jnp.sin(emb)[None, None].astype(dtype)
            return (sin, cos)
        bsz, seq_len, _ = x.shape
        scale = HD ** (-0.5)
        q = (x @ Wq).reshape(bsz, seq_len, NH, HD).transpose(0, 2, 1, 3)
        k = (x @ Wk).reshape(bsz, seq_len, KVH, HD).transpose(0, 2, 1, 3)
        v = (x @ Wv).reshape(bsz, seq_len, KVH, HD).transpose(0, 2, 1, 3)
        sin, cos = rope_cache(seq_len, HD, ROPE_BASE, q.dtype)
        q = q * cos + rotate_half(q) * sin
        k = k * cos + rotate_half(k) * sin
        rep = NH // KVH
        k = jnp.repeat(k, rep, axis=1)
        v = jnp.repeat(v, rep, axis=1)
        att = jnp.einsum('bhqd,bhkd->bhqk', q, k) * scale
        causal = jnp.tril(jnp.ones((seq_len, seq_len), dtype=bool))
        att = jnp.where(causal, att, jnp.finfo(att.dtype).min)
        att = jax.nn.softmax(att, axis=-1)
        y = jnp.einsum('bhqk,bhkd->bhqd', att, v)
        y = y.transpose(0, 2, 1, 3).reshape(bsz, seq_len, NH * HD)
        return y @ Wo

    def _L1_ffn_ref(hidden_states, gate_w, w_gate, w_up, w_down, sw_gate, sw_up, sw_down, shared_gate_w):
        import jax, jax.numpy as jnp
        import numpy as np
        B, S, H = (2, 1024, 256)
        E, K, I = (8, 2, 352)
        b, s, h = hidden_states.shape
        x = hidden_states.reshape(-1, h)
        logits = jnp.einsum('th,eh->te', x, gate_w)
        probs = jax.nn.softmax(logits.astype(jnp.float32), axis=-1)
        topk_w, topk_i = jax.lax.top_k(probs, K)
        topk_w = topk_w / jnp.sum(topk_w, axis=-1, keepdims=True)
        combine = jnp.sum(jax.nn.one_hot(topk_i, E, dtype=topk_w.dtype) * topk_w[..., None], axis=1)
        combine = combine.astype(x.dtype)
        g = jnp.einsum('th,ehi->eti', x, w_gate)
        u = jnp.einsum('th,ehi->eti', x, w_up)
        eo = jnp.einsum('eti,eih->eth', jax.nn.silu(g) * u, w_down)
        out = jnp.einsum('te,eth->th', combine, eo)
        sg = jax.nn.sigmoid(jnp.einsum('th,oh->to', x, shared_gate_w))
        so = jax.nn.silu(x @ sw_gate) * (x @ sw_up) @ sw_down
        out = out + sg * so
        return out.reshape(b, s, h)
    x = L0_attn_out
    x = x + _L0_attn_ref(_layernorm(x, axis=-1), L0_attn_W_write, L0_attn_W_read, L0_attn_W_alpha, L0_attn_W_beta, L0_attn_A_log, L0_attn_dt_bias)
    x = x + _L0_ffn_ref(_layernorm(x, axis=-1), L0_ffn_qweights, L0_ffn_scales, L0_ffn_biases, L0_ffn_lora_a, L0_ffn_lora_b, L0_ffn_ln_gamma, L0_ffn_ln_beta)
    x = x + _L1_attn_ref(_layernorm(x, axis=-1), L1_attn_Wq, L1_attn_Wk, L1_attn_Wv, L1_attn_Wo)
    x = x + _L1_ffn_ref(_layernorm(x, axis=-1), L1_ffn_gate_w, L1_ffn_w_gate, L1_ffn_w_up, L1_ffn_w_down, L1_ffn_sw_gate, L1_ffn_sw_up, L1_ffn_sw_down, L1_ffn_shared_gate_w)
    return x

_drawn_inputs = setup_inputs


def setup_inputs(seed=0):
    import zlib

    import numpy as np

    out = dict(_drawn_inputs(seed))
    spreads = {'L0_attn_dt_bias': (1.0, 0.6), 'L0_ffn_ln_gamma': (1.0, 0.2), 'L0_ffn_ln_beta': (0.0, 0.1)}
    factors = {'L0_attn_W_write': 8.0,
     'L0_attn_W_read': 8.0,
     'L0_attn_W_alpha': 8.0,
     'L0_attn_W_beta': 8.0,
     'L0_attn_A_log': 8.0,
     'L0_ffn_biases': 8.0,
     'L0_ffn_lora_a': 5.044,
     'L0_ffn_lora_b': 4.922,
     'L1_attn_Wq': 8.0,
     'L1_attn_Wk': 8.0,
     'L1_attn_Wv': 8.0,
     'L1_attn_Wo': 8.0,
     'L1_ffn_gate_w': 8.0,
     'L1_ffn_w_gate': 8.0,
     'L1_ffn_w_up': 8.0,
     'L1_ffn_w_down': 8.0,
     'L1_ffn_sw_gate': 8.0,
     'L1_ffn_sw_up': 8.0,
     'L1_ffn_sw_down': 8.0,
     'L1_ffn_shared_gate_w': 8.0}
    for name, (base, spread) in spreads.items():
        noise = np.random.default_rng([zlib.crc32(name.encode()), seed]).standard_normal(out[name].shape)
        drawn = base * np.exp(spread * noise) if base else spread * noise
        out[name] = jnp.asarray(drawn.astype(out[name].dtype))
    for name, factor in factors.items():
        out[name] = (out[name] * factor).astype(out[name].dtype)
    return out
```

```python
import math
from contextlib import ExitStack

import numpy as np

import concourse.bass as bass
from concourse import mybir

F32 = mybir.dt.float32
F16 = mybir.dt.float16
BF16 = mybir.dt.bfloat16
I32 = mybir.dt.int32
ACT = mybir.ActivationFunctionType
ALU = mybir.AluOpType
AX_X = mybir.AxisListType.X

P = 128
B, T, D = 8, 1024, 256
TPB = T // P
NT = B * TPB
KD = D // P
EPS = 1e-5

H0, HD0, CH = 2, 128, 64
LEVELS = int(math.log2(CH))
BL = 2
NCUM = 12
LN0 = BL * H0

NBLK, GROUP, RANK = 3, 16, 32
NLIN = 2 * NBLK
FL = 4

NH, NKV, HD = 16, 4, 16
FEAT = 64
NSET = 2 + FL + FL + 1

NR, TOPK = 8, 2
NEXP = NR + 1
WIDTH = 352
KI = -(-WIDTH // P)
IP = KI * P
ROUTE = 15

MASKS = ["ident", "ones"] + [f"level{k}" for k in range(LEVELS)]


def mask_arrays():
    r, c = np.arange(P)[:, None], np.arange(P)[None, :]
    out = {
        "ident": r == c,
        "ones": np.ones((P, P), bool),
    }
    for k in range(LEVELS):
        half = 1 << k
        low = ((r // (2 * half)) == (c // (2 * half))) & ((r // half) % 2 == 1) & ((c // half) % 2 == 0)
        out[f"level{k}"] = low.T if k == 0 else low
    return np.ascontiguousarray(np.stack([out[m] for m in MASKS], 1).astype(np.float32))


def clear_semaphores(nc, semaphores):
    with nc.Block() as block:

        @block.gpsimd
        def _(pool):
            for s in semaphores:
                pool.sem_clear(s)


class Chain:

    def __init__(self, eng, sem, base=0, per_round=None):
        self.eng, self.sem, self.base, self.n, self.per_round = eng, sem, base, 0, per_round

    def __call__(self, ins):
        self.n += 1
        ins.then_inc(self.sem, 1)
        self.eng.wait_ge(self.sem, self.base + self.n)

    def close(self):
        assert self.per_round is None or self.n == self.per_round, self.n


EXP_P = [1.9875691500e-4, 1.3981999507e-3, 8.3334519073e-3, 4.1665795894e-2, 1.6666665459e-1, 5.0000001201e-1]
LOG_P = [4.5270000862445199635215e-5, 4.9854102823193375972212e-1, 6.5787325942061044846969, 2.9911919328553073277375e1,
         6.0949667980987787057556e1, 5.7112963590585538103336e1, 2.0039553499201281259648e1]
LOG_Q = [1.0, 1.5062909083469192043167e1, 8.3047565967967209469434e1, 2.2176239823732856465394e2,
         3.0909872225312059774938e2, 2.1642788614495947685003e2, 6.0118660497603843919306e1]
SPLIT = 4097.0
ROUND = 12582912.0


def exp_f32(nc, link, out, x, n, t, z, y, bits):
    v = nc.vector
    link(v.tensor_scalar(n, x, 1.44269504088896341, ROUND, ALU.mult, ALU.add))
    link(v.tensor_scalar(n, n, -ROUND, None, ALU.add))
    link(v.scalar_tensor_tensor(out=t, in0=n, scalar=-0.693359375, in1=x, op0=ALU.mult, op1=ALU.add))
    link(v.scalar_tensor_tensor(out=t, in0=n, scalar=2.12194440e-4, in1=t, op0=ALU.mult, op1=ALU.add))
    link(v.tensor_tensor(z, t, t, ALU.mult))
    link(v.tensor_scalar(y, t, EXP_P[0], None, ALU.mult))
    for c in EXP_P[1:-1]:
        link(v.scalar_tensor_tensor(out=y, in0=y, scalar=c, in1=t, op0=ALU.add, op1=ALU.mult))
    link(v.scalar_tensor_tensor(out=y, in0=y, scalar=EXP_P[-1], in1=z, op0=ALU.add, op1=ALU.mult))
    link(v.tensor_tensor(y, y, t, ALU.add))
    link(v.tensor_scalar(y, y, 1.0, None, ALU.add))
    link(v.tensor_scalar(bits, n, 127.0, 8388608.0, ALU.add, ALU.mult))
    link(v.tensor_tensor(out, y, bits.bitcast(F32), ALU.mult))


def horner(nc, link, out, x, cs):
    v = nc.vector
    link(v.tensor_scalar(out, x, cs[0], None, ALU.mult))
    for c in cs[1:-1]:
        link(v.scalar_tensor_tensor(out=out, in0=out, scalar=c, in1=x, op0=ALU.add, op1=ALU.mult))
    link(v.tensor_scalar(out, out, cs[-1], None, ALU.add))


def first_norm(nc, x, small, dram, cums):
    HT = NT // 2
    with ExitStack() as ctx:
        def sb(name, shape, dt=F32):
            return ctx.enter_context(nc.sbuf_tensor("norm_" + name, shape, dt))

        mean = sb("mean", [P, NT])
        var = sb("var", [P, NT])
        root = sb("root", [P, NT])
        inv_root = sb("inv_root", [P, NT])
        root_hi, root_lo = sb("root_hi", [P, NT]), sb("root_lo", [P, NT])
        s0, s1 = sb("s0", [P, NT]), sb("s1", [P, NT])
        with ExitStack() as c1:
            acc = c1.enter_context(nc.sbuf_tensor("norm_acc", [P, HT, 16], F32))
            square = c1.enter_context(nc.sbuf_tensor("norm_square", [P, HT, D], F32))
            x_loaded = c1.enter_context(nc.semaphore("norm_x_loaded"))
            stats_done = c1.enter_context(nc.semaphore("norm_stats_done"))
            root_done = c1.enter_context(nc.semaphore("norm_root_done"))
            root_first = c1.enter_context(nc.semaphore("norm_root_first"))
            c1.callback(clear_semaphores, nc, [x_loaded, stats_done, root_done, root_first])
            block = c1.enter_context(nc.Block())

            @block.sync
            def _(sp):
                for half in range(2):
                    sp.dma_start(x[:, half * HT:(half + 1) * HT, :],
                                 dram["x"][half * HT * P:(half + 1) * HT * P, :].rearrange("(t p) d -> p t d", p=P))\
                        .then_inc(x_loaded, 16)
                    sp.wait_ge(x_loaded, 16 * (half + 1))

            @block.gpsimd
            def _(pool):
                pool.wait_ge(stats_done, 1)
                pool.tensor_tensor(root[:, :], var[:, :], small[:, 4:5].broadcast_to([P, NT]), ALU.pow).then_inc(root_first, 1)

            @block.vector
            def _(dve):
                link = Chain(dve, root_done)
                v = nc.vector
                for half in range(2):
                    xs = x[:, half * HT:(half + 1) * HT, :]
                    ms = mean[:, half * HT:(half + 1) * HT]
                    vs = var[:, half * HT:(half + 1) * HT]
                    dve.wait_ge(x_loaded, 16 * (half + 1))
                    link(v.tensor_tensor(acc[:, :, :], xs[:, :, 0:16], xs[:, :, 16:32], ALU.add))
                    for i in range(2, 16):
                        link(v.tensor_tensor(acc[:, :, :], acc[:, :, :], xs[:, :, 16 * i:16 * i + 16], ALU.add))
                    a4 = acc[:, :, :].rearrange("p t (b c) -> p t b c", b=4)
                    link(v.tensor_tensor(a4[:, :, 0, :], a4[:, :, 0, :], a4[:, :, 1, :], ALU.add))
                    link(v.tensor_tensor(a4[:, :, 2, :], a4[:, :, 2, :], a4[:, :, 3, :], ALU.add))
                    link(v.tensor_tensor(a4[:, :, 0, :], a4[:, :, 0, :], a4[:, :, 2, :], ALU.add))
                    link(v.tensor_tensor(acc[:, :, 0], acc[:, :, 0], acc[:, :, 1], ALU.add))
                    link(v.tensor_tensor(acc[:, :, 2], acc[:, :, 2], acc[:, :, 3], ALU.add))
                    link(v.tensor_tensor(acc[:, :, 0], acc[:, :, 0], acc[:, :, 2], ALU.add))
                    link(v.tensor_scalar(ms, acc[:, :, 0], 1.0 / D, None, ALU.mult))
                    link(v.tensor_tensor(xs, xs, ms[:, :, None].broadcast_to([P, HT, D]), ALU.subtract))
                    link(v.tensor_tensor(square[:, :, :], xs, xs, ALU.mult))
                    runs = square[:, :, :].rearrange("p t (r c) -> p t r c", c=32)
                    a8 = acc[:, :, 0:8]
                    link(v.tensor_tensor(a8, runs[:, :, :, 0], runs[:, :, :, 1], ALU.add))
                    for i in range(2, 32):
                        link(v.tensor_tensor(a8, a8, runs[:, :, :, i], ALU.add))
                    link(v.tensor_tensor(acc[:, :, 0:4], acc[:, :, 0:4], acc[:, :, 4:8], ALU.add))
                    link(v.tensor_tensor(acc[:, :, 0], acc[:, :, 0], acc[:, :, 1], ALU.add))
                    link(v.tensor_tensor(acc[:, :, 2], acc[:, :, 2], acc[:, :, 3], ALU.add))
                    link(v.tensor_tensor(acc[:, :, 0], acc[:, :, 0], acc[:, :, 2], ALU.add))
                    last = v.tensor_scalar(vs, acc[:, :, 0], 1.0 / D, EPS, ALU.mult, ALU.add)
                    link(last)
                v.memset(s1[:, :], 0.0).then_inc(stats_done, 1)
                dve.wait_ge(root_first, 1)
                dve.wait_ge(stats_done, 1)
                def halves(hi, lo, a, t):
                    link(v.scalar_tensor_tensor(out=t, in0=a, scalar=SPLIT, in1=a, op0=ALU.mult, op1=ALU.subtract))
                    link(v.scalar_tensor_tensor(out=hi, in0=a, scalar=SPLIT, in1=t, op0=ALU.mult, op1=ALU.subtract))
                    link(v.tensor_tensor(lo, a, hi, ALU.subtract))
                halves(root_hi[:, :], root_lo[:, :], root[:, :], s0[:, :])
                link(v.reciprocal(inv_root[:, :], root[:, :]))
                link(v.tensor_tensor(s0[:, :], root_hi[:, :], root_hi[:, :], ALU.mult))
                link(v.tensor_tensor(s1[:, :], var[:, :], s0[:, :], ALU.subtract))
                link(v.scalar_tensor_tensor(out=s0[:, :], in0=root_hi[:, :], scalar=-2.0, in1=root_lo[:, :], op0=ALU.mult, op1=ALU.mult))
                link(v.tensor_tensor(s1[:, :], s1[:, :], s0[:, :], ALU.add))
                link(v.tensor_tensor(s0[:, :], root_lo[:, :], root_lo[:, :], ALU.mult))
                link(v.tensor_tensor(s1[:, :], s1[:, :], s0[:, :], ALU.subtract))
                link(v.scalar_tensor_tensor(out=s1[:, :], in0=s1[:, :], scalar=0.5, in1=inv_root[:, :], op0=ALU.mult, op1=ALU.mult))
                link(v.tensor_tensor(root[:, :], root[:, :], s1[:, :], ALU.add))
                link(v.tensor_scalar(cums[:, :, 10], root[:, :], 1.0, None, ALU.add))
                link(v.tensor_copy(cums[:, :, 11], mean[:, :]))
                link(v.reciprocal(inv_root[:, :], root[:, :]))
                halves(root_hi[:, :], root_lo[:, :], root[:, :], s0[:, :])
                link(v.tensor_scalar(root_hi[:, :], root_hi[:, :], -1.0, None, ALU.mult))
                link(v.tensor_scalar(root_lo[:, :], root_lo[:, :], -1.0, None, ALU.mult))

        with ExitStack() as c2:
            q, t, qh, ql = (c2.enter_context(nc.sbuf_tensor("norm_" + n, [P, TPB, D], F32)) for n in ("q", "t", "qh", "ql"))
            tile_s = c2.enter_context(nc.sbuf_tensor("norm_tile_s", [P, 4, TPB], F32))
            step = c2.enter_context(nc.semaphore("norm_step"))
            c2.callback(clear_semaphores, nc, [step])
            block = c2.enter_context(nc.Block())

            @block.vector
            def _(dve):
                v = nc.vector
                STEPS = 12
                with dve.Fori(0, B) as b:
                    link = Chain(dve, step, dve.snap(b * STEPS), STEPS)
                    at = bass.ds(b * TPB, TPB)
                    xs = x[:, at, :]
                    v.tensor_copy(tile_s[:, 0, :], inv_root[:, at])
                    v.tensor_copy(tile_s[:, 1, :], root_hi[:, at])
                    link(v.tensor_copy(tile_s[:, 2, :], root_lo[:, at]))

                    def tiles(fn):
                        for i in range(TPB):
                            ins = fn(i)
                        return ins
                    link(tiles(lambda i: v.tensor_scalar(q[:, i, :], x[:, b * TPB + i, :], tile_s[:, 0, i:i + 1], None, ALU.mult)))
                    qf, tf, hf, lf = (a[:, :, :].rearrange("p t d -> p (t d)") for a in (q, t, qh, ql))
                    link(v.scalar_tensor_tensor(out=tf, in0=qf, scalar=SPLIT, in1=qf, op0=ALU.mult, op1=ALU.subtract))
                    link(v.scalar_tensor_tensor(out=hf, in0=qf, scalar=SPLIT, in1=tf, op0=ALU.mult, op1=ALU.subtract))
                    link(v.tensor_tensor(lf, qf, hf, ALU.subtract))
                    for n, (a, r) in enumerate(((qh, 1), (qh, 2), (ql, 1), (ql, 2))):
                        def one(i):
                            return v.scalar_tensor_tensor(out=t[:, i, :], in0=a[:, i, :], scalar=tile_s[:, r, i:i + 1],
                                                          in1=x[:, b * TPB + i, :] if n == 0 else t[:, i, :],
                                                          op0=ALU.mult, op1=ALU.add)
                        link(tiles(one))
                    link(tiles(lambda i: v.tensor_scalar(t[:, i, :], t[:, i, :], tile_s[:, 0, i:i + 1], None, ALU.mult)))
                    link(v.tensor_tensor(xs, q[:, :, :], t[:, :, :], ALU.add))
                    link(v.tensor_copy(tile_s[:, 3, 0:1], tile_s[:, 0, 0:1]))
                    link.close()


def decay_sums(nc, x, ident, small, dram, cums):
    KB = 32
    NKB = D // KB
    with ExitStack() as ctx:
        def sb(name, shape, dt=F32):
            return ctx.enter_context(nc.sbuf_tensor("norm_" + name, shape, dt))

        acc = [sb(f"chain{h}", [P, NT, 4]) for h in range(H0)]
        with ExitStack() as c1:
            def sc(name, shape):
                return c1.enter_context(nc.sbuf_tensor("norm_" + name, shape, F32))

            semaphores = []

            def sem(name):
                s = c1.enter_context(nc.semaphore("norm_" + name))
                semaphores.append(s)
                return s
            w = [sc(f"w{h}", [P, D]) for h in range(H0)]
            w_hi = [sc(f"w_hi{h}", [P, D]) for h in range(H0)]
            w_lo = [sc(f"w_lo{h}", [P, D]) for h in range(H0)]
            wt = sc("wt", [P, D])
            xh, xl, xt = (sc(n, [P, NT, KB]) for n in ("xh", "xl", "xt"))
            ph = [sc(f"ph{h}", [P, NT, KB]) for h in range(H0)]
            pl = [sc(f"pl{h}", [P, NT, KB]) for h in range(H0)]
            tmp = [[sc(f"tmp{h}_{i}", [P, NT, 4]) for i in range(4)] for h in range(H0)]
            w_loaded, setup, products, chain0, chain1, made1 = (sem(n) for n in ("w_loaded", "wsetup", "products", "chain0", "chain1", "made1"))
            c1.callback(clear_semaphores, nc, semaphores)
            block = c1.enter_context(nc.Block())
            PER = (KB // 4) * 8

            @block.sync
            def _(sp):
                for h in range(H0):
                    sp.dma_start(w[h][:, :], dram["w_alpha_rows"][h:h + 1, :].broadcast_to([P, D])).then_inc(w_loaded, 16)

            def chain(v, link, h):
                s, bb, t, e = (a[:, :, :] for a in tmp[h])
                a = acc[h][:, :, :]
                for k in range(KB // 4):
                    p_hi, p_lo = (u[h][:, :, 4 * k:4 * k + 4] for u in (ph, pl))
                    link(v.tensor_tensor(s, a, p_hi, ALU.add))
                    link(v.tensor_tensor(bb, s, a, ALU.subtract))
                    link(v.tensor_tensor(t, s, bb, ALU.subtract))
                    link(v.tensor_tensor(t, a, t, ALU.subtract))
                    link(v.tensor_tensor(e, p_hi, bb, ALU.subtract))
                    link(v.tensor_tensor(e, t, e, ALU.add))
                    link(v.tensor_tensor(e, e, p_lo, ALU.add))
                    link(v.tensor_tensor(a, s, e, ALU.add))

            @block.gpsimd
            def _(pool):
                pool.memset(acc[1][:, :, :], 0.0).then_inc(chain1, 1)
                pool.wait_ge(chain1, 1)
                with pool.Fori(0, NKB) as kb:
                    pool.wait_ge(made1, kb + 1)
                    link = Chain(pool, chain1, pool.snap(kb * PER + 1), PER)
                    chain(nc.gpsimd, link, 1)
                    link.close()

            @block.vector
            def _(dve):
                v = nc.vector
                link = Chain(dve, setup)
                link(v.memset(acc[0][:, :, :], 0.0))
                dve.wait_ge(w_loaded, 16 * H0)
                for h in range(H0):
                    link(v.scalar_tensor_tensor(out=wt[:, :], in0=w[h][:, :], scalar=SPLIT, in1=w[h][:, :], op0=ALU.mult, op1=ALU.subtract))
                    link(v.scalar_tensor_tensor(out=w_hi[h][:, :], in0=w[h][:, :], scalar=SPLIT, in1=wt[:, :], op0=ALU.mult, op1=ALU.subtract))
                    link(v.tensor_tensor(w_lo[h][:, :], w[h][:, :], w_hi[h][:, :], ALU.subtract))
                STEPS = 3 + 9 * H0
                with dve.Fori(0, NKB) as kb:
                    link = Chain(dve, products, dve.snap(kb * STEPS), STEPS)
                    at = bass.ds(kb * KB, KB)
                    xs = x[:, :, at]
                    a3, h3, l3 = xt[:, :, :], xh[:, :, :], xl[:, :, :]
                    link(v.scalar_tensor_tensor(out=a3, in0=xs, scalar=SPLIT, in1=xs, op0=ALU.mult, op1=ALU.subtract))
                    link(v.scalar_tensor_tensor(out=h3, in0=xs, scalar=SPLIT, in1=a3, op0=ALU.mult, op1=ALU.subtract))
                    link(v.tensor_tensor(l3, xs, h3, ALU.subtract))
                    for h in (1, 0):
                        def row(a):
                            return a[:, None, at].broadcast_to([P, NT, KB])
                        p3, e3 = ph[h][:, :, :], pl[h][:, :, :]
                        if h == 1:
                            dve.wait_ge(chain1, kb * PER + 1)
                        link(v.tensor_tensor(p3, xs, row(w[h]), ALU.mult))
                        link(v.tensor_tensor(e3, h3, row(w_hi[h]), ALU.mult))
                        link(v.tensor_tensor(e3, e3, p3, ALU.subtract))
                        for a, b in ((h3, w_lo[h]), (l3, w_hi[h]), (l3, w_lo[h])):
                            link(v.tensor_tensor(a3, a, row(b), ALU.mult))
                            link(v.tensor_tensor(e3, e3, a3, ALU.add))
                        if h == 1:
                            dve.sem_inc(made1, 1)
                    link.close()
                    link = Chain(dve, chain0, dve.snap(kb * PER), PER)
                    chain(nc.vector, link, 0)
                    link.close()

        with ExitStack() as c1:
            def sc(name, shape, dt=F32):
                return c1.enter_context(nc.sbuf_tensor("norm_" + name, shape, dt))

            semaphores = []

            def sem(name):
                s = c1.enter_context(nc.semaphore("norm_" + name))
                semaphores.append(s)
                return s
            z = sc("z", [P, H0, NT])
            bias = sc("bias", [P, H0])
            gain = sc("gain", [P, H0])
            gtmp = [sc(f"gtmp{i}", [P, H0]) for i in range(4)]
            gbits = sc("gbits", [P, H0], I32)
            n, t, zz, y, ex, big, wv, q, ll = (sc(f"sp{i}", [P, H0 * NT]) for i in range(9))
            bits = sc("bits", [P, H0 * NT], I32)
            log_decay = sc("log_decay", [P, NT, H0])
            rows = sc("rows", [P, 8, 16])
            to_end = sc("to_end", [P, 2, CH])
            off = sc("off", [P, 2, 4])
            last_row = [sc(f"last_row{c}", [P, P]) for c in range(2)]
            tok = sc("tok", [P, NT, H0])
            ps = [c1.enter_context(nc.psum_tensor(f"norm_ps{i}", [P, 512], F32)) for i in range(6)]
            loaded, s, turned, turned_back, ends, exps, cum_tok = (sem(i) for i in ("g_loaded", "g_steps", "turned", "turned_back", "ends", "exps", "cum_tok"))
            c1.callback(clear_semaphores, nc, semaphores)
            block = c1.enter_context(nc.Block())
            done = {}

            @block.sync
            def _(sp):
                sp.dma_start(gain[:, :], dram["a_log"].rearrange("(a h) -> a h", a=1).broadcast_to([P, H0])).then_inc(loaded, 16)
                sp.dma_start(bias[:, :], dram["dt_bias"].rearrange("(a h) -> a h", a=1).broadcast_to([P, H0])).then_inc(loaded, 16)
                for c in range(2):
                    sp.dma_start(last_row[c][:, :], dram["last_row"][c]).then_inc(loaded, 16)

            @block.vector
            def _(dve):
                v = nc.vector
                link = Chain(dve, s)
                dve.wait_ge(loaded, 64)
                for h in range(H0):
                    a = acc[h][:, :, :]
                    link(v.tensor_tensor(a[:, :, 0], a[:, :, 0], a[:, :, 1], ALU.add))
                    link(v.tensor_tensor(a[:, :, 2], a[:, :, 2], a[:, :, 3], ALU.add))
                    link(v.tensor_tensor(z[:, h, :], a[:, :, 0], a[:, :, 2], ALU.add))
                    link(v.tensor_scalar(z[:, h, :], z[:, h, :], bias[:, h:h + 1], None, ALU.add))
                zf = z[:, :, :].rearrange("p h t -> p (h t)")
                link(v.scalar_tensor_tensor(out=y[:, :], in0=zf, scalar=-1.0, in1=zf, op0=ALU.mult, op1=ALU.min))
                link(v.tensor_scalar(wv[:, :], y[:, :], -87.3, None, ALU.max))
                exp_f32(nc, link, ex[:, :], wv[:, :], n[:, :], t[:, :], zz[:, :], y[:, :], bits[:, :])
                link(v.tensor_scalar(big[:, :], ex[:, :], 0.41421356, None, ALU.is_ge))
                link(v.tensor_scalar(wv[:, :], ex[:, :], 1.0, -2.0, ALU.add, ALU.add))
                link(v.scalar_tensor_tensor(out=wv[:, :], in0=wv[:, :], scalar=0.5, in1=big[:, :], op0=ALU.mult, op1=ALU.mult))
                link(v.tensor_scalar(n[:, :], big[:, :], -1.0, 1.0, ALU.mult, ALU.add))
                link(v.tensor_tensor(t[:, :], ex[:, :], n[:, :], ALU.mult))
                link(v.tensor_tensor(wv[:, :], wv[:, :], t[:, :], ALU.add))
                horner(nc, link, y[:, :], wv[:, :], LOG_Q)
                link(v.reciprocal(y[:, :], y[:, :]))
                horner(nc, link, q[:, :], wv[:, :], LOG_P)
                link(v.tensor_tensor(q[:, :], q[:, :], y[:, :], ALU.mult))
                link(v.tensor_tensor(zz[:, :], wv[:, :], wv[:, :], ALU.mult))
                link(v.tensor_tensor(t[:, :], wv[:, :], zz[:, :], ALU.mult))
                link(v.tensor_tensor(t[:, :], t[:, :], q[:, :], ALU.mult))
                link(v.scalar_tensor_tensor(out=t[:, :], in0=zz[:, :], scalar=-0.5, in1=t[:, :], op0=ALU.mult, op1=ALU.add))
                link(v.tensor_tensor(ll[:, :], wv[:, :], t[:, :], ALU.add))
                LN2_HI = 0.693147182464599609375
                link(v.scalar_tensor_tensor(out=ll[:, :], in0=big[:, :], scalar=math.log(2) - LN2_HI, in1=ll[:, :], op0=ALU.mult, op1=ALU.add))
                link(v.scalar_tensor_tensor(out=ll[:, :], in0=big[:, :], scalar=LN2_HI, in1=ll[:, :], op0=ALU.mult, op1=ALU.add))
                link(v.scalar_tensor_tensor(out=ll[:, :], in0=zf, scalar=0.0, in1=ll[:, :], op0=ALU.max, op1=ALU.add))
                exp_f32(nc, link, gain[:, :], gain[:, :], *(g[:, :] for g in gtmp), gbits[:, :])
                link(v.tensor_scalar(gain[:, :], gain[:, :], -1.0, None, ALU.mult))
                for h in range(H0):
                    link(v.tensor_scalar(log_decay[:, :, h], ll[:, h * NT:(h + 1) * NT], gain[:, h:h + 1], None, ALU.mult))
                done["log_decay"] = link.n
                dve.wait_ge(turned, 1)
                link(v.tensor_copy(rows[:, :, :], ps[0][:, 0:P].rearrange("p (r i) -> p r i", i=16)))
                for i in range(1, 16):
                    link(v.tensor_tensor(rows[:, :, i], rows[:, :, i - 1], rows[:, :, i], ALU.add))
                runs = rows[:, :, :].rearrange("p (c r) i -> p c r i", c=2)
                link(v.memset(off[:, :, 0:1], 0.0))
                link(v.tensor_copy(off[:, :, 1], runs[:, :, 0, 15]))
                link(v.tensor_tensor(off[:, :, 2], off[:, :, 1], runs[:, :, 1, 15], ALU.add))
                link(v.tensor_tensor(off[:, :, 3], off[:, :, 2], runs[:, :, 2, 15], ALU.add))
                link(v.tensor_tensor(rows[:, :, :], rows[:, :, :],
                                     off[:, :, :].rearrange("p c r -> p (c r)")[:, :, None].broadcast_to([P, 8, 16]), ALU.add))
                flat = rows[:, :, :].rearrange("p (c r) i -> p c (r i)", c=2)
                link(v.tensor_tensor(to_end[:, :, :], flat[:, :, CH - 1:CH].broadcast_to([P, 2, CH]), flat, ALU.subtract))
                done["rows"] = link.n
                dve.wait_ge(turned_back, 2)
                link(v.tensor_copy(cums[:, :, 0:2], ps[1][:, 0:P].rearrange("p (t h) -> p t h", h=H0)))
                v.tensor_copy(tok[:, :, :], ps[1][:, 0:P].rearrange("p (t h) -> p t h", h=H0)).then_inc(cum_tok, 1)

            @block.tensor
            def _(pe):
                pe.wait_ge(s, done["log_decay"])
                pe.transpose(ps[0][:, 0:P], log_decay[:, :, :].rearrange("p t h -> p (t h)"), ident).then_inc(turned, 1)
                pe.wait_ge(s, done["rows"])
                pe.transpose(ps[1][:, 0:P], rows[:, :, :].rearrange("p r i -> p (r i)"), ident).then_inc(turned_back, 1)
                pe.transpose(ps[2][:, 0:P], to_end[:, :, :].rearrange("p c i -> p (c i)"), ident).then_inc(turned_back, 1)
                pe.wait_ge(loaded, 64)
                pe.wait_ge(cum_tok, 1)
                for c in range(2):
                    pe.matmul(ps[3 + c][:, 0:P], last_row[c][:, :], tok[:, :, :].rearrange("p t h -> p (t h)"),
                              start=True, stop=True).then_inc(ends, 1)

            @block.scalar
            def _(act):
                act.wait_ge(cum_tok, 1)
                act.activation(cums[:, :, 2:4], tok[:, :, :], ACT.Exp).then_inc(exps, 1)
                act.wait_ge(turned_back, 2)
                act.activation(cums[:, :, 4:6], ps[2][:, 0:P].rearrange("p (t h) -> p t h", h=H0), ACT.Exp).then_inc(exps, 1)
                act.wait_ge(ends, 2)
                for c in range(2):
                    act.activation(cums[:, :, 6 + 2 * c:8 + 2 * c], ps[3 + c][:, 0:P].rearrange("p (t h) -> p t h", h=H0), ACT.Exp)\
                        .then_inc(exps, 1)


def delta_attention(nc, x, ident, masks, small, dram, cums):
    semaphores = []
    with ExitStack() as ctx:
        def sb(name, shape, dt=F32):
            return ctx.enter_context(nc.sbuf_tensor("delta_" + name, shape, dt))

        def sem(name):
            s = ctx.enter_context(nc.semaphore("delta_" + name))
            semaphores.append(s)
            return s

        w_in = sb("w_in", [P, KD, D + H0])
        w_out = sb("w_out", [P, H0, D])
        minus_half = small[:, 0:2]
        cap = sb("cap", [P, P])

        h_tok = [sb(f"h_tok{b}", [P, D]) for b in range(BL)]
        square = [sb(f"square{b}", [P, D]) for b in range(BL)]
        ssq = [sb(f"ssq{b}", [P, H0]) for b in range(BL)]
        ssq_min = [sb(f"ssq_min{b}", [P, H0]) for b in range(BL)]
        rnorm = [sb(f"rnorm{b}", [P, H0]) for b in range(BL)]
        rk = [sb(f"rk{b}", [P, H0, HD0]) for b in range(BL)]
        h_T = [sb(f"h_T{b}", [P, KD, P]) for b in range(BL)]
        rk_T = [sb(f"rk_T{b}", [P, H0, P + 1]) for b in range(BL)]
        v_tok = [sb(f"v_tok{b}", [P, D]) for b in range(BL)]
        gate_nz = [sb(f"gate_nz{b}", [P, H0]) for b in range(BL)]
        gate_e = [sb(f"gate_e{b}", [P, H0]) for b in range(BL)]
        gate_d = [sb(f"gate_d{b}", [P, H0]) for b in range(BL)]
        nbeta = [sb(f"nbeta{b}", [P, H0]) for b in range(BL)]
        cum_rows = [sb(f"cum_rows{b}", [P, H0, P]) for b in range(BL)]
        scal = [sb(f"scal{b}", [P, NCUM]) for b in range(BL)]
        low_arg = [sb(f"low_arg{b}", [P, H0, P]) for b in range(BL)]
        decay_low = [sb(f"decay_low{b}", [P, H0, P]) for b in range(BL)]
        decay_row = [sb(f"decay_row{b}", [P, H0, P]) for b in range(BL)]
        lanes = range(LN0)
        rk_decay_T = [sb(f"rk_decay_T{l}", [P, P]) for l in lanes]
        wk_tail = [sb(f"wk_tail{l}", [P, HD0]) for l in lanes]
        gram = [sb(f"gram{l}", [P, P]) for l in lanes]
        intra = [sb(f"intra{l}", [P, P]) for l in lanes]
        gram0 = [sb(f"gram0{l}", [P, P]) for l in lanes]
        inv = [sb(f"inv{l}", [P, 2 * P]) for l in lanes]
        prod = [sb(f"prod{l}", [P, P]) for l in lanes]
        neg_r = [sb(f"neg_r{l}", [P, HD0]) for l in lanes]
        v_new = [sb(f"v_new{l}", [P, HD0]) for l in lanes]
        state = [sb(f"state{l}", [P, HD0]) for l in lanes]
        o_T = [sb(f"o_T{l}", [P, P]) for l in lanes]

        pa = [ctx.enter_context(nc.psum_tensor(f"delta_pa{l}", [P, 512], F32)) for l in lanes]
        pb = [ctx.enter_context(nc.psum_tensor(f"delta_pb{l}", [P, 512], F32)) for l in lanes]

        names_dve = ["h_s", "ssm_s", "rk_s", "scal_s", "carry_s", "rkT_s", "z_s", "den_s", "rows_s", "arg_s",
                     "nbeta_s", "xh_s", "x_s", "gram_s", "intra_s"]
        names_act = ["ssq_s", "hT_s", "v_s", "ge_s", "low_s", "row_s", "tail_s", "inv1_s", "oTe_s"]
        names_pe = ["hTp_s", "rkTp_s", "proj_s", "rowp_s", "gramp_s", "wkp_s", "inv1p_s", "outp_s"]
        names_pool = ["rnorm_s", "rkd_s", "g0_s", "inv0_s"]
        S = {}
        for group in (names_dve, names_act, names_pe, names_pool):
            for n in group:
                S[n] = sem(n)
        prodp_s = [sem(f"prodp{k}_s") for k in range(LEVELS)]
        prod_s = [sem(f"prod{k}_s") for k in range(LEVELS)]
        invp_s = [sem(f"grownp{k}_s") for k in range(LEVELS)]
        inv_s = [sem(f"grown{k}_s") for k in range(LEVELS)]
        wS_s = [sem(f"wS{c}_s") for c in range(2)]
        negr_s = [sem(f"negr{c}_s") for c in range(2)]
        br_s = [sem(f"br{c}_s") for c in range(2)]
        vnew_s = [sem(f"vnew{c}_s") for c in range(2)]
        oTp_s = [sem(f"oTp{c}_s") for c in range(2)]
        upd_s = [sem(f"upd{c}_s") for c in range(2)]
        state_s = [sem(f"state{c}_s") for c in range(2)]
        loaded = sem("loaded")
        reset = sem("reset")
        NLOAD = 4

        m = {n: masks[:, i, :] for i, n in enumerate(MASKS)}
        ctx.callback(clear_semaphores, nc, semaphores)
        block = ctx.enter_context(nc.Block())

        def counts(eng, bp, j):
            it = bp * TPB + j
            return [eng.snap(it * BL + k + 1) for k in range(BL + 1)], [eng.snap(it * LN0 + k + 1) for k in range(LN0 + 1)]

        @block.sync
        def _(sp):
            sp.dma_start(w_in[:, :, 0:D], dram["w_write"].rearrange("(k p) e -> p k e", p=P)).then_inc(loaded, 16)
            sp.dma_start(w_in[:, :, D:], dram["w_beta"].rearrange("(k p) e -> p k e", p=P)).then_inc(loaded, 16)
            sp.dma_start(w_out[:, :, :], dram["w_read"].rearrange("(k p) e -> p k e", p=P)).then_inc(loaded, 16)
            sp.dma_start(cap[:, :], dram["cap"]).then_inc(loaded, 16)

        @block.gpsimd
        def _(pool):
            for n in names_pool:
                pool.sem_inc(S[n], 1)
            pool.wait_ge(loaded, 16 * NLOAD)
            with pool.Fori(0, B // BL) as bp:
                with pool.Fori(0, TPB) as j:
                    n2, n4 = counts(pool, bp, j)
                    for b in range(BL):
                        pool.wait_ge(S["ssm_s"], n2[b + 1])
                        pool.tensor_tensor(rnorm[b][:, :], ssq_min[b][:, :], minus_half, ALU.pow).then_inc(S["rnorm_s"], 1)
                    for l in lanes:
                        b, h = divmod(l, H0)
                        pool.wait_ge(S["row_s"], n2[b + 1])
                        pool.wait_ge(S["rkT_s"], n2[b + 1])
                        pool.tensor_tensor(rk_decay_T[l][:, :], rk_T[b][:, h, 1:P + 1], decay_row[b][:, h, :], ALU.mult)\
                            .then_inc(S["rkd_s"], 1)
                    for l in lanes:
                        pool.wait_ge(S["gram_s"], n4[l + 1])
                        pool.tensor_tensor(gram0[l][:, :], gram[l][:, :], m["level0"], ALU.mult).then_inc(S["g0_s"], 1)
                        pool.wait_ge(S["g0_s"], n4[l + 1])
                        pool.tensor_tensor(inv[l][:, P:2 * P], gram0[l][:, :], ident, ALU.add).then_inc(S["inv0_s"], 1)




        @block.scalar
        def _(act):
            for n in names_act:
                act.sem_inc(S[n], 1)
            for s in vnew_s:
                act.sem_inc(s, 1)
            act.wait_ge(loaded, 16 * NLOAD)
            with act.Fori(0, B // BL) as bp:
                with act.Fori(0, TPB) as j:
                    n2, n4 = counts(act, bp, j)
                    for b in range(BL):
                        act.wait_ge(S["h_s"], n2[b + 1])
                        act.activation(square[b][:, 0:HD0], h_tok[b][:, 0:HD0], ACT.Square, accum_out=ssq[b][:, 0:1])
                        act.activation(square[b][:, HD0:D], h_tok[b][:, HD0:D], ACT.Square, accum_out=ssq[b][:, 1:2])\
                            .then_inc(S["ssq_s"], 1)
                    for b in range(BL):
                        act.wait_ge(S["hTp_s"], n2[b + 1])
                        act.activation(h_T[b][:, :, :], pa[2 * b][:, 0:D], ACT.Copy).then_inc(S["hT_s"], 1)
                    for b in range(BL):
                        act.wait_ge(S["proj_s"], n2[b + 1])
                        act.activation(v_tok[b][:, :], pa[2 * b + 1][:, 0:D], ACT.Copy).then_inc(S["v_s"], 1)
                    for b in range(BL):
                        act.wait_ge(S["z_s"], n2[b + 1])
                        act.activation(gate_e[b][:, :], gate_nz[b][:, :], ACT.Exp).then_inc(S["ge_s"], 1)
                    for b in range(BL):
                        act.wait_ge(S["arg_s"], n2[b + 1])
                        act.activation(decay_low[b][:, :, :], low_arg[b][:, :, :], ACT.Exp).then_inc(S["low_s"], 1)
                        act.activation(decay_row[b][:, :, :], pb[2 * b][:, 0:H0 * P], ACT.Exp).then_inc(S["row_s"], 1)
                    for l in lanes:
                        b, h = divmod(l, H0)
                        act.wait_ge(S["scal_s"], n2[b + 1])
                        act.wait_ge(S["wkp_s"], n4[l + 1])
                        act.activation(wk_tail[l][:, :], pa[l][:, 0:HD0], ACT.Copy, scale=scal[b][:, 4 + h:5 + h])\
                            .then_inc(S["tail_s"], 1)
                    for l in lanes:
                        act.wait_ge(S["inv1p_s"], n4[l + 1])
                        act.activation(inv[l][:, 0:P], pa[l][:, P:2 * P], ACT.Copy).then_inc(S["inv1_s"], 1)
                    for c in range(2):
                        rows = slice(CH * c, CH * c + CH)
                        for l in lanes:
                            b, h = divmod(l, H0)
                            act.wait_ge(br_s[c], n4[l + 1])
                            act.activation(v_new[l][rows, :], pa[l][rows, P:2 * P], ACT.Copy, scale=nbeta[b][rows, h:h + 1])\
                                .then_inc(vnew_s[c], 1)
                    for l in lanes:
                        act.wait_ge(oTp_s[1], n4[l + 1])
                        act.activation(o_T[l][:, :], pb[l][:, 2 * P:3 * P], ACT.Copy).then_inc(S["oTe_s"], 1)

        @block.vector
        def _(dve):
            for n in names_dve:
                dve.sem_inc(S[n], 1)
            for group in (prod_s, inv_s, negr_s, state_s):
                for s in group:
                    dve.sem_inc(s, 1)
            dve.wait_ge(loaded, 16 * NLOAD)
            with dve.Fori(0, B // BL) as bp:
                for l in lanes:
                    dve.memset(state[l][:, :], 0.0).then_inc(reset, 1)
                for b in range(BL):
                    dve.memset(rk_T[b][:, :, P:P + 1], 0.0).then_inc(reset, 1)
                with dve.Fori(0, TPB) as j:
                    n2, n4 = counts(dve, bp, j)
                    tile = [dve.snap((bp * BL + b) * TPB + j) for b in range(BL)]
                    for b in range(BL):
                        dve.tensor_copy(h_tok[b][:, :], x[:, tile[b], :]).then_inc(S["h_s"], 1)
                        dve.tensor_copy(scal[b][:, :], cums[:, tile[b], :]).then_inc(S["scal_s"], 1)
                    for b in range(BL):
                        dve.wait_ge(S["scal_s"], n2[b + 1])
                        for h in range(H0):
                            last = dve.tensor_scalar(cum_rows[b][:, h, :], m["ones"], scal[b][:, h:h + 1], None, ALU.mult)
                        last.then_inc(S["rows_s"], 1)
                    for b in range(BL):
                        dve.wait_ge(S["ssq_s"], n2[b + 1])
                        dve.tensor_scalar(ssq_min[b][:, :], ssq[b][:, :], 1e-24, None, ALU.max).then_inc(S["ssm_s"], 1)
                    for b in range(BL):
                        dve.wait_ge(S["rnorm_s"], n2[b + 1])
                        dve.tensor_scalar(rk[b][:, 0, :], h_tok[b][:, 0:HD0], rnorm[b][:, 0:1], None, ALU.mult)
                        dve.tensor_scalar(rk[b][:, 1, :], h_tok[b][:, HD0:D], rnorm[b][:, 1:2], None, ALU.mult)\
                            .then_inc(S["rk_s"], 1)
                        dve.wait_ge(reset, bp * 6 + 6)
                        dve.tensor_copy(rk_T[b][:, :, 0:1], rk_T[b][:, :, P:P + 1]).then_inc(S["carry_s"], 1)
                    for b in range(BL):
                        dve.wait_ge(S["rkTp_s"], n2[b + 1])
                        dve.wait_ge(S["carry_s"], n2[b + 1])
                        dve.tensor_copy(rk_T[b][:, :, 1:P + 1], pa[2 * b][:, D:2 * D].rearrange("p (h t) -> p h t", h=H0))\
                            .then_inc(S["rkT_s"], 1)
                    for b in range(BL):
                        dve.wait_ge(S["v_s"], n2[b + 1])
                        dve.tensor_scalar(gate_nz[b][:, :], pa[2 * b + 1][:, D:D + H0], -80.0, -1.0, ALU.max, ALU.mult)\
                            .then_inc(S["z_s"], 1)
                    for b in range(BL):
                        dve.wait_ge(S["rowp_s"], n2[b + 1])
                        for h in range(H0):
                            last = dve.scalar_tensor_tensor(out=low_arg[b][:, h, :], in0=pb[2 * b][:, h * P:(h + 1) * P],
                                                            scalar=scal[b][:, h:h + 1], in1=cap[:, :], op0=ALU.subtract, op1=ALU.min)
                        last.then_inc(S["arg_s"], 1)
                    for b in range(BL):
                        dve.wait_ge(S["ge_s"], n2[b + 1])
                        dve.tensor_scalar(gate_d[b][:, :], gate_e[b][:, :], -1.0, -1.0, ALU.mult, ALU.add).then_inc(S["den_s"], 1)
                        dve.wait_ge(S["den_s"], n2[b + 1])
                        dve.reciprocal(nbeta[b][:, :], gate_d[b][:, :]).then_inc(S["nbeta_s"], 1)
                    for b in range(BL):
                        dve.tensor_scalar(x[:, tile[b], :], h_tok[b][:, :], scal[b][:, 10:11], scal[b][:, 11:12],
                                          ALU.mult, ALU.add).then_inc(S["xh_s"], 1)
                    for l in lanes:
                        b, h = divmod(l, H0)
                        dve.wait_ge(S["nbeta_s"], n2[b + 1])
                        dve.wait_ge(S["gramp_s"], n4[l + 1])
                        dve.wait_ge(S["low_s"], n2[b + 1])
                        dve.scalar_tensor_tensor(out=gram[l][:, :], in0=pb[l][:, 0:P], scalar=nbeta[b][:, h:h + 1],
                                                 in1=decay_low[b][:, h, :], op0=ALU.mult, op1=ALU.mult).then_inc(S["gram_s"], 1)
                        dve.tensor_tensor(intra[l][:, :], pb[l][:, 1:P + 1], decay_low[b][:, h, :], ALU.mult).then_inc(S["intra_s"], 1)
                    for k in range(1, LEVELS):
                        for l in lanes:
                            dve.wait_ge(prodp_s[k], n4[l + 1])
                            dve.tensor_tensor(prod[l][:, :], pa[l][:, 2 * P:3 * P], m[f"level{k}"], ALU.mult).then_inc(prod_s[k], 1)
                        for l in lanes:
                            part = slice(0, 2 * P) if k < LEVELS - 1 else slice(P, 2 * P)
                            dve.wait_ge(invp_s[k], n4[l + 1])
                            dve.tensor_tensor(inv[l][:, part], inv[l][:, part], pa[l][:, part], ALU.add).then_inc(inv_s[k], 1)
                    for c in range(2):
                        rows = slice(CH * c, CH * c + CH)
                        for l in lanes:
                            b, h = divmod(l, H0)
                            dve.wait_ge(wS_s[c], n4[l + 1])
                            dve.scalar_tensor_tensor(out=neg_r[l][rows, :], in0=pa[l][rows, 0:HD0], scalar=scal[b][rows, 2 + h:3 + h],
                                                     in1=v_tok[b][rows, h * HD0:(h + 1) * HD0], op0=ALU.mult, op1=ALU.subtract)\
                                .then_inc(negr_s[c], 1)
                        for l in lanes:
                            b, h = divmod(l, H0)
                            at = 6 + 2 * c + h
                            dve.wait_ge(upd_s[c], n4[l + 1])
                            dve.scalar_tensor_tensor(out=state[l][:, :], in0=state[l][:, :], scalar=scal[b][:, at:at + 1],
                                                     in1=pa[l][:, 2 * P:3 * P], op0=ALU.mult, op1=ALU.add).then_inc(state_s[c], 1)
                    for b in range(BL):
                        dve.wait_ge(S["outp_s"], n2[b + 1])
                        dve.wait_ge(S["xh_s"], n2[b + 1])
                        dve.tensor_tensor(x[:, tile[b], :], x[:, tile[b], :], pa[2 * b][:, 0:D], ALU.add).then_inc(S["x_s"], 1)

        @block.tensor
        def _(pe):
            for n in names_pe:
                pe.sem_inc(S[n], 1)
            for group in (prodp_s, invp_s, wS_s, br_s, oTp_s, upd_s):
                for s in group:
                    pe.sem_inc(s, 1)
            pe.wait_ge(loaded, 16 * NLOAD)
            with pe.Fori(0, B // BL) as bp:
                with pe.Fori(0, TPB) as j:
                    n2, n4 = counts(pe, bp, j)
                    for b in range(BL):
                        pe.wait_ge(S["h_s"], n2[b + 1])
                        pe.wait_ge(S["x_s"], n2[0])
                        for k in range(KD):
                            last = pe.transpose(pa[2 * b][:, k * P:(k + 1) * P], h_tok[b][:, k * P:(k + 1) * P], ident)
                        last.then_inc(S["hTp_s"], 1)
                    for b in range(BL):
                        pe.wait_ge(S["rk_s"], n2[b + 1])
                        pe.wait_ge(S["hT_s"], n2[b + 1])
                        for h in range(H0):
                            last = pe.transpose(pa[2 * b][:, D + h * P:D + (h + 1) * P], rk[b][:, h, :], ident)
                        last.then_inc(S["rkTp_s"], 1)
                    for b in range(BL):
                        pe.wait_ge(state_s[1], n4[0])
                        for k in range(KD):
                            last = pe.matmul(pa[2 * b + 1][:, 0:D + H0], h_T[b][:, k, :], w_in[:, k, :],
                                             start=(k == 0), stop=(k == KD - 1))
                        last.then_inc(S["proj_s"], 1)
                    for b in range(BL):
                        pe.wait_ge(S["rows_s"], n2[b + 1])
                        pe.wait_ge(S["oTe_s"], n4[0])
                        for h in range(H0):
                            last = pe.transpose(pb[2 * b][:, h * P:(h + 1) * P], cum_rows[b][:, h, :], ident)
                        last.then_inc(S["rowp_s"], 1)
                    for l in lanes:
                        b, h = divmod(l, H0)
                        pe.wait_ge(S["rkT_s"], n2[b + 1])
                        pe.wait_ge(S["z_s"], n2[b + 1])
                        pe.transpose(pa[l][:, 0:HD0], rk_T[b][:, h, 0:P], ident).then_inc(S["wkp_s"], 1)
                    for l in lanes:
                        b, h = divmod(l, H0)
                        pe.wait_ge(S["row_s"], n2[b + 1])
                        pe.matmul(pb[l][:, 0:P + 1], rk_T[b][:, h, 0:P], rk_T[b][:, h, 0:P + 1], start=True, stop=True)\
                            .then_inc(S["gramp_s"], 1)
                    for l in lanes:
                        pe.wait_ge(S["tail_s"], n4[l + 1])
                        pe.wait_ge(S["inv0_s"], n4[l + 1])
                        pe.transpose(pa[l][:, P:2 * P], inv[l][:, P:2 * P], ident).then_inc(S["inv1p_s"], 1)
                    for k in range(1, LEVELS):
                        for l in lanes:
                            if k == 1:
                                pe.wait_ge(S["inv1_s"], n4[l + 1])
                            else:
                                pe.wait_ge(inv_s[k - 1], n4[l + 1])
                            pe.matmul(pa[l][:, 2 * P:3 * P], gram[l][:, :], inv[l][:, 0:P], start=True, stop=True).then_inc(prodp_s[k], 1)
                        for l in lanes:
                            pe.wait_ge(prod_s[k], n4[l + 1])
                            if k < LEVELS - 1:
                                pe.matmul(pa[l][:, 0:P], inv[l][:, P:2 * P], prod[l][:, :], start=True, stop=True)
                            pe.matmul(pa[l][:, P:2 * P], prod[l][:, :], inv[l][:, P:2 * P], start=True, stop=True).then_inc(invp_s[k], 1)
                    for c in range(2):
                        rows = slice(CH * c, CH * c + CH)
                        for l in lanes:
                            b, h = divmod(l, H0)
                            if c == 0:
                                pe.wait_ge(inv_s[LEVELS - 1], n4[l + 1])
                            else:
                                pe.wait_ge(state_s[0], n4[l + 1])
                            pe.matmul(pa[l][rows, 0:HD0], rk_T[b][:, h, rows], state[l][:, :], start=True, stop=True).then_inc(wS_s[c], 1)
                        for l in lanes:
                            pe.wait_ge(negr_s[c], n4[l + 1])
                            pe.matmul(pa[l][:, P:2 * P], inv[l][rows, P:2 * P], neg_r[l][rows, :],
                                      start=True, stop=True).then_inc(br_s[c], 1)
                        for l in lanes:
                            b, h = divmod(l, H0)
                            if c == 0:
                                pe.wait_ge(S["rkd_s"], n4[l + 1])
                                pe.wait_ge(S["intra_s"], n4[l + 1])
                            pe.matmul(pb[l][:, 2 * P + CH * c:2 * P + CH * c + CH], state[l][:, :], rk_decay_T[l][:, rows],
                                      start=True, stop=False)
                            pe.wait_ge(vnew_s[c], n4[l + 1])
                            pe.matmul(pb[l][:, 2 * P + CH * c:2 * P + CH * c + CH], v_new[l][rows, :], intra[l][rows, rows],
                                      start=False, stop=True).then_inc(oTp_s[c], 1)
                            pe.matmul(pa[l][:, 2 * P:3 * P], wk_tail[l][rows, :], v_new[l][rows, :], start=True, stop=True)\
                                .then_inc(upd_s[c], 1)
                    for b in range(BL):
                        pe.wait_ge(state_s[1], n4[2 * b + 2])
                        for h in range(H0):
                            pe.wait_ge(S["oTe_s"], n4[2 * b + h + 1])
                            last = pe.matmul(pa[2 * b][:, 0:D], o_T[2 * b + h][:, :], w_out[:, h, :], start=(h == 0), stop=(h == H0 - 1))
                        last.then_inc(S["outp_s"], 1)


def quantised_ffn(nc, x, ident, small, dram):
    semaphores = []
    with ExitStack() as ctx:
        def sb(name, shape, dt=F32):
            return ctx.enter_context(nc.sbuf_tensor("ffn_" + name, shape, dt))

        def sem(name):
            s = ctx.enter_context(nc.semaphore("ffn_" + name))
            semaphores.append(s)
            return s

        w = sb("w", [P, NLIN, KD, D])
        bias = sb("bias", [P, NLIN, D])
        gamma, beta = sb("gamma", [P, NBLK, KD]), sb("beta", [P, NBLK, KD])

        with ExitStack() as c1:
            q = c1.enter_context(nc.sbuf_tensor("ffn_q", [P, NLIN, KD, D], I32))
            scales = c1.enter_context(nc.sbuf_tensor("ffn_scales", [GROUP, NLIN, D], F32))
            spread = c1.enter_context(nc.sbuf_tensor("ffn_spread", [GROUP, KD, P], F32))
            lora_a = c1.enter_context(nc.sbuf_tensor("ffn_lora_a", [RANK, NLIN, D], F32))
            lora_b = c1.enter_context(nc.sbuf_tensor("ffn_lora_b", [RANK, NLIN, D], F32))
            scale_rows = [c1.enter_context(nc.psum_tensor(f"ffn_scale_rows{i}", [P, D], F32)) for i in range(2)]
            low_rank = [c1.enter_context(nc.psum_tensor(f"ffn_low_rank{i}", [P, D], F32)) for i in range(2)]
            loaded = c1.enter_context(nc.semaphore("ffn_ffn_loaded"))
            multiplied = c1.enter_context(nc.semaphore("ffn_multiplied"))
            built = c1.enter_context(nc.semaphore("ffn_built"))
            c1.callback(clear_semaphores, nc, [loaded, multiplied, built])
            block = c1.enter_context(nc.Block())
            slices = [(i, k) for i in range(NLIN) for k in range(KD)]

            @block.sync
            def _(sp):
                for dst, src in ((q, dram["qweights"].rearrange("i (k p) o -> p i k o", p=P)), (scales, dram["scales"]),
                                 (spread, dram["spread"]), (lora_a, dram["lora_a"]), (lora_b, dram["lora_b"]),
                                 (gamma, dram["ln_gamma"]), (beta, dram["ln_beta"])):
                    sp.dma_start(dst[(slice(None),) * len(dst.shape)], src).then_inc(loaded, 16)
                sp.dma_start(bias[:, :, :], dram["biases"].rearrange("(a i) o -> a i o", a=1).broadcast_to([P, NLIN, D])).then_inc(loaded, 16)

            @block.tensor
            def _(pe):
                pe.wait_ge(loaded, 16 * 8)
                for n, (i, k) in enumerate(slices):
                    if n >= 2:
                        pe.wait_ge(built, 3 * (n - 1))
                    pe.matmul(scale_rows[n % 2][:, :], spread[:, k, :], scales[:, i, :], start=True, stop=True)
                    pe.matmul(low_rank[n % 2][:, :], lora_a[:, i, k * P:(k + 1) * P], lora_b[:, i, :], start=True, stop=True)\
                        .then_inc(multiplied, 1)

            @block.vector
            def _(dve):
                dve.wait_ge(loaded, 16 * 8)
                for n, (i, k) in enumerate(slices):
                    at = w[:, i, k, :]
                    dve.tensor_scalar(at, q[:, i, k, :], 1.0 / 7.5, -1.0, ALU.mult, ALU.add).then_inc(built, 1)
                    dve.wait_ge(multiplied, n + 1)
                    dve.wait_ge(built, 3 * n + 1)
                    dve.tensor_tensor(at, at, scale_rows[n % 2][:, :], ALU.mult).then_inc(built, 1)
                    dve.wait_ge(built, 3 * n + 2)
                    dve.tensor_tensor(at, at, low_rank[n % 2][:, :], ALU.add).then_inc(built, 1)

        lanes = range(FL)
        stats = [sb(f"stats{l}", [P, 6]) for l in lanes]
        mv = [sb(f"mv{l}", [P, 2]) for l in lanes]
        var_eps = [sb(f"var_eps{l}", [P, 1]) for l in lanes]
        rstd = [sb(f"rstd{l}", [P, 1]) for l in lanes]
        h = [sb(f"h{l}", [P, D]) for l in lanes]
        h_bias = [sb(f"h_bias{l}", [P, D]) for l in lanes]
        h_T = [sb(f"h_T{l}", [P, KD, P]) for l in lanes]
        y = [sb(f"y{l}", [P, D]) for l in lanes]
        y_norm = [sb(f"y_norm{l}", [P, D]) for l in lanes]
        act_T = [sb(f"act_T{l}", [P, KD, P]) for l in lanes]
        turn = [ctx.enter_context(nc.psum_tensor(f"ffn_turn{l}", [P, 512], F32)) for l in lanes]
        acc = [ctx.enter_context(nc.psum_tensor(f"ffn_acc{l}", [P, 512], F32)) for l in lanes]
        NORMS = NBLK + 1
        stats_s = [sem(f"stats{n}_s") for n in range(NORMS)]
        mv_s = [sem(f"mv{n}_s") for n in range(NORMS)]
        ve_s = [sem(f"ve{n}_s") for n in range(NORMS)]
        rstd_s = [sem(f"rstd{n}_s") for n in range(NORMS)]
        h_s = [sem(f"h{n}_s") for n in range(NBLK + 1)]
        y_s, yn_s = [sem(f"y{n}_s") for n in range(NBLK)], [sem(f"yn{n}_s") for n in range(NBLK)]
        hb_s = [sem(f"hb{n}_s") for n in range(NBLK)]
        hT_s, aT_s = [sem(f"hT{n}_s") for n in range(NBLK)], [sem(f"aT{n}_s") for n in range(NBLK)]
        hTp_s, ynp_s = [sem(f"hTp{n}_s") for n in range(NBLK)], [sem(f"ynp{n}_s") for n in range(NBLK)]
        mm1_s, mm2_s = [sem(f"mm1{n}_s") for n in range(NBLK)], [sem(f"mm2{n}_s") for n in range(NBLK)]
        fence = sem("fence")
        x_s = sem("xffn_s")
        ctx.callback(clear_semaphores, nc, semaphores)
        block = ctx.enter_context(nc.Block())

        def counts(eng, it):
            return [eng.snap(it * FL + k + 1) for k in range(FL + 1)]

        @block.gpsimd
        def _(pool):
            for s in ve_s + rstd_s + hb_s:
                pool.sem_inc(s, 1)
            with pool.Fori(0, NT // FL) as it:
                n = counts(pool, it)
                for norm in range(NORMS):
                    for l in lanes:
                        pool.wait_ge(mv_s[norm], n[l + 1])
                        pool.tensor_tensor(var_eps[l][:, :], mv[l][:, 1:2], small[:, 2:3], ALU.add).then_inc(ve_s[norm], 1)
                        pool.wait_ge(ve_s[norm], n[l + 1])
                        pool.tensor_tensor(rstd[l][:, :], var_eps[l][:, :], small[:, 0:1], ALU.pow).then_inc(rstd_s[norm], 1)
                    if norm < NBLK:
                        for l in lanes:
                            pool.wait_ge(h_s[norm], n[l + 1])
                            pool.tensor_tensor(h_bias[l][:, :], h[l][:, :], bias[:, 2 * norm + 1, :], ALU.add).then_inc(hb_s[norm], 1)

        @block.scalar
        def _(act):
            for s in hT_s + aT_s:
                act.sem_inc(s, 1)
            with act.Fori(0, NT // FL) as it:
                n = counts(act, it)
                for b in range(NBLK):
                    for l in lanes:
                        act.wait_ge(hTp_s[b], n[l + 1])
                        act.activation(h_T[l][:, :, :], turn[l][:, 0:D], ACT.Copy).then_inc(hT_s[b], 1)
                    for l in lanes:
                        act.wait_ge(ynp_s[b], n[l + 1])
                        for k in range(KD):
                            last = act.activation(act_T[l][:, k, :], turn[l][:, k * P:(k + 1) * P], ACT.Gelu,
                                                  scale=gamma[:, b, k:k + 1], bias=beta[:, b, k:k + 1])
                        last.then_inc(aT_s[b], 1)

        @block.vector
        def _(dve):
            for s in stats_s + mv_s + h_s + y_s + yn_s + [x_s]:
                dve.sem_inc(s, 1)
            with dve.Fori(0, NT // FL) as it:
                n = counts(dve, it)
                tile = [dve.snap(it * FL + l) for l in lanes]

                def norm_of(l, norm, source):
                    dve.bn_stats(stats[l][:, :], source).then_inc(stats_s[norm], 1)
                    dve.wait_ge(stats_s[norm], n[l + 1])
                    dve.sem_inc(fence, 1)
                    dve.bn_aggr(mv[l][:, :], stats[l][:, :]).then_inc(mv_s[norm], 1)

                def normalise(l, norm, out, source, s):
                    dve.wait_ge(mv_s[norm], n[l + 1])
                    dve.wait_ge(rstd_s[norm], n[l + 1])
                    dve.tensor_scalar(out, source, mv[l][:, 0:1], rstd[l][:, 0:1], ALU.subtract, ALU.mult).then_inc(s, 1)

                for l in lanes:
                    norm_of(l, 0, x[:, tile[l], :])
                for l in lanes:
                    normalise(l, 0, h[l][:, :], x[:, tile[l], :], h_s[0])
                for b in range(NBLK):
                    for l in lanes:
                        dve.wait_ge(mm1_s[b], n[l + 1])
                        dve.tensor_tensor(y[l][:, :], acc[l][:, 0:D], bias[:, 2 * b, :], ALU.add).then_inc(y_s[b], 1)
                        dve.wait_ge(y_s[b], n[l + 1])
                        dve.sem_inc(fence, 1)
                        norm_of(l, b + 1, y[l][:, :])
                        if l > 0:
                            normalise(l - 1, b + 1, y_norm[l - 1][:, :], y[l - 1][:, :], yn_s[b])
                    normalise(FL - 1, b + 1, y_norm[FL - 1][:, :], y[FL - 1][:, :], yn_s[b])
                    for l in lanes:
                        dve.wait_ge(mm2_s[b], n[l + 1])
                        dve.wait_ge(hb_s[b], n[l + 1])
                        dve.tensor_tensor(h[l][:, :], h_bias[l][:, :], acc[l][:, 0:D], ALU.add).then_inc(h_s[b + 1], 1)
                for l in lanes:
                    dve.wait_ge(h_s[NBLK], n[l + 1])
                    dve.tensor_tensor(x[:, tile[l], :], x[:, tile[l], :], h[l][:, :], ALU.add).then_inc(x_s, 1)

        @block.tensor
        def _(pe):
            for s in hTp_s + ynp_s + mm1_s + mm2_s:
                pe.sem_inc(s, 1)
            with pe.Fori(0, NT // FL) as it:
                n = counts(pe, it)
                for b in range(NBLK):
                    for l in lanes:
                        pe.wait_ge(h_s[b], n[l + 1])
                        if b == 0:
                            pe.wait_ge(h_s[NBLK], n[0])
                        for k in range(KD):
                            last = pe.transpose(turn[l][:, k * P:(k + 1) * P], h[l][:, k * P:(k + 1) * P], ident)
                        last.then_inc(hTp_s[b], 1)
                    for l in lanes:
                        pe.wait_ge(hT_s[b], n[l + 1])
                        for k in range(KD):
                            last = pe.matmul(acc[l][:, 0:D], h_T[l][:, k, :], w[:, 2 * b, k, :], start=(k == 0), stop=(k == KD - 1))
                        last.then_inc(mm1_s[b], 1)
                    for l in lanes:
                        pe.wait_ge(yn_s[b], n[l + 1])
                        for k in range(KD):
                            last = pe.transpose(turn[l][:, k * P:(k + 1) * P], y_norm[l][:, k * P:(k + 1) * P], ident)
                        last.then_inc(ynp_s[b], 1)
                    for l in lanes:
                        pe.wait_ge(aT_s[b], n[l + 1])
                        for k in range(KD):
                            last = pe.matmul(acc[l][:, 0:D], act_T[l][:, k, :], w[:, 2 * b + 1, k, :], start=(k == 0), stop=(k == KD - 1))
                        last.then_inc(mm2_s[b], 1)


def gqa_attention(nc, x, ident, small, dram):
    semaphores = []
    with ExitStack() as ctx:
        def sb(name, shape, dt=F32):
            return ctx.enter_context(nc.sbuf_tensor("gqa_" + name, shape, dt))

        def sem(name):
            s = ctx.enter_context(nc.semaphore("gqa_" + name))
            semaphores.append(s)
            return s

        lanes, slots = range(FL), range(4)
        HB = NH // 2
        QW = NH * HD
        w_qkv = sb("w_qkv", [P, KD, QW + 2 * NKV * HD])
        w_o = sb("w_o", [P, KD, D])
        cos, sin = sb("cos", [P, TPB, HD]), sb("sin", [P, TPB, HD])
        mask32 = sb("mask32", [P, 2, P])
        mask = sb("mask", [P, 2, P], BF16)
        ident_b, ident_h = sb("ident_b", [P, P], BF16), sb("ident_h", [P, P], F16)
        stats = [sb(f"stats{l}", [P, 6]) for l in lanes]
        mv = [sb(f"mv{l}", [P, 2]) for l in lanes]
        var_eps = [sb(f"var_eps{l}", [P, 1]) for l in lanes]
        rstd = [sb(f"rstd{l}", [P, 1]) for l in lanes]
        x_norm = [sb(f"x_norm{l}", [P, D]) for l in lanes]
        x_T = [sb(f"x_T{l}", [P, KD, P]) for l in lanes]
        NR_ = NH + NKV
        by_cos = [sb(f"by_cos{l}", [P, NR_, HD]) for l in lanes]
        by_sin = [sb(f"by_sin{l}", [P, NR_, HD]) for l in lanes]
        rot = [sb(f"rot{l}", [P, NR_, HD]) for l in lanes]
        q_feat = sb("q_feat", [P, TPB, NH, FEAT], F16)
        k_feat = [sb(f"k_feat{l}", [P, NKV, 2, 2 * FEAT], F16) for l in lanes]
        q_T, k_T = sb("q_T", [P, HB, T], F16), sb("k_T", [P, NKV, 2, T], F16)
        v_aug = sb("v_aug", [P, TPB, NKV, 32])
        v_group = sb("v_group", [P, TPB, 32])
        row_max = sb("row_max", [P, TPB, NH])
        prob = [sb(f"prob{i}", [P, T]) for i in slots]
        o_T = sb("o_T", [P, T])
        inv_sum = sb("inv_sum", [P, TPB * 4])
        y = sb("y", [P, TPB, D])
        y_T = [sb(f"y_T{l}", [P, KD, P]) for l in lanes]
        bank = [ctx.enter_context(nc.psum_tensor(f"gqa_bank{i}", [P, 1024], F32)) for i in range(4)]
        pv, back = bank[2], bank[3]

        S = {n: sem(n) for n in (
            "fd", "fa", "fp", "stats", "mv", "ve", "rstd", "xn", "xTp", "xT", "proj", "cos", "sin", "rot", "v", "qhi", "qlo", "khi", "klo",
            "kdup", "qTp", "qT", "kTp", "kT", "score", "max", "m16", "vg", "q2p", "q2", "st", "exp", "pv", "oT", "oTp", "inv", "y",
            "yTp", "yT", "out", "x")}
        owner = {"dve": "stats mv xn cos sin v qlo klo kdup kT max m16 vg oT inv y x".split(),
                 "act": "xT qhi khi qT q2 exp yT".split(), "pool": "ve rstd rot".split(),
                 "pe": "xTp proj qTp kTp score q2p st pv oTp yTp out".split()}
        START = {"max": 4, "pv": 4, "exp": 2}
        loaded, setup = sem("loaded"), sem("setup")
        ctx.callback(clear_semaphores, nc, semaphores)
        block = ctx.enter_context(nc.Block())
        NS = TPB * 2
        NC = 4 * TPB

        def first(eng, who):
            for n in owner[who]:
                eng.sem_inc(S[n], START.get(n, 1))

        def wait(eng, name, index, back_by=0):
            eng.wait_ge(S[name], eng.snap(index + (START.get(name, 1) + 1 - back_by)))

        def fenced(eng, fence, name, index, back_by=0):
            wait(eng, name, index, back_by)
            eng.sem_inc(S[fence], 1)

        @block.sync
        def _(sp):
            for dst, src in ((w_qkv, "w_qkv"), (w_o, "w_o"), (cos, "cos"), (sin, "sin"), (mask32, "causal")):
                sp.dma_start(dst[:, :, :], dram[src]).then_inc(loaded, 16)

        @block.gpsimd
        def _(pool):
            first(pool, "pool")
            with pool.Fori(0, B) as b:
                with pool.Fori(0, 2) as half:
                    at = pool.snap((b * 2 + half) * FL)
                    for l in lanes:
                        wait(pool, "mv", at + l)
                        pool.tensor_tensor(var_eps[l][:, :], mv[l][:, 1:2], small[:, 2:3], ALU.add).then_inc(S["ve"], 1)
                        wait(pool, "ve", at + l)
                        pool.tensor_tensor(rstd[l][:, :], var_eps[l][:, :], small[:, 0:1], ALU.pow).then_inc(S["rstd"], 1)
                    for l in lanes:
                        wait(pool, "cos", at + l)
                        wait(pool, "sin", at + l)
                        pool.tensor_tensor(rot[l][:, :, :], by_cos[l][:, :, :], by_sin[l][:, :, :], ALU.add).then_inc(S["rot"], 1)

        @block.scalar
        def _(act):
            first(act, "act")
            act.wait_ge(loaded, 16 * 5)
            act.activation(mask[:, :, :], mask32[:, :, :], ACT.Copy).then_inc(setup, 1)
            act.activation(ident_b[:, :], ident, ACT.Copy).then_inc(setup, 1)
            act.activation(ident_h[:, :], ident, ACT.Copy).then_inc(setup, 1)
            act.wait_ge(setup, 3 + NSET)
            with act.Fori(0, B) as b:
                with act.Fori(0, 2) as half:
                    at = act.snap((b * 2 + half) * FL)
                    for l in lanes:
                        wait(act, "xTp", at + l)
                        act.activation(x_T[l][:, :, :], bank[l][:, 0:D], ACT.Copy).then_inc(S["xT"], 1)
                    for l in lanes:
                        fenced(act, "fa", "rot", at + l)
                        rq = rot[l][:, 0:NH, :]
                        tile = half * FL + l
                        act.activation(q_feat[:, tile, :, 0:HD], rq, ACT.Copy)
                        act.activation(q_feat[:, tile, :, HD:2 * HD], rq, ACT.Copy).then_inc(S["qhi"], 1)
                        act.activation(k_feat[l][:, :, 0, 0:HD], rot[l][:, NH:, :], ACT.Copy)
                        act.activation(k_feat[l][:, :, 0, 2 * HD:3 * HD], rot[l][:, NH:, :], ACT.Copy).then_inc(S["khi"], 1)
                    for l in lanes:
                        fenced(act, "fa", "qTp", at + l)
                        act.activation(q_T[:, :, bass.ds((half * FL + l) * P, P)],
                                       bank[l][:, :].rearrange("p (h t) -> p h t", t=P), ACT.Copy).then_inc(S["qT"], 1)
                for t in range(TPB):
                    wait(act, "q2p", b * TPB + t)
                    act.activation(q_T[:, :, t * P:(t + 1) * P], bank[t % 4][:, :].rearrange("p (h t) -> p h t", t=P), ACT.Copy)\
                        .then_inc(S["q2"], 1)
                with act.Fori(0, NKV) as g:
                    for r in range(4):
                        for kt in range(TPB):
                            u = (b * NKV + g) * NC + (r * TPB + kt)
                            wait(act, "st", u)
                            wait(act, "pv", u, 4)
                            act.activation(prob[kt % 4][:, kt * P:T], bank[kt % 2][:, kt * P:T], ACT.Exp, scale=HD ** -0.5)\
                                .then_inc(S["exp"], 1)
                for h in range(2):
                    for l in lanes:
                        wait(act, "yTp", b * TPB + h * FL + l)
                        act.activation(y_T[l][:, :, :], bank[l][:, 0:D], ACT.Copy).then_inc(S["yT"], 1)

        @block.vector
        def _(dve):
            V = nc.vector
            first(dve, "dve")
            V.memset(q_feat[:, :, :, 3 * HD:], 0.0).then_inc(setup, 1)
            for l in lanes:
                V.memset(k_feat[l][:, :, :, :], 0.0).then_inc(setup, 1)
            V.memset(v_aug[:, :, :, HD:], 0.0).then_inc(setup, 1)
            dve.wait_ge(setup, 3 + 2 + FL)
            for l in lanes:
                V.memset(k_feat[l][:, :, 0, 3 * HD:3 * HD + 1], -1.0)
                V.memset(k_feat[l][:, :, 1, FEAT + 3 * HD:FEAT + 3 * HD + 1], -1.0).then_inc(setup, 1)
            V.memset(v_aug[:, :, :, HD:HD + 1], 1.0).then_inc(setup, 1)
            dve.wait_ge(setup, 3 + NSET)
            dve.wait_ge(loaded, 16 * 5)
            with dve.Fori(0, B) as b:
                with dve.Fori(0, 2) as half:
                    at = dve.snap((b * 2 + half) * FL)
                    for l in lanes:
                        V.bn_stats(stats[l][:, :], x[:, dve.snap(at + l), :]).then_inc(S["stats"], 1)
                    for l in lanes:
                        fenced(dve, "fd", "stats", at + l)
                        V.bn_aggr(mv[l][:, :], stats[l][:, :]).then_inc(S["mv"], 1)
                    for l in lanes:
                        wait(dve, "mv", at + l)
                        wait(dve, "rstd", at + l)
                        V.tensor_scalar(x_norm[l][:, :], x[:, dve.snap(at + l), :], mv[l][:, 0:1], rstd[l][:, 0:1],
                                        ALU.subtract, ALU.mult).then_inc(S["xn"], 1)
                    for l in lanes:
                        fenced(dve, "fd", "proj", at + l)
                        tile = half * FL + l
                        heads = bank[l][:, 512:512 + NR_ * HD].rearrange("p (h d) -> p h d", d=HD)
                        H2 = HD // 2
                        V.tensor_tensor(by_cos[l][:, :, :], heads, cos[:, tile, :][:, None, :].broadcast_to([P, NR_, HD]), ALU.mult)\
                            .then_inc(S["cos"], 1)
                        V.tensor_tensor(by_sin[l][:, :, 0:H2], heads[:, :, H2:], sin[:, tile, 0:H2][:, None, :].broadcast_to([P, NR_, H2]), ALU.mult)
                        V.tensor_tensor(by_sin[l][:, :, H2:], heads[:, :, 0:H2], sin[:, tile, H2:][:, None, :].broadcast_to([P, NR_, H2]), ALU.mult)\
                            .then_inc(S["sin"], 1)
                        V.tensor_copy(v_aug[:, tile, :, 0:HD],
                                      bank[l][:, 512 + NR_ * HD:512 + (NR_ + NKV) * HD].rearrange("p (h d) -> p h d", d=HD)).then_inc(S["v"], 1)
                    for l in lanes:
                        tile = half * FL + l
                        fenced(dve, "fd", "qhi", at + l)
                        V.tensor_tensor(q_feat[:, tile, :, 2 * HD:3 * HD], rot[l][:, 0:NH, :], q_feat[:, tile, :, 0:HD], ALU.subtract)\
                            .then_inc(S["qlo"], 1)
                        wait(dve, "khi", at + l)
                        V.tensor_tensor(k_feat[l][:, :, 0, HD:2 * HD], rot[l][:, NH:, :], k_feat[l][:, :, 0, 0:HD], ALU.subtract)\
                            .then_inc(S["klo"], 1)
                        wait(dve, "klo", at + l)
                        V.tensor_copy(k_feat[l][:, :, 1, FEAT:FEAT + 3 * HD], k_feat[l][:, :, 0, 0:3 * HD]).then_inc(S["kdup"], 1)
                    for l in lanes:
                        fenced(dve, "fd", "kTp", at + l)
                        V.tensor_copy(k_T[:, :, :, :].rearrange("p g c t -> p (g c) t")[:, :, bass.ds((half * FL + l) * P, P)],
                                      bank[l][:, :].rearrange("p (h t) -> p h t", t=P)).then_inc(S["kT"], 1)
                with dve.Fori(0, NKV) as g:
                    for i in range(2 * TPB):
                        half, t = divmod(i, TPB)
                        for h in range(2):
                            fenced(dve, "fd", "score", (b * NKV + g) * 2 * NS + (2 * i + h))
                            V.reduce_max(row_max[:, t, bass.ds(g * 4 + (2 * half + h), 1)], bank[(2 * t + h) % 4][:, 0:(t + 1) * P], axis=AX_X)\
                                .then_inc(S["max"], 1)
                wait(dve, "max", (b * HB + HB) * NS - 1)
                V.tensor_copy(q_feat[:, :, :, 3 * HD], row_max[:, :, :]).then_inc(S["m16"], 1)
                with dve.Fori(0, NKV) as g:
                    at = dve.snap(b * NKV + g)
                    V.tensor_copy(v_group[:, :, :], v_aug[:, :, g, :]).then_inc(S["vg"], 1)
                    wait(dve, "pv", (b * NKV + g) * NC + (NC - 1))
                    V.tensor_copy(o_T[:, :], pv[:, :]).then_inc(S["oT"], 1)
                    wait(dve, "oTp", at)
                    heads = back[:, :].rearrange("p (h d) -> p h d", d=32)
                    V.reciprocal(inv_sum[:, :], heads[:, :, HD]).then_inc(S["inv"], 1)
                    wait(dve, "inv", at)
                    for t in range(TPB):
                        four = slice(4 * t, 4 * t + 4)
                        last = V.tensor_tensor(y[:, t, bass.ds(g * 4 * HD, 4 * HD)].rearrange("p (r d) -> p r d", d=HD), heads[:, four, 0:HD],
                                               inv_sum[:, four][:, :, None].broadcast_to([P, 4, HD]), ALU.mult)
                    last.then_inc(S["y"], 1)
                for h in range(2):
                    for l in lanes:
                        tile = b * TPB + h * FL + l
                        wait(dve, "out", tile)
                        V.tensor_tensor(x[:, tile, :], x[:, tile, :], bank[l][:, 512:512 + D], ALU.add).then_inc(S["x"], 1)

        @block.tensor
        def _(pe):
            first(pe, "pe")
            pe.wait_ge(setup, 3 + NSET)
            with pe.Fori(0, B) as b:
                with pe.Fori(0, 2) as half:
                    at = pe.snap((b * 2 + half) * FL)
                    for l in lanes:
                        wait(pe, "xn", at + l)
                        wait(pe, "kT", at, 1)
                        for k in range(KD):
                            last = pe.transpose(bank[l][:, k * P:(k + 1) * P], x_norm[l][:, k * P:(k + 1) * P], ident)
                        last.then_inc(S["xTp"], 1)
                    for l in lanes:
                        wait(pe, "xT", at + l)
                        for k in range(KD):
                            last = pe.matmul(bank[l][:, 512:512 + QW + 2 * NKV * HD], x_T[l][:, k, :], w_qkv[:, k, :],
                                             start=(k == 0), stop=(k == KD - 1))
                        last.then_inc(S["proj"], 1)
                    for l in lanes:
                        fenced(pe, "fp", "qlo", at + l)
                        fenced(pe, "fp", "v", at + l)
                        flat = q_feat[:, half * FL + l, :, :].rearrange("p h f -> p (h f)")
                        for i in range(HB):
                            last = pe.matmul(bank[l][:, i * P:(i + 1) * P], flat[:, i * P:(i + 1) * P], ident_h[:, :], start=True, stop=True)
                        last.then_inc(S["qTp"], 1)
                    for l in lanes:
                        wait(pe, "qT", at + l)
                        wait(pe, "kdup", at + l)
                        flat = k_feat[l][:, :, :, :].rearrange("p g c f -> p (g c f)")
                        for i in range(2 * NKV):
                            last = pe.matmul(bank[l][:, i * P:(i + 1) * P], flat[:, i * P:(i + 1) * P], ident_h[:, :], start=True, stop=True)
                        last.then_inc(S["kTp"], 1)
                fenced(pe, "fp", "kT", b * TPB + (TPB - 1))
                with pe.Fori(0, NKV) as g:
                    for i in range(2 * TPB):
                        half, t = divmod(i, TPB)
                        hb = pe.snap(g * 2 + half)
                        for h in range(2):
                            out = bank[(2 * t + h) % 4]
                            fenced(pe, "fp", "max", (b * NKV + g) * 2 * NS + (2 * i + h), 4)
                            n = (t + 1) * P
                            for lo in range(0, n, 512):
                                hi = min(lo + 512, n)
                                pe.matmul(out[:, lo:hi], q_T[:, hb, t * P:(t + 1) * P], k_T[:, g, h, lo:hi],
                                          start=True, stop=(hi < n))
                            pe.matmul(out[:, t * P:n], ident_b[:, :], mask[:, 0, :], start=False, stop=True).then_inc(S["score"], 1)
                for t in range(TPB):
                    wait(pe, "m16", b)
                    if t >= 4:
                        wait(pe, "q2", b * TPB + (t - 4))
                    flat = q_feat[:, t, :, :].rearrange("p h f -> p (h f)")
                    for i in range(HB):
                        last = pe.matmul(bank[t % 4][:, i * P:(i + 1) * P], flat[:, i * P:(i + 1) * P], ident_h[:, :], start=True, stop=True)
                    last.then_inc(S["q2p"], 1)
                fenced(pe, "fp", "q2", b * TPB + (TPB - 1))
                with pe.Fori(0, NKV) as g:
                    group = pe.snap(b * NKV + g)

                    def values(i):
                        r, kt = divmod(i, TPB)
                        fenced(pe, "fp", "exp", group * NC + i)
                        if i == 0:
                            fenced(pe, "fp", "vg", group)
                            fenced(pe, "fp", "oT", group, 1)
                        for lo in (0, 512):
                            start = max(lo, kt * P)
                            if start < lo + 512:
                                last = pe.matmul(pv[32 * r:32 * r + 32, start:lo + 512], v_group[:, kt, :], prob[kt % 4][:, start:lo + 512],
                                                 start=(kt == 0), stop=(kt * P + P == lo + 512), tile_position=(0, 32 * r))
                        last.then_inc(S["pv"], 1)

                    for r in range(4):
                        hb = pe.snap(g * 2 + r // 2)
                        for kt in range(TPB):
                            i = r * TPB + kt
                            fenced(pe, "fp", "exp", group * NC + i, 2)
                            out = bank[kt % 2]
                            for lo in (0, 512):
                                start = max(lo, kt * P)
                                if start < lo + 512:
                                    pe.matmul(out[:, start:lo + 512], k_T[:, g, r % 2, kt * P:(kt + 1) * P], q_T[:, hb, start:lo + 512],
                                              start=True, stop=(start != kt * P))
                            pe.matmul(out[:, kt * P:(kt + 1) * P], ident_b[:, :], mask[:, 1, :], start=False, stop=True).then_inc(S["st"], 1)
                            if i > 0:
                                values(i - 1)
                    values(NC - 1)
                    wait(pe, "oT", group)
                    wait(pe, "y", group, 1)
                    for t in range(TPB):
                        last = pe.transpose(back[:, t * P:(t + 1) * P], o_T[:, t * P:(t + 1) * P], ident)
                    last.then_inc(S["oTp"], 1)
                wait(pe, "y", b * NKV + (NKV - 1))
                for h in range(2):
                    for l in lanes:
                        if h == 1:
                            wait(pe, "x", b * TPB + l)
                        t = h * FL + l
                        for k in range(KD):
                            last = pe.transpose(bank[l][:, k * P:(k + 1) * P], y[:, t, k * P:(k + 1) * P], ident)
                        last.then_inc(S["yTp"], 1)
                    for l in lanes:
                        wait(pe, "yT", b * TPB + h * FL + l)
                        for k in range(KD):
                            last = pe.matmul(bank[l][:, 512:512 + D], y_T[l][:, k, :], w_o[:, k, :], start=(k == 0), stop=(k == KD - 1))
                        last.then_inc(S["out"], 1)


def moe_ffn(nc, x, ident, small, dram):
    with ExitStack() as ctx:
        def sb(name, shape, dt=F32):
            return ctx.enter_context(nc.sbuf_tensor("moe_" + name, shape, dt))

        def sem(name):
            return ctx.enter_context(nc.semaphore("moe_" + name))

        lanes = range(FL)
        TOK = FL * P
        parts = ("hi", "lo")
        w_gu = {s: sb(f"w_gu_{s}", [P, KD, NEXP * 2 * IP], F16) for s in parts}
        w_dn = {s: sb(f"w_dn_{s}", [P, KI, NEXP * D], F16) for s in parts}
        w_route = sb("w_route", [P, KD, NEXP])
        before = sb("before", [P, FL * NR * NR])
        stage = [sb(f"stage{i}", [P, KD * 2 * IP]) for i in range(2)]

        with ExitStack() as c1:
            staged = c1.enter_context(nc.semaphore("moe_staged"))
            others = c1.enter_context(nc.semaphore("moe_route_loaded"))
            hi_done = c1.enter_context(nc.semaphore("moe_hi_done"))
            lo_done = c1.enter_context(nc.semaphore("moe_lo_done"))
            c1.callback(clear_semaphores, nc, [staged, others, hi_done, lo_done])
            block = c1.enter_context(nc.Block())
            jobs = [(e, kind) for e in range(NEXP) for kind in range(2)]

            def views(n):
                e, kind = jobs[n]
                if kind == 0:
                    st = stage[n % 2][:, :].rearrange("p (k i) -> p k i", k=KD)
                    return st, [w_gu[s][:, :, e * 2 * IP:(e + 1) * 2 * IP] for s in parts], dram["w_gate_up"][e]
                st = stage[n % 2][:, 0:KI * D].rearrange("p (k i) -> p k i", k=KI)
                return st, [w_dn[s][:, :, e * D:(e + 1) * D] for s in parts], dram["w_down"][e]

            @block.sync
            def _(sp):
                sp.dma_start(w_route[:, :, :], dram["w_route"]).then_inc(others, 16)
                sp.dma_start(before[:, :], dram["before"]).then_inc(others, 16)
                for n in range(len(jobs)):
                    st, _, src = views(n)
                    if n >= 2:
                        sp.wait_ge(lo_done, n - 1)
                    sp.dma_start(st, src).then_inc(staged, 16)
                    if n % 2 == 1:
                        sp.wait_ge(staged, 16 * (n + 1))
                sp.wait_ge(others, 32)

            @block.scalar
            def _(act):
                for n in range(len(jobs)):
                    st, (hi, lo), _ = views(n)
                    act.wait_ge(staged, 16 * (n + 1 + (n + 1) % 2))
                    act.activation(hi, st, ACT.Copy).then_inc(hi_done, 1)

            @block.vector
            def _(dve):
                for n in range(len(jobs)):
                    st, (hi, lo), _ = views(n)
                    dve.wait_ge(hi_done, n + 1)
                    dve.tensor_tensor(lo, st, hi, ALU.subtract).then_inc(lo_done, 1)

        stats = [sb(f"stats{l}", [P, 6]) for l in lanes]
        mv = [sb(f"mv{l}", [P, 2]) for l in lanes]
        var_eps = [sb(f"var_eps{l}", [P, 1]) for l in lanes]
        rstd = [sb(f"rstd{l}", [P, 1]) for l in lanes]
        res = [sb(f"res{l}", [P, D]) for l in lanes]
        x_norm = [sb(f"x_norm{l}", [P, D]) for l in lanes]
        x_T = sb("x_T", [P, KD, TOK])
        x_T_hi, x_T_lo = sb("x_T_hi", [P, KD, TOK], F16), sb("x_T_lo", [P, KD, TOK], F16)
        silu = [sb(f"silu{i}", [P, TOK]) for i in range(2)]
        hidden = [sb(f"hidden{i}", [P, TOK]) for i in range(2)]
        hid_hi = sb("hid_hi", [P, 2 * KI, TOK], F16)
        hid_lo = sb("hid_lo", [P, 2 * KI, TOK], F16)
        logit = sb("logit", [P, FL, NEXP])
        score = sb("score", [P, FL * NR])
        top = sb("top", [P, FL])
        e_arg, e_val = sb("e_arg", [P, FL, NEXP]), sb("e_val", [P, FL, NEXP])
        other = sb("other", [P, FL * NR, NR])
        above, not_below = sb("above", [P, FL * NR, NR]), sb("not_below", [P, FL * NR, NR])
        rank, chosen = sb("rank", [P, FL * NR]), sb("chosen", [P, FL * NR])
        total, inv_total = sb("total", [P, FL]), sb("inv_total", [P, FL])
        shared_d = sb("shared_d", [P, FL])
        share = [sb(f"share{i}", [P, FL, NEXP]) for i in range(1)]
        turn = [ctx.enter_context(nc.psum_tensor(f"moe_turn{k}", [P, 512], F32)) for k in range(KD)]
        gate_p = [ctx.enter_context(nc.psum_tensor(f"moe_gate_p{i}", [P, 512], F32)) for i in range(2)]
        up_p = [ctx.enter_context(nc.psum_tensor(f"moe_up_p{i}", [P, 512], F32)) for i in range(2)]
        out_p = [ctx.enter_context(nc.psum_tensor(f"moe_out_p{i}", [P, 512], F32)) for i in range(2)]

        names = {"dve": ["res_s", "stats_s", "mv_s", "xn_s", "lo_s", "hid_s", "hlo_s", "sum_s", "back_s", "fence"],
                 "act": ["xT_s", "xhi_s", "exp_s", "silu_s", "hhi_s"],
                 "pe": ["turn_s", "logit_s", "gu_s", "out_s"], "pool": ["ve_s", "rstd_s"]}
        S = {n: sem(n) for g in names.values() for n in g}
        route = sem("route")
        block = ctx.enter_context(nc.Block())
        NU = NEXP * KI

        SUM0 = FL + 1

        def buf(half, i):
            return (half * KI + i) % 2

        def first(eng, g):
            for n in names[g]:
                eng.sem_inc(S[n], 1)

        def lane_counts(eng, it):
            return [eng.snap(it * FL + k + 1) for k in range(FL + 1)]

        @block.gpsimd
        def _(pool):
            first(pool, "pool")
            with pool.Fori(0, NT // FL) as it:
                n = lane_counts(pool, it)
                for l in lanes:
                    pool.wait_ge(S["mv_s"], n[l + 1])
                    pool.tensor_tensor(var_eps[l][:, :], mv[l][:, 1:2], small[:, 2:3], ALU.add).then_inc(S["ve_s"], 1)
                    pool.wait_ge(S["ve_s"], n[l + 1])
                    pool.tensor_tensor(rstd[l][:, :], var_eps[l][:, :], small[:, 0:1], ALU.pow).then_inc(S["rstd_s"], 1)

        @block.tensor
        def _(pe):
            first(pe, "pe")

            def units(it, e, half):
                for i in range(KI):
                    u = it * NU + e * KI + i
                    pe.wait_ge(S["hid_s"], pe.snap(u + 1 if isinstance(e, int) and i == 0 else u))
                    for which, bank in enumerate((gate_p[buf(half, i)], up_p[buf(half, i)])):
                        n = 0
                        for k in range(KD):
                            col = bass.ds(e * 2 * IP + which * IP + i * P, P)
                            for w_, x_ in ((w_gu["hi"], x_T_hi), (w_gu["lo"], x_T_hi), (w_gu["hi"], x_T_lo)):
                                last = pe.matmul(bank[:, :], w_[:, k, col], x_[:, k, :], start=(n == 0), stop=(n == 3 * KD - 1))
                                n += 1
                    last.then_inc(S["gu_s"], 1)

            def down(it, e, half):
                pe.wait_ge(S["hlo_s"], pe.snap(it * NU + e * KI + KI + 1))
                for l in lanes:
                    pe.wait_ge(S["sum_s"], pe.snap(it * (NEXP * FL) + e * FL + l + SUM0 - 1))
                    n = 0
                    for i in range(KI):
                        tok = slice(l * P, (l + 1) * P)
                        col = bass.ds(e * D, D)
                        for h_, w_ in ((hid_hi, w_dn["hi"]), (hid_hi, w_dn["lo"]), (hid_lo, w_dn["hi"])):
                            last = pe.matmul(out_p[l % 2][:, 0:D], h_[:, half * KI + i, tok], w_[:, i, col],
                                             start=(n == 0), stop=(n == 3 * KI - 1))
                            n += 1
                    last.then_inc(S["out_s"], 1)

            with pe.Fori(0, NT // FL) as it:
                n = lane_counts(pe, it)
                for l in lanes:
                    pe.wait_ge(S["xn_s"], n[l + 1])
                    for k in range(KD):
                        last = pe.transpose(turn[k][:, l * P:(l + 1) * P], x_norm[l][:, k * P:(k + 1) * P], ident)
                    last.then_inc(S["turn_s"], 1)
                pe.wait_ge(S["lo_s"], pe.snap(it * KD + KD + 1))
                for l in lanes:
                    for k in range(KD):
                        last = pe.matmul(turn[0][:, l * 16:l * 16 + NEXP], x_T[:, k, l * P:(l + 1) * P], w_route[:, k, :],
                                         start=(k == 0), stop=(k == KD - 1))
                last.then_inc(S["logit_s"], 1)
                units(it, 0, 0)
                with pe.Fori(0, NEXP // 2) as pair:
                    units(it, 2 * pair + 1, 1)
                    down(it, 2 * pair, 0)
                    units(it, 2 * pair + 2, 0)
                    down(it, 2 * pair + 1, 1)
                down(it, NEXP - 1, 0)

        @block.scalar
        def _(act):
            first(act, "act")

            def units(it, e, half):
                for i in range(KI):
                    u = act.snap(it * NU + e * KI + i + 2)
                    act.wait_ge(S["gu_s"], u)
                    act.activation(silu[buf(half, i)][:, :], gate_p[buf(half, i)][:, :], ACT.Silu).then_inc(S["silu_s"], 1)
                    act.wait_ge(S["hid_s"], u)
                    act.activation(hid_hi[:, half * KI + i, :], hidden[buf(half, i)][:, :], ACT.Copy).then_inc(S["hhi_s"], 1)

            with act.Fori(0, NT // FL) as it:
                n = lane_counts(act, it)
                act.wait_ge(S["turn_s"], n[FL])
                for k in range(KD):
                    act.activation(x_T[:, k, :], turn[k][:, :], ACT.Copy).then_inc(S["xT_s"], 1)
                    act.activation(x_T_hi[:, k, :], turn[k][:, :], ACT.Copy).then_inc(S["xhi_s"], 1)
                act.wait_ge(route, act.snap(it * ROUTE + 4))
                act.activation(e_val[:, :, :], e_arg[:, :, :], ACT.Exp).then_inc(S["exp_s"], 1)
                units(it, 0, 0)
                with act.Fori(0, NEXP // 2) as pair:
                    units(it, 2 * pair + 1, 1)
                    units(it, 2 * pair + 2, 0)

        @block.vector
        def _(dve):
            first(dve, "dve")
            dve.sem_inc(S["sum_s"], SUM0 - 1)
            V = nc.vector

            def units(it, e, half):
                for i in range(KI):
                    u = dve.snap(it * NU + e * KI + i + 2)
                    dve.wait_ge(S["silu_s"], u)
                    dve.tensor_tensor(hidden[buf(half, i)][:, :], silu[buf(half, i)][:, :], up_p[buf(half, i)][:, :], ALU.mult).then_inc(S["hid_s"], 1)
                    dve.wait_ge(S["hhi_s"], u)
                    dve.tensor_tensor(hid_lo[:, half * KI + i, :], hidden[buf(half, i)][:, :], hid_hi[:, half * KI + i, :], ALU.subtract)\
                        .then_inc(S["hlo_s"], 1)

            def down(it, e):
                for l in lanes:
                    base = it * (NEXP * FL) + e * FL + l
                    dve.wait_ge(S["out_s"], dve.snap(base + 2))
                    dve.wait_ge(S["sum_s"], dve.snap(base + 1 + SUM0 - FL))
                    dve.scalar_tensor_tensor(out=res[l][:, :], in0=out_p[l % 2][:, 0:D], scalar=share[0][:, l, bass.ds(e, 1)],
                                             in1=res[l][:, :], op0=ALU.mult, op1=ALU.add).then_inc(S["sum_s"], 1)

            with dve.Fori(0, NT // FL) as it:
                n = lane_counts(dve, it)
                dve.wait_ge(S["back_s"], n[0])
                dve.sem_inc(S["fence"], 1)
                for l in lanes:
                    dve.tensor_copy(res[l][:, :], x[:, dve.snap(it * FL + l), :]).then_inc(S["res_s"], 1)
                for l in lanes:
                    dve.wait_ge(S["res_s"], n[l + 1])
                    dve.sem_inc(S["fence"], 1)
                    dve.bn_stats(stats[l][:, :], res[l][:, :]).then_inc(S["stats_s"], 1)
                for l in lanes:
                    dve.wait_ge(S["stats_s"], n[l + 1])
                    dve.sem_inc(S["fence"], 1)
                    dve.bn_aggr(mv[l][:, :], stats[l][:, :]).then_inc(S["mv_s"], 1)
                for l in lanes:
                    dve.wait_ge(S["mv_s"], n[l + 1])
                    dve.wait_ge(S["rstd_s"], n[l + 1])
                    dve.tensor_scalar(x_norm[l][:, :], res[l][:, :], mv[l][:, 0:1], rstd[l][:, 0:1],
                                      ALU.subtract, ALU.mult).then_inc(S["xn_s"], 1)
                for k in range(KD):
                    dve.wait_ge(S["xhi_s"], dve.snap(it * KD + k + 2))
                    dve.tensor_tensor(x_T_lo[:, k, :], turn[k][:, :], x_T_hi[:, k, :], ALU.subtract).then_inc(S["lo_s"], 1)

                link = Chain(dve, route, dve.snap(it * ROUTE), ROUTE)
                dve.wait_ge(S["logit_s"], dve.snap(it + 2))
                link(V.tensor_copy(logit[:, :, :], turn[0][:, 0:FL * 16].rearrange("p (t e) -> p t e", t=FL)[:, :, 0:NEXP]))
                V.tensor_copy(score[:, :].rearrange("p (t e) -> p t e", t=FL), logit[:, :, 0:NR])
                V.tensor_scalar(e_arg[:, :, NR], logit[:, :, NR], -80.0, -1.0, ALU.max, ALU.mult)
                link(V.reduce_max(top[:, :], logit[:, :, 0:NR], axis=AX_X))
                link(V.tensor_tensor(e_arg[:, :, 0:NR], logit[:, :, 0:NR], top[:, :, None].broadcast_to([P, FL, NR]), ALU.subtract))
                link(V.tensor_copy(total[:, :], top[:, :]))
                for l in lanes:
                    ins = V.tensor_copy(other[:, l * NR:(l + 1) * NR, :],
                                        score[:, l * NR:(l + 1) * NR][:, None, :].broadcast_to([P, NR, NR]))
                link(ins)
                mine = score[:, :, None].broadcast_to([P, FL * NR, NR])
                V.tensor_tensor(above[:, :, :], other[:, :, :], mine, ALU.is_gt)
                link(V.tensor_tensor(not_below[:, :, :], other[:, :, :], mine, ALU.is_ge))
                link(V.tensor_tensor(not_below[:, :, :], not_below[:, :, :], above[:, :, :], ALU.subtract))
                link(V.tensor_tensor(not_below[:, :, :], not_below[:, :, :], before[:, :].rearrange("p (e j) -> p e j", j=NR), ALU.mult))
                link(V.tensor_tensor(above[:, :, :], above[:, :, :], not_below[:, :, :], ALU.add))
                link(V.reduce_sum(rank[:, :], above[:, :, :], axis=AX_X))
                link(V.tensor_scalar(chosen[:, :], rank[:, :], float(TOPK), None, ALU.is_lt))
                dve.wait_ge(S["exp_s"], dve.snap(it + 2))
                V.tensor_scalar(shared_d[:, :], e_val[:, :, NR], 1.0, None, ALU.add)
                link(V.tensor_tensor(share[0][:, :, 0:NR], e_val[:, :, 0:NR], chosen[:, :].rearrange("p (t e) -> p t e", t=FL), ALU.mult))
                V.reciprocal(share[0][:, :, NR], shared_d[:, :])
                link(V.reduce_sum(total[:, :], share[0][:, :, 0:NR], axis=AX_X))
                link(V.reciprocal(inv_total[:, :], total[:, :]))
                link(V.tensor_tensor(share[0][:, :, 0:NR], share[0][:, :, 0:NR], inv_total[:, :, None].broadcast_to([P, FL, NR]), ALU.mult))
                link.close()

                units(it, 0, 0)
                with dve.Fori(0, NEXP // 2) as pair:
                    units(it, 2 * pair + 1, 1)
                    down(it, 2 * pair)
                    units(it, 2 * pair + 2, 0)
                    down(it, 2 * pair + 1)
                down(it, NEXP - 1)
                for l in lanes:
                    dve.wait_ge(S["sum_s"], dve.snap(it * (NEXP * FL) + (NEXP - 1) * FL + l + 1 + SUM0))
                    dve.sem_inc(S["fence"], 1)
                    dve.tensor_copy(x[:, dve.snap(it * FL + l), :], res[l][:, :]).then_inc(S["back_s"], 1)


def cap_array():
    r, c = np.arange(P)[:, None], np.arange(P)[None, :]
    return np.where((r < c) & (r // CH == c // CH), 3e38, -1e30).astype(np.float32)


def last_row_arrays():
    out = np.zeros((2, P, P), np.float32)
    for c in range(2):
        out[c, (c + 1) * CH - 1] = 1.0
    return out


def layouts(a):
    out = {
        "x": a["L0_attn_out"].reshape(B * T, D),
        "masks": mask_arrays(),
        "w_write": a["L0_attn_W_write"].T,
        "w_alpha_rows": a["L0_attn_W_alpha"],
        "cap": cap_array(),
        "last_row": last_row_arrays(),
        "w_beta": a["L0_attn_W_beta"].T,
        "w_read": a["L0_attn_W_read"].T,
        "a_log": a["L0_attn_A_log"],
        "dt_bias": a["L0_attn_dt_bias"],
        "small": np.repeat(np.array([[-0.5, -0.5, EPS, EPS, 0.5]], np.float32), P, 0),
    }
    group_of = np.arange(D) // GROUP
    out.update({
        "qweights": a["L0_ffn_qweights"].transpose(0, 2, 1),
        "scales": a["L0_ffn_scales"].transpose(2, 0, 1),
        "spread": (np.arange(D // GROUP)[:, None] == group_of[None, :]).astype(np.float32).reshape(D // GROUP, KD, P),
        "biases": a["L0_ffn_biases"],
        "lora_a": a["L0_ffn_lora_a"].transpose(1, 0, 2),
        "lora_b": a["L0_ffn_lora_b"].transpose(2, 0, 1),
        "ln_gamma": a["L0_ffn_ln_gamma"].reshape(NBLK, KD, P).transpose(2, 0, 1),
        "ln_beta": a["L0_ffn_ln_beta"].reshape(NBLK, KD, P).transpose(2, 0, 1),
    })

    half = HD // 2
    inv_freq = (1.0 / np.power(10000.0, np.arange(half) / half)).astype(np.float32)
    angle = (np.arange(T, dtype=np.float32)[:, None] * inv_freq[None, :]).astype(np.float32).astype(np.float64)
    sines = np.concatenate([-np.sin(angle), np.sin(angle)], 1)
    cosines = np.concatenate([np.cos(angle)] * 2, 1)

    def by_tile(v):
        return v.astype(np.float32).reshape(TPB, P, HD).transpose(1, 0, 2)

    def slices(w):
        return w.reshape(KD, P, -1).transpose(1, 0, 2)

    later = (np.arange(P)[None, :] > np.arange(P)[:, None])
    out.update({
        "w_qkv": slices(np.concatenate([a["L1_attn_Wq"], a["L1_attn_Wk"], a["L1_attn_Wv"]], 1)),
        "w_o": slices(a["L1_attn_Wo"]),
        "cos": by_tile(cosines),
        "sin": by_tile(sines),
        "causal": np.stack([np.where(later, -1e30, 0), np.where(later.T, -1e30, 0)], 1).astype(np.float32),
    })

    def padded(w, axis):
        pad = [(0, 0)] * w.ndim
        pad[axis] = (0, IP - w.shape[axis])
        return np.pad(w, pad)

    gate, up, dn = (np.concatenate([a["L1_ffn_w_" + n], a["L1_ffn_sw_" + n][None]], 0) for n in ("gate", "up", "down"))
    both = np.concatenate([padded(gate, 2), padded(up, 2)], 2)
    earlier = (np.arange(NR)[None, :] < np.arange(NR)[:, None]).astype(np.float32).reshape(1, -1)
    out.update({
        "w_gate_up": both.reshape(NEXP, KD, P, 2 * IP).transpose(0, 2, 1, 3),
        "w_down": padded(dn, 1).reshape(NEXP, KI, P, D).transpose(0, 2, 1, 3),
        "w_route": np.concatenate([a["L1_ffn_gate_w"], a["L1_ffn_shared_gate_w"]], 0).T.reshape(KD, P, NEXP).transpose(1, 0, 2),
        "before": np.repeat(np.tile(earlier, (1, FL)), P, 0),
    })
    return out


def store(nc, x, out_dram):
    with ExitStack() as ctx:
        stored = ctx.enter_context(nc.semaphore("stored"))
        block = ctx.enter_context(nc.Block())

        @block.sync
        def _(sp):
            for b in range(B):
                sp.dma_start(out_dram[b * T:(b + 1) * T, :].rearrange("(t p) d -> p t d", p=P),
                             x[:, b * TPB:(b + 1) * TPB, :]).then_inc(stored, 16)
            sp.wait_ge(stored, 16 * B)


def load_constants(nc, masks, small, dram, x=None):
    with ExitStack() as ctx:
        constants_loaded = ctx.enter_context(nc.semaphore("constants_loaded"))
        ctx.callback(clear_semaphores, nc, [constants_loaded])
        block = ctx.enter_context(nc.Block())

        @block.sync
        def _(sp):
            sp.dma_start(masks[:, :, :], dram["masks"]).then_inc(constants_loaded, 16)
            sp.dma_start(small[:, :], dram["small"]).then_inc(constants_loaded, 16)
            if x is not None:
                sp.dma_start(x[:, :, :], dram["x"].rearrange("(t p) d -> p t d", p=P)).then_inc(constants_loaded, 16)
            sp.wait_ge(constants_loaded, 48 if x is not None else 32)


def build_program(nc, dram, out_dram, stages):
    with ExitStack() as ctx:
        x = ctx.enter_context(nc.sbuf_tensor("x", [P, NT, D], F32))
        masks = ctx.enter_context(nc.sbuf_tensor("masks", [P, len(MASKS), P], F32))
        small = ctx.enter_context(nc.sbuf_tensor("small", [P, 5], F32))
        ident = masks[:, 0, :]
        if 1 in stages:
            with ExitStack() as c2:
                cums = c2.enter_context(nc.sbuf_tensor("cums", [P, NT, NCUM], F32))
                load_constants(nc, masks, small, dram)
                first_norm(nc, x, small, dram, cums)
                decay_sums(nc, x, ident, small, dram, cums)
                delta_attention(nc, x, ident, masks, small, dram, cums)
        else:
            load_constants(nc, masks, small, dram, x)
        if 2 in stages:
            quantised_ffn(nc, x, ident, small, dram)
        if 3 in stages:
            gqa_attention(nc, x, ident, small, dram)
        if 4 in stages:
            moe_ffn(nc, x, ident, small, dram)
        store(nc, x, out_dram)


STAGES = (1, 2, 3, 4)


def kernel(**inputs):
    import concourse.bacc as bacc
    from concourse.bass_utils import run_bass_kernel_spmd as run

    a = {k: np.asarray(v) for k, v in inputs.items()}
    arrays = layouts(a)
    nc = bacc.Bacc("TRN2", target_bir_lowering=False, num_devices=1)
    dram, feed = {}, {}
    for name, value in arrays.items():
        value = np.ascontiguousarray(value)
        feed["in_" + name] = value
        dram[name] = nc.dram_tensor("in_" + name, value.shape, mybir.dt.from_np(value.dtype), kind="ExternalInput").ap()
    out = nc.dram_tensor("out", (B * T, D), F32, kind="ExternalOutput").ap()
    build_program(nc, dram, out, STAGES)
    got = run(nc, [feed], core_ids=[0]).results[0]["out"]
    return got.reshape(B, T, D)
```

```python
import math
from contextlib import ExitStack

import numpy as np

import concourse.bass as bass
from concourse import mybir

F32 = mybir.dt.float32
F16 = mybir.dt.float16
BF16 = mybir.dt.bfloat16
I32 = mybir.dt.int32
ACT = mybir.ActivationFunctionType
ALU = mybir.AluOpType
AX_X = mybir.AxisListType.X

P = 128
B, T, D = 8, 1024, 256
TPB = T // P
NT = B * TPB
KD = D // P
EPS = 1e-5

H0, HD0, CH = 2, 128, 64
LEVELS = int(math.log2(CH))
BL = 2
NCUM = 12
LN0 = BL * H0

NBLK, GROUP, RANK = 3, 16, 32
NLIN = 2 * NBLK
FL = 4

NH, NKV, HD = 16, 4, 16
FEAT = 64
NSET = 4 + FL + FL + 1

NR, TOPK = 8, 2
NEXP = NR + 1
WIDTH = 352
KI = -(-WIDTH // P)
IP = KI * P
ROUTE = 14

MASKS = ["ident", "ones"] + [f"level{k}" for k in range(LEVELS)]


def mask_arrays():
    r, c = np.arange(P)[:, None], np.arange(P)[None, :]
    out = {
        "ident": r == c,
        "ones": np.ones((P, P), bool),
    }
    for k in range(LEVELS):
        half = 1 << k
        low = ((r // (2 * half)) == (c // (2 * half))) & ((r // half) % 2 == 1) & ((c // half) % 2 == 0)
        out[f"level{k}"] = low.T if k == 0 else low
    return np.ascontiguousarray(np.stack([out[m] for m in MASKS], 1).astype(np.float32))


def clear_semaphores(nc, semaphores):
    with nc.Block() as block:

        @block.gpsimd
        def _(pool):
            for s in semaphores:
                pool.sem_clear(s)


class Chain:

    def __init__(self, eng, sem, base=0, per_round=None):
        self.eng, self.sem, self.base, self.n, self.per_round = eng, sem, base, 0, per_round

    def __call__(self, ins):
        self.n += 1
        ins.then_inc(self.sem, 1)
        self.eng.wait_ge(self.sem, self.base + self.n)

    def close(self):
        assert self.per_round is None or self.n == self.per_round, self.n


EXP_P = [1.9875691500e-4, 1.3981999507e-3, 8.3334519073e-3, 4.1665795894e-2, 1.6666665459e-1, 5.0000001201e-1]
LOG_P = [4.5270000862445199635215e-5, 4.9854102823193375972212e-1, 6.5787325942061044846969, 2.9911919328553073277375e1,
         6.0949667980987787057556e1, 5.7112963590585538103336e1, 2.0039553499201281259648e1]
LOG_Q = [1.0, 1.5062909083469192043167e1, 8.3047565967967209469434e1, 2.2176239823732856465394e2,
         3.0909872225312059774938e2, 2.1642788614495947685003e2, 6.0118660497603843919306e1]
SPLIT = 4097.0
ROUND = 12582912.0


def exp_f32(nc, link, out, x, n, t, z, y, bits):
    v = nc.vector
    link(v.tensor_scalar(n, x, 1.44269504088896341, ROUND, ALU.mult, ALU.add))
    link(v.tensor_scalar(n, n, -ROUND, None, ALU.add))
    link(v.scalar_tensor_tensor(out=t, in0=n, scalar=-0.693359375, in1=x, op0=ALU.mult, op1=ALU.add))
    link(v.scalar_tensor_tensor(out=t, in0=n, scalar=2.12194440e-4, in1=t, op0=ALU.mult, op1=ALU.add))
    link(v.tensor_tensor(z, t, t, ALU.mult))
    link(v.tensor_scalar(y, t, EXP_P[0], None, ALU.mult))
    for c in EXP_P[1:-1]:
        link(v.scalar_tensor_tensor(out=y, in0=y, scalar=c, in1=t, op0=ALU.add, op1=ALU.mult))
    link(v.scalar_tensor_tensor(out=y, in0=y, scalar=EXP_P[-1], in1=z, op0=ALU.add, op1=ALU.mult))
    link(v.tensor_tensor(y, y, t, ALU.add))
    link(v.tensor_scalar(y, y, 1.0, None, ALU.add))
    link(v.tensor_scalar(bits, n, 127.0, 8388608.0, ALU.add, ALU.mult))
    link(v.tensor_tensor(out, y, bits.bitcast(F32), ALU.mult))


def horner(nc, link, out, x, cs):
    v = nc.vector
    link(v.tensor_scalar(out, x, cs[0], None, ALU.mult))
    for c in cs[1:-1]:
        link(v.scalar_tensor_tensor(out=out, in0=out, scalar=c, in1=x, op0=ALU.add, op1=ALU.mult))
    link(v.tensor_scalar(out, out, cs[-1], None, ALU.add))


def first_norm(nc, x, small, dram, cums):
    HT = NT // 2
    with ExitStack() as ctx:
        def sb(name, shape, dt=F32):
            return ctx.enter_context(nc.sbuf_tensor("norm_" + name, shape, dt))

        mean = sb("mean", [P, NT])
        var = sb("var", [P, NT])
        root = sb("root", [P, NT])
        inv_root = sb("inv_root", [P, NT])
        root_hi, root_lo = sb("root_hi", [P, NT]), sb("root_lo", [P, NT])
        s0, s1 = sb("s0", [P, NT]), sb("s1", [P, NT])
        with ExitStack() as c1:
            acc = c1.enter_context(nc.sbuf_tensor("norm_acc", [P, HT, 16], F32))
            square = c1.enter_context(nc.sbuf_tensor("norm_square", [P, HT, D], F32))
            x_loaded = c1.enter_context(nc.semaphore("norm_x_loaded"))
            stats_done = c1.enter_context(nc.semaphore("norm_stats_done"))
            root_done = c1.enter_context(nc.semaphore("norm_root_done"))
            root_first = c1.enter_context(nc.semaphore("norm_root_first"))
            c1.callback(clear_semaphores, nc, [x_loaded, stats_done, root_done, root_first])
            block = c1.enter_context(nc.Block())

            @block.sync
            def _(sp):
                for half in range(2):
                    sp.dma_start(x[:, half * HT:(half + 1) * HT, :],
                                 dram["x"][half * HT * P:(half + 1) * HT * P, :].rearrange("(t p) d -> p t d", p=P))\
                        .then_inc(x_loaded, 16)
                    sp.wait_ge(x_loaded, 16 * (half + 1))

            @block.gpsimd
            def _(pool):
                pool.wait_ge(stats_done, 1)
                pool.tensor_tensor(root[:, :], var[:, :], small[:, 4:5].broadcast_to([P, NT]), ALU.pow).then_inc(root_first, 1)

            @block.vector
            def _(dve):
                link = Chain(dve, root_done)
                v = nc.vector
                for half in range(2):
                    xs = x[:, half * HT:(half + 1) * HT, :]
                    ms = mean[:, half * HT:(half + 1) * HT]
                    vs = var[:, half * HT:(half + 1) * HT]
                    dve.wait_ge(x_loaded, 16 * (half + 1))
                    link(v.tensor_tensor(acc[:, :, :], xs[:, :, 0:16], xs[:, :, 16:32], ALU.add))
                    for i in range(2, 16):
                        link(v.tensor_tensor(acc[:, :, :], acc[:, :, :], xs[:, :, 16 * i:16 * i + 16], ALU.add))
                    a4 = acc[:, :, :].rearrange("p t (b c) -> p t b c", b=4)
                    link(v.tensor_tensor(a4[:, :, 0, :], a4[:, :, 0, :], a4[:, :, 1, :], ALU.add))
                    link(v.tensor_tensor(a4[:, :, 2, :], a4[:, :, 2, :], a4[:, :, 3, :], ALU.add))
                    link(v.tensor_tensor(a4[:, :, 0, :], a4[:, :, 0, :], a4[:, :, 2, :], ALU.add))
                    link(v.tensor_tensor(acc[:, :, 0], acc[:, :, 0], acc[:, :, 1], ALU.add))
                    link(v.tensor_tensor(acc[:, :, 2], acc[:, :, 2], acc[:, :, 3], ALU.add))
                    link(v.tensor_tensor(acc[:, :, 0], acc[:, :, 0], acc[:, :, 2], ALU.add))
                    link(v.tensor_scalar(ms, acc[:, :, 0], 1.0 / D, None, ALU.mult))
                    link(v.tensor_tensor(xs, xs, ms[:, :, None].broadcast_to([P, HT, D]), ALU.subtract))
                    link(v.tensor_tensor(square[:, :, :], xs, xs, ALU.mult))
                    runs = square[:, :, :].rearrange("p t (r c) -> p t r c", c=32)
                    a8 = acc[:, :, 0:8]
                    link(v.tensor_tensor(a8, runs[:, :, :, 0], runs[:, :, :, 1], ALU.add))
                    for i in range(2, 32):
                        link(v.tensor_tensor(a8, a8, runs[:, :, :, i], ALU.add))
                    link(v.tensor_tensor(acc[:, :, 0:4], acc[:, :, 0:4], acc[:, :, 4:8], ALU.add))
                    link(v.tensor_tensor(acc[:, :, 0], acc[:, :, 0], acc[:, :, 1], ALU.add))
                    link(v.tensor_tensor(acc[:, :, 2], acc[:, :, 2], acc[:, :, 3], ALU.add))
                    link(v.tensor_tensor(acc[:, :, 0], acc[:, :, 0], acc[:, :, 2], ALU.add))
                    last = v.tensor_scalar(vs, acc[:, :, 0], 1.0 / D, EPS, ALU.mult, ALU.add)
                    link(last)
                v.memset(s1[:, :], 0.0).then_inc(stats_done, 1)
                dve.wait_ge(root_first, 1)
                dve.wait_ge(stats_done, 1)
                def halves(hi, lo, a, t):
                    link(v.scalar_tensor_tensor(out=t, in0=a, scalar=SPLIT, in1=a, op0=ALU.mult, op1=ALU.subtract))
                    link(v.scalar_tensor_tensor(out=hi, in0=a, scalar=SPLIT, in1=t, op0=ALU.mult, op1=ALU.subtract))
                    link(v.tensor_tensor(lo, a, hi, ALU.subtract))
                halves(root_hi[:, :], root_lo[:, :], root[:, :], s0[:, :])
                link(v.reciprocal(inv_root[:, :], root[:, :]))
                link(v.tensor_tensor(s0[:, :], root_hi[:, :], root_hi[:, :], ALU.mult))
                link(v.tensor_tensor(s1[:, :], var[:, :], s0[:, :], ALU.subtract))
                link(v.scalar_tensor_tensor(out=s0[:, :], in0=root_hi[:, :], scalar=-2.0, in1=root_lo[:, :], op0=ALU.mult, op1=ALU.mult))
                link(v.tensor_tensor(s1[:, :], s1[:, :], s0[:, :], ALU.add))
                link(v.tensor_tensor(s0[:, :], root_lo[:, :], root_lo[:, :], ALU.mult))
                link(v.tensor_tensor(s1[:, :], s1[:, :], s0[:, :], ALU.subtract))
                link(v.scalar_tensor_tensor(out=s1[:, :], in0=s1[:, :], scalar=0.5, in1=inv_root[:, :], op0=ALU.mult, op1=ALU.mult))
                link(v.tensor_tensor(root[:, :], root[:, :], s1[:, :], ALU.add))
                link(v.tensor_scalar(cums[:, :, 10], root[:, :], 1.0, None, ALU.add))
                link(v.tensor_copy(cums[:, :, 11], mean[:, :]))
                link(v.reciprocal(inv_root[:, :], root[:, :]))
                halves(root_hi[:, :], root_lo[:, :], root[:, :], s0[:, :])
                link(v.tensor_scalar(root_hi[:, :], root_hi[:, :], -1.0, None, ALU.mult))
                link(v.tensor_scalar(root_lo[:, :], root_lo[:, :], -1.0, None, ALU.mult))

        with ExitStack() as c2:
            q, t, qh, ql = (c2.enter_context(nc.sbuf_tensor("norm_" + n, [P, TPB, D], F32)) for n in ("q", "t", "qh", "ql"))
            tile_s = c2.enter_context(nc.sbuf_tensor("norm_tile_s", [P, 3, TPB], F32))
            step = c2.enter_context(nc.semaphore("norm_step"))
            c2.callback(clear_semaphores, nc, [step])
            block = c2.enter_context(nc.Block())

            @block.vector
            def _(dve):
                v = nc.vector
                STEPS = 9
                with dve.Fori(0, B) as b:
                    link = Chain(dve, step, dve.snap(b * STEPS), STEPS)
                    at = bass.ds(b * TPB, TPB)
                    xs = x[:, at, :]
                    v.tensor_copy(tile_s[:, 0, :], inv_root[:, at])
                    v.tensor_copy(tile_s[:, 1, :], root_hi[:, at])
                    link(v.tensor_copy(tile_s[:, 2, :], root_lo[:, at]))

                    def tiles(fn):
                        for i in range(TPB):
                            ins = fn(i)
                        return ins
                    link(tiles(lambda i: v.tensor_scalar(q[:, i, :], x[:, b * TPB + i, :], tile_s[:, 0, i:i + 1], None, ALU.mult)))
                    qf, tf, hf, lf = (a[:, :, :].rearrange("p t d -> p (t d)") for a in (q, t, qh, ql))
                    link(v.tensor_scalar(hf.bitcast(I32), qf.bitcast(I32), -4096, None, ALU.bitwise_and))
                    link(v.tensor_tensor(lf, qf, hf, ALU.subtract))
                    for n, (a, r) in enumerate(((qh, 1), (qh, 2), (ql, 1), (ql, 2))):
                        def one(i):
                            return v.scalar_tensor_tensor(out=t[:, i, :], in0=a[:, i, :], scalar=tile_s[:, r, i:i + 1],
                                                          in1=x[:, b * TPB + i, :] if n == 0 else t[:, i, :],
                                                          op0=ALU.mult, op1=ALU.add)
                        link(tiles(one))
                    link(tiles(lambda i: v.scalar_tensor_tensor(out=x[:, b * TPB + i, :], in0=t[:, i, :], scalar=tile_s[:, 0, i:i + 1],
                                                                in1=q[:, i, :], op0=ALU.mult, op1=ALU.add)))
                    link.close()


def decay_sums(nc, x, ident, small, dram, cums):
    KB = 32
    NKB = D // KB
    with ExitStack() as ctx:
        def sb(name, shape, dt=F32):
            return ctx.enter_context(nc.sbuf_tensor("norm_" + name, shape, dt))

        acc = [sb(f"chain{h}", [P, NT, 4]) for h in range(H0)]
        with ExitStack() as c1:
            def sc(name, shape):
                return c1.enter_context(nc.sbuf_tensor("norm_" + name, shape, F32))

            semaphores = []

            def sem(name):
                s = c1.enter_context(nc.semaphore("norm_" + name))
                semaphores.append(s)
                return s
            w = [sc(f"w{h}", [P, D]) for h in range(H0)]
            w_hi = [sc(f"w_hi{h}", [P, D]) for h in range(H0)]
            w_lo = [sc(f"w_lo{h}", [P, D]) for h in range(H0)]
            wt = sc("wt", [P, D])
            xh, xl, xt = (sc(n, [P, NT, KB]) for n in ("xh", "xl", "xt"))
            ph = [sc(f"ph{h}", [P, NT, KB]) for h in range(H0)]
            pl = [sc(f"pl{h}", [P, NT, KB]) for h in range(H0)]
            tmp = [[sc(f"tmp{h}_{i}", [P, NT, 4]) for i in range(4)] for h in range(H0)]
            w_loaded, setup, products, chain0, chain1, made1 = (sem(n) for n in ("w_loaded", "wsetup", "products", "chain0", "chain1", "made1"))
            c1.callback(clear_semaphores, nc, semaphores)
            block = c1.enter_context(nc.Block())
            PER = (KB // 4) * 8

            @block.sync
            def _(sp):
                for h in range(H0):
                    sp.dma_start(w[h][:, :], dram["w_alpha_rows"][h:h + 1, :].broadcast_to([P, D])).then_inc(w_loaded, 16)

            def chain(v, link, h):
                s, bb, t, e = (a[:, :, :] for a in tmp[h])
                a = acc[h][:, :, :]
                for k in range(KB // 4):
                    p_hi, p_lo = (u[h][:, :, 4 * k:4 * k + 4] for u in (ph, pl))
                    link(v.tensor_tensor(s, a, p_hi, ALU.add))
                    link(v.tensor_tensor(bb, s, a, ALU.subtract))
                    link(v.tensor_tensor(t, s, bb, ALU.subtract))
                    link(v.tensor_tensor(t, a, t, ALU.subtract))
                    link(v.tensor_tensor(e, p_hi, bb, ALU.subtract))
                    link(v.tensor_tensor(e, t, e, ALU.add))
                    link(v.tensor_tensor(e, e, p_lo, ALU.add))
                    link(v.tensor_tensor(a, s, e, ALU.add))

            @block.gpsimd
            def _(pool):
                pool.memset(acc[1][:, :, :], 0.0).then_inc(chain1, 1)
                pool.wait_ge(chain1, 1)
                with pool.Fori(0, NKB) as kb:
                    pool.wait_ge(made1, kb + 1)
                    link = Chain(pool, chain1, pool.snap(kb * PER + 1), PER)
                    chain(nc.gpsimd, link, 1)
                    link.close()

            @block.vector
            def _(dve):
                v = nc.vector
                link = Chain(dve, setup)
                link(v.memset(acc[0][:, :, :], 0.0))
                dve.wait_ge(w_loaded, 16 * H0)
                for h in range(H0):
                    link(v.scalar_tensor_tensor(out=wt[:, :], in0=w[h][:, :], scalar=SPLIT, in1=w[h][:, :], op0=ALU.mult, op1=ALU.subtract))
                    link(v.scalar_tensor_tensor(out=w_hi[h][:, :], in0=w[h][:, :], scalar=SPLIT, in1=wt[:, :], op0=ALU.mult, op1=ALU.subtract))
                    link(v.tensor_tensor(w_lo[h][:, :], w[h][:, :], w_hi[h][:, :], ALU.subtract))
                STEPS = 2 + 9 * H0
                with dve.Fori(0, NKB) as kb:
                    link = Chain(dve, products, dve.snap(kb * STEPS), STEPS)
                    at = bass.ds(kb * KB, KB)
                    xs = x[:, 0:NT, at]
                    a3, h3, l3 = xt[:, :, :], xh[:, :, :], xl[:, :, :]
                    link(v.tensor_scalar(h3.bitcast(I32), xs.bitcast(I32), -4096, None, ALU.bitwise_and))
                    link(v.tensor_tensor(l3, xs, h3, ALU.subtract))
                    for h in (1, 0):
                        def row(a):
                            return a[:, None, at].broadcast_to([P, NT, KB])
                        p3, e3 = ph[h][:, :, :], pl[h][:, :, :]
                        if h == 1:
                            dve.wait_ge(chain1, kb * PER + 1)
                        link(v.tensor_tensor(p3, xs, row(w[h]), ALU.mult))
                        link(v.tensor_tensor(e3, h3, row(w_hi[h]), ALU.mult))
                        link(v.tensor_tensor(e3, e3, p3, ALU.subtract))
                        for a, b in ((h3, w_lo[h]), (l3, w_hi[h]), (l3, w_lo[h])):
                            link(v.tensor_tensor(a3, a, row(b), ALU.mult))
                            link(v.tensor_tensor(e3, e3, a3, ALU.add))
                        if h == 1:
                            dve.sem_inc(made1, 1)
                    link.close()
                    link = Chain(dve, chain0, dve.snap(kb * PER), PER)
                    chain(nc.vector, link, 0)
                    link.close()

        with ExitStack() as c1:
            def sc(name, shape, dt=F32):
                return c1.enter_context(nc.sbuf_tensor("norm_" + name, shape, dt))

            semaphores = []

            def sem(name):
                s = c1.enter_context(nc.semaphore("norm_" + name))
                semaphores.append(s)
                return s
            z = sc("z", [P, H0, NT])
            bias = sc("bias", [P, H0])
            gain = sc("gain", [P, H0])
            gtmp = [sc(f"gtmp{i}", [P, H0]) for i in range(4)]
            gbits = sc("gbits", [P, H0], I32)
            n, t, zz, y, ex, big, wv, q, ll = (sc(f"sp{i}", [P, H0 * NT]) for i in range(9))
            bits = sc("bits", [P, H0 * NT], I32)
            log_decay = sc("log_decay", [P, NT, H0])
            rows = sc("rows", [P, 8, 16])
            to_end = sc("to_end", [P, 2, CH])
            off = sc("off", [P, 2, 4])
            last_row = [sc(f"last_row{c}", [P, P]) for c in range(2)]
            tok = sc("tok", [P, NT, H0])
            ps = [c1.enter_context(nc.psum_tensor(f"norm_ps{i}", [P, 512], F32)) for i in range(6)]
            loaded, s, turned, turned_back, ends, exps, cum_tok = (sem(i) for i in ("g_loaded", "g_steps", "turned", "turned_back", "ends", "exps", "cum_tok"))
            c1.callback(clear_semaphores, nc, semaphores)
            block = c1.enter_context(nc.Block())
            done = {}

            @block.sync
            def _(sp):
                sp.dma_start(gain[:, :], dram["a_log"].rearrange("(a h) -> a h", a=1).broadcast_to([P, H0])).then_inc(loaded, 16)
                sp.dma_start(bias[:, :], dram["dt_bias"].rearrange("(a h) -> a h", a=1).broadcast_to([P, H0])).then_inc(loaded, 16)
                for c in range(2):
                    sp.dma_start(last_row[c][:, :], dram["last_row"][c]).then_inc(loaded, 16)

            @block.vector
            def _(dve):
                v = nc.vector
                link = Chain(dve, s)
                dve.wait_ge(loaded, 64)
                for h in range(H0):
                    a = acc[h][:, :, :]
                    link(v.tensor_tensor(a[:, :, 0], a[:, :, 0], a[:, :, 1], ALU.add))
                    link(v.tensor_tensor(a[:, :, 2], a[:, :, 2], a[:, :, 3], ALU.add))
                    link(v.tensor_tensor(z[:, h, :], a[:, :, 0], a[:, :, 2], ALU.add))
                    link(v.tensor_scalar(z[:, h, :], z[:, h, :], bias[:, h:h + 1], None, ALU.add))
                zf = z[:, :, :].rearrange("p h t -> p (h t)")
                link(v.scalar_tensor_tensor(out=y[:, :], in0=zf, scalar=-1.0, in1=zf, op0=ALU.mult, op1=ALU.min))
                link(v.tensor_scalar(wv[:, :], y[:, :], -87.3, None, ALU.max))
                exp_f32(nc, link, ex[:, :], wv[:, :], n[:, :], t[:, :], zz[:, :], y[:, :], bits[:, :])
                link(v.tensor_scalar(big[:, :], ex[:, :], 0.41421356, None, ALU.is_ge))
                link(v.tensor_scalar(wv[:, :], ex[:, :], 1.0, -2.0, ALU.add, ALU.add))
                link(v.scalar_tensor_tensor(out=wv[:, :], in0=wv[:, :], scalar=0.5, in1=big[:, :], op0=ALU.mult, op1=ALU.mult))
                link(v.tensor_scalar(n[:, :], big[:, :], -1.0, 1.0, ALU.mult, ALU.add))
                link(v.tensor_tensor(t[:, :], ex[:, :], n[:, :], ALU.mult))
                link(v.tensor_tensor(wv[:, :], wv[:, :], t[:, :], ALU.add))
                horner(nc, link, y[:, :], wv[:, :], LOG_Q)
                link(v.reciprocal(y[:, :], y[:, :]))
                horner(nc, link, q[:, :], wv[:, :], LOG_P)
                link(v.tensor_tensor(q[:, :], q[:, :], y[:, :], ALU.mult))
                link(v.tensor_tensor(zz[:, :], wv[:, :], wv[:, :], ALU.mult))
                link(v.tensor_tensor(t[:, :], wv[:, :], zz[:, :], ALU.mult))
                link(v.tensor_tensor(t[:, :], t[:, :], q[:, :], ALU.mult))
                link(v.scalar_tensor_tensor(out=t[:, :], in0=zz[:, :], scalar=-0.5, in1=t[:, :], op0=ALU.mult, op1=ALU.add))
                link(v.tensor_tensor(ll[:, :], wv[:, :], t[:, :], ALU.add))
                LN2_HI = 0.693147182464599609375
                link(v.scalar_tensor_tensor(out=ll[:, :], in0=big[:, :], scalar=math.log(2) - LN2_HI, in1=ll[:, :], op0=ALU.mult, op1=ALU.add))
                link(v.scalar_tensor_tensor(out=ll[:, :], in0=big[:, :], scalar=LN2_HI, in1=ll[:, :], op0=ALU.mult, op1=ALU.add))
                link(v.scalar_tensor_tensor(out=ll[:, :], in0=zf, scalar=0.0, in1=ll[:, :], op0=ALU.max, op1=ALU.add))
                exp_f32(nc, link, gain[:, :], gain[:, :], *(g[:, :] for g in gtmp), gbits[:, :])
                link(v.tensor_scalar(gain[:, :], gain[:, :], -1.0, None, ALU.mult))
                for h in range(H0):
                    link(v.tensor_scalar(log_decay[:, :, h], ll[:, h * NT:(h + 1) * NT], gain[:, h:h + 1], None, ALU.mult))
                done["log_decay"] = link.n
                dve.wait_ge(turned, 1)
                link(v.tensor_copy(rows[:, :, :], ps[0][:, 0:P].rearrange("p (r i) -> p r i", i=16)))
                for i in range(1, 16):
                    link(v.tensor_tensor(rows[:, :, i], rows[:, :, i - 1], rows[:, :, i], ALU.add))
                runs = rows[:, :, :].rearrange("p (c r) i -> p c r i", c=2)
                link(v.memset(off[:, :, 0:1], 0.0))
                link(v.tensor_copy(off[:, :, 1], runs[:, :, 0, 15]))
                link(v.tensor_tensor(off[:, :, 2], off[:, :, 1], runs[:, :, 1, 15], ALU.add))
                link(v.tensor_tensor(off[:, :, 3], off[:, :, 2], runs[:, :, 2, 15], ALU.add))
                link(v.tensor_tensor(rows[:, :, :], rows[:, :, :],
                                     off[:, :, :].rearrange("p c r -> p (c r)")[:, :, None].broadcast_to([P, 8, 16]), ALU.add))
                flat = rows[:, :, :].rearrange("p (c r) i -> p c (r i)", c=2)
                link(v.tensor_tensor(to_end[:, :, :], flat[:, :, CH - 1:CH].broadcast_to([P, 2, CH]), flat, ALU.subtract))
                done["rows"] = link.n
                dve.wait_ge(turned_back, 2)
                link(v.tensor_copy(cums[:, :, 0:2], ps[1][:, 0:P].rearrange("p (t h) -> p t h", h=H0)))
                v.tensor_copy(tok[:, :, :], ps[1][:, 0:P].rearrange("p (t h) -> p t h", h=H0)).then_inc(cum_tok, 1)

            @block.tensor
            def _(pe):
                pe.wait_ge(s, done["log_decay"])
                pe.transpose(ps[0][:, 0:P], log_decay[:, :, :].rearrange("p t h -> p (t h)"), ident).then_inc(turned, 1)
                pe.wait_ge(s, done["rows"])
                pe.transpose(ps[1][:, 0:P], rows[:, :, :].rearrange("p r i -> p (r i)"), ident).then_inc(turned_back, 1)
                pe.transpose(ps[2][:, 0:P], to_end[:, :, :].rearrange("p c i -> p (c i)"), ident).then_inc(turned_back, 1)
                pe.wait_ge(loaded, 64)
                pe.wait_ge(cum_tok, 1)
                for c in range(2):
                    pe.matmul(ps[3 + c][:, 0:P], last_row[c][:, :], tok[:, :, :].rearrange("p t h -> p (t h)"),
                              start=True, stop=True).then_inc(ends, 1)

            @block.scalar
            def _(act):
                act.wait_ge(cum_tok, 1)
                act.activation(cums[:, :, 2:4], tok[:, :, :], ACT.Exp).then_inc(exps, 1)
                act.wait_ge(turned_back, 2)
                act.activation(cums[:, :, 4:6], ps[2][:, 0:P].rearrange("p (t h) -> p t h", h=H0), ACT.Exp).then_inc(exps, 1)
                act.wait_ge(ends, 2)
                for c in range(2):
                    act.activation(cums[:, :, 6 + 2 * c:8 + 2 * c], ps[3 + c][:, 0:P].rearrange("p (t h) -> p t h", h=H0), ACT.Exp)\
                        .then_inc(exps, 1)


def delta_attention(nc, x, ident, masks, small, dram, cums):
    semaphores = []
    with ExitStack() as ctx:
        def sb(name, shape, dt=F32):
            return ctx.enter_context(nc.sbuf_tensor("delta_" + name, shape, dt))

        def sem(name):
            s = ctx.enter_context(nc.semaphore("delta_" + name))
            semaphores.append(s)
            return s

        w_in = sb("w_in", [P, KD, D + H0])
        w_out = sb("w_out", [P, H0, D])
        minus_half = small[:, 0:2]
        cap = sb("cap", [P, P])

        h_tok = [sb(f"h_tok{b}", [P, D]) for b in range(BL)]
        square = [sb(f"square{b}", [P, D]) for b in range(BL)]
        ssq = [sb(f"ssq{b}", [P, H0]) for b in range(BL)]
        ssq_min = [sb(f"ssq_min{b}", [P, H0]) for b in range(BL)]
        rnorm = [sb(f"rnorm{b}", [P, H0]) for b in range(BL)]
        rk = [sb(f"rk{b}", [P, H0, HD0]) for b in range(BL)]
        h_T = [sb(f"h_T{b}", [P, KD, P]) for b in range(BL)]
        rk_T = [sb(f"rk_T{b}", [P, H0, P + 1]) for b in range(BL)]
        v_tok = [sb(f"v_tok{b}", [P, D]) for b in range(BL)]
        gate_nz = [sb(f"gate_nz{b}", [P, H0]) for b in range(BL)]
        gate_e = [sb(f"gate_e{b}", [P, H0]) for b in range(BL)]
        gate_d = [sb(f"gate_d{b}", [P, H0]) for b in range(BL)]
        nbeta = [sb(f"nbeta{b}", [P, H0]) for b in range(BL)]
        cum_rows = [sb(f"cum_rows{b}", [P, H0, P]) for b in range(BL)]
        scal = [sb(f"scal{b}", [P, NCUM]) for b in range(BL)]
        low_arg = [sb(f"low_arg{b}", [P, H0, P]) for b in range(BL)]
        decay_low = [sb(f"decay_low{b}", [P, H0, P]) for b in range(BL)]
        decay_row = [sb(f"decay_row{b}", [P, H0, P]) for b in range(BL)]
        lanes = range(LN0)
        rk_decay_T = [sb(f"rk_decay_T{l}", [P, P]) for l in lanes]
        wk_tail = [sb(f"wk_tail{l}", [P, HD0]) for l in lanes]
        gram = [sb(f"gram{l}", [P, P]) for l in lanes]
        intra = [sb(f"intra{l}", [P, P]) for l in lanes]
        gram0 = [sb(f"gram0{l}", [P, P]) for l in lanes]
        inv = [sb(f"inv{l}", [P, 2 * P]) for l in lanes]
        prod = [sb(f"prod{l}", [P, P]) for l in lanes]
        neg_r = [sb(f"neg_r{l}", [P, HD0]) for l in lanes]
        v_new = [sb(f"v_new{l}", [P, HD0]) for l in lanes]
        state = [sb(f"state{l}", [P, HD0]) for l in lanes]
        o_T = [sb(f"o_T{l}", [P, P]) for l in lanes]

        pa = [ctx.enter_context(nc.psum_tensor(f"delta_pa{l}", [P, 512], F32)) for l in lanes]
        pb = [ctx.enter_context(nc.psum_tensor(f"delta_pb{l}", [P, 512], F32)) for l in lanes]

        names_dve = ["h_s", "ssm_s", "rk_s", "scal_s", "carry_s", "rkT_s", "z_s", "den_s", "rows_s", "arg_s",
                     "nbeta_s", "xh_s", "x_s", "gram_s", "intra_s", "g0d_s", "inv0_s"]
        names_act = ["ssq_s", "hT_s", "v_s", "ge_s", "low_s", "row_s", "tail_s", "inv1_s", "oTe_s"]
        names_pe = ["hTp_s", "rkTp_s", "proj_s", "rowp_s", "gramp_s", "wkp_s", "inv1p_s", "outp_s"]
        names_pool = ["rnorm_s", "rkd_s", "g0_s"]
        S = {}
        for group in (names_dve, names_act, names_pe, names_pool):
            for n in group:
                S[n] = sem(n)
        prodp_s = [sem(f"prodp{k}_s") for k in range(LEVELS)]
        prod_s = [sem(f"prod{k}_s") for k in range(LEVELS)]
        invp_s = [sem(f"grownp{k}_s") for k in range(LEVELS)]
        inv_s = [sem(f"grown{k}_s") for k in range(LEVELS)]
        wS_s = [sem(f"wS{c}_s") for c in range(2)]
        negr_s = [sem(f"negr{c}_s") for c in range(2)]
        br_s = [sem(f"br{c}_s") for c in range(2)]
        vnew_s = [sem(f"vnew{c}_s") for c in range(2)]
        oTp_s = [sem(f"oTp{c}_s") for c in range(2)]
        upd_s = [sem(f"upd{c}_s") for c in range(2)]
        state_s = [sem(f"state{c}_s") for c in range(2)]
        loaded = sem("loaded")
        pad_done = sem("pad_done")
        copy_fence = sem("copy_fence")
        reset = sem("reset")
        NLOAD = 4

        m = {n: masks[:, i, :] for i, n in enumerate(MASKS)}
        ctx.callback(clear_semaphores, nc, semaphores)
        block = ctx.enter_context(nc.Block())

        def counts(eng, bp, j):
            it = bp * TPB + j
            return [eng.snap(it * BL + k + 1) for k in range(BL + 1)], [eng.snap(it * LN0 + k + 1) for k in range(LN0 + 1)]

        def front_counts(eng, bp, j):
            return [eng.snap((bp * (TPB + 1) + j) * BL + k + 1) for k in range(BL + 1)]

        @block.sync
        def _(sp):
            sp.dma_start(w_in[:, :, 0:D], dram["w_write"].rearrange("(k p) e -> p k e", p=P)).then_inc(loaded, 16)
            sp.dma_start(w_in[:, :, D:], dram["w_beta"].rearrange("(k p) e -> p k e", p=P)).then_inc(loaded, 16)
            sp.dma_start(w_out[:, :, :], dram["w_read"].rearrange("(k p) e -> p k e", p=P)).then_inc(loaded, 16)
            sp.dma_start(cap[:, :], dram["cap"]).then_inc(loaded, 16)

        @block.gpsimd
        def _(pool):
            for n in names_pool:
                pool.sem_inc(S[n], 1)
            pool.wait_ge(loaded, 16 * NLOAD)

            def front(bp, j):
                nf = front_counts(pool, bp, j)
                for b in range(BL):
                    pool.wait_ge(S["ssm_s"], nf[b + 1])
                    pool.tensor_tensor(rnorm[b][:, :], ssq_min[b][:, :], minus_half, ALU.pow).then_inc(S["rnorm_s"], 1)

            with pool.Fori(0, B // BL) as bp:
                front(bp, 0)
                with pool.Fori(0, TPB) as j:
                    n2, n4 = counts(pool, bp, j)
                    for l in lanes:
                        b, h = divmod(l, H0)
                        pool.wait_ge(S["row_s"], n2[b + 1])
                        pool.wait_ge(S["rkT_s"], n2[b + 1])
                        pool.tensor_tensor(rk_decay_T[l][:, :], rk_T[b][:, h, 1:P + 1], decay_row[b][:, h, :], ALU.mult)\
                            .then_inc(S["rkd_s"], 1)
                    for l in lanes[:LN0 - 1]:
                        pool.wait_ge(S["gram_s"], n4[l + 1])
                        pool.tensor_tensor(gram0[l][:, :], gram[l][:, :], m["level0"], ALU.mult).then_inc(S["g0_s"], 1)
                    front(bp, j + 1)




        @block.scalar
        def _(act):
            for n in names_act:
                act.sem_inc(S[n], 1)
            for s in vnew_s:
                act.sem_inc(s, 1)
            act.wait_ge(loaded, 16 * NLOAD)

            def front(bp, j):
                nf = front_counts(act, bp, j)
                for b in range(BL):
                    act.wait_ge(S["h_s"], nf[b + 1])
                    act.activation(square[b][:, 0:HD0], h_tok[b][:, 0:HD0], ACT.Square, accum_out=ssq[b][:, 0:1])
                    act.activation(square[b][:, HD0:D], h_tok[b][:, HD0:D], ACT.Square, accum_out=ssq[b][:, 1:2])\
                        .then_inc(S["ssq_s"], 1)

            with act.Fori(0, B // BL) as bp:
                front(bp, 0)
                with act.Fori(0, TPB) as j:
                    n2, n4 = counts(act, bp, j)
                    for b in range(BL):
                        act.wait_ge(S["hTp_s"], n2[b + 1])
                        act.activation(h_T[b][:, :, :], pa[2 * b][:, 0:D], ACT.Copy).then_inc(S["hT_s"], 1)
                    for b in range(BL):
                        act.wait_ge(S["proj_s"], n2[b + 1])
                        act.activation(v_tok[b][:, :], pa[2 * b + 1][:, 0:D], ACT.Copy).then_inc(S["v_s"], 1)
                    for b in range(BL):
                        act.wait_ge(S["z_s"], n2[b + 1])
                        act.activation(gate_e[b][:, :], gate_nz[b][:, :], ACT.Exp).then_inc(S["ge_s"], 1)
                    for b in range(BL):
                        act.wait_ge(S["arg_s"], n2[b + 1])
                        act.activation(decay_low[b][:, :, :], low_arg[b][:, :, :], ACT.Exp).then_inc(S["low_s"], 1)
                        act.activation(decay_row[b][:, :, :], pb[2 * b][:, 0:H0 * P], ACT.Exp).then_inc(S["row_s"], 1)
                    for l in lanes:
                        b, h = divmod(l, H0)
                        act.wait_ge(S["scal_s"], n2[b + 1])
                        act.wait_ge(S["wkp_s"], n4[l + 1])
                        act.activation(wk_tail[l][:, :], pa[l][:, 0:HD0], ACT.Copy, scale=scal[b][:, 4 + h:5 + h])\
                            .then_inc(S["tail_s"], 1)
                    for l in lanes:
                        act.wait_ge(S["inv1p_s"], n4[l + 1])
                        act.activation(inv[l][:, 0:P], pa[l][:, P:2 * P], ACT.Copy).then_inc(S["inv1_s"], 1)
                    for c in range(2):
                        rows = slice(CH * c, CH * c + CH)
                        for l in lanes:
                            b, h = divmod(l, H0)
                            act.wait_ge(br_s[c], n4[l + 1])
                            act.activation(v_new[l][rows, :], pa[l][rows, P:2 * P], ACT.Copy, scale=nbeta[b][rows, h:h + 1])\
                                .then_inc(vnew_s[c], 1)
                        if c == 0:
                            front(bp, j + 1)
                    for l in lanes:
                        act.wait_ge(oTp_s[1], n4[l + 1])
                        act.activation(o_T[l][:, :], pb[l][:, 2 * P:3 * P], ACT.Copy).then_inc(S["oTe_s"], 1)

        @block.vector
        def _(dve):
            for n in names_dve:
                dve.sem_inc(S[n], 1)
            for group in (prod_s, inv_s, negr_s, state_s):
                for s in group:
                    dve.sem_inc(s, 1)
            dve.wait_ge(loaded, 16 * NLOAD)
            dve.memset(x[:, NT:, :], 0.0).then_inc(pad_done, 1)
            dve.wait_ge(pad_done, 1)

            def tile_ahead(bp, j):
                for b in range(BL):
                    dve.tensor_copy(h_tok[b][:, :], x[:, dve.snap((bp * BL + b) * TPB + j), :]).then_inc(S["h_s"], 1)

            def keys_ahead(bp, j):
                nf = front_counts(dve, bp, j)
                for b in range(BL):
                    dve.wait_ge(S["ssq_s"], nf[b + 1])
                    dve.tensor_scalar(ssq_min[b][:, :], ssq[b][:, :], 1e-24, None, ALU.max).then_inc(S["ssm_s"], 1)
                for b in range(BL):
                    dve.wait_ge(S["rnorm_s"], nf[b + 1])
                    dve.tensor_scalar(rk[b][:, 0, :], h_tok[b][:, 0:HD0], rnorm[b][:, 0:1], None, ALU.mult)
                    dve.tensor_scalar(rk[b][:, 1, :], h_tok[b][:, HD0:D], rnorm[b][:, 1:2], None, ALU.mult)\
                        .then_inc(S["rk_s"], 1)

            with dve.Fori(0, B // BL) as bp:
                for l in lanes:
                    dve.memset(state[l][:, :], 0.0).then_inc(reset, 1)
                for b in range(BL):
                    dve.memset(rk_T[b][:, :, P:P + 1], 0.0).then_inc(reset, 1)
                dve.wait_ge(S["rk_s"], front_counts(dve, bp, 0)[0])
                dve.sem_inc(copy_fence, 1)
                tile_ahead(bp, 0)
                keys_ahead(bp, 0)
                with dve.Fori(0, TPB) as j:
                    n2, n4 = counts(dve, bp, j)
                    tile = [dve.snap((bp * BL + b) * TPB + j) for b in range(BL)]
                    g0 = [dve.snap((bp * TPB + j) * (LN0 - 1) + l + 2) for l in range(LN0 - 1)]
                    g0d = dve.snap(bp * TPB + j + 2)
                    for b in range(BL):
                        dve.tensor_copy(scal[b][:, :], cums[:, tile[b], :]).then_inc(S["scal_s"], 1)
                    for b in range(BL):
                        dve.wait_ge(S["scal_s"], n2[b + 1])
                        for h in range(H0):
                            last = dve.tensor_scalar(cum_rows[b][:, h, :], m["ones"], scal[b][:, h:h + 1], None, ALU.mult)
                        last.then_inc(S["rows_s"], 1)
                    for b in range(BL):
                        dve.wait_ge(reset, bp * 6 + 6)
                        dve.tensor_copy(rk_T[b][:, :, 0:1], rk_T[b][:, :, P:P + 1]).then_inc(S["carry_s"], 1)
                    for b in range(BL):
                        dve.wait_ge(S["rowp_s"], n2[b + 1])
                        for h in range(H0):
                            last = dve.scalar_tensor_tensor(out=low_arg[b][:, h, :], in0=pb[2 * b][:, h * P:(h + 1) * P],
                                                            scalar=scal[b][:, h:h + 1], in1=cap[:, :], op0=ALU.subtract, op1=ALU.min)
                        last.then_inc(S["arg_s"], 1)
                    for b in range(BL):
                        dve.wait_ge(S["v_s"], n2[b + 1])
                        dve.tensor_scalar(gate_nz[b][:, :], pa[2 * b + 1][:, D:D + H0], -80.0, -1.0, ALU.max, ALU.mult)\
                            .then_inc(S["z_s"], 1)
                    for b in range(BL):
                        dve.wait_ge(S["rkTp_s"], n2[b + 1])
                        dve.wait_ge(S["carry_s"], n2[b + 1])
                        dve.tensor_copy(rk_T[b][:, :, 1:P + 1], pa[2 * b][:, D:2 * D].rearrange("p (h t) -> p h t", h=H0))\
                            .then_inc(S["rkT_s"], 1)
                    for b in range(BL):
                        dve.wait_ge(S["ge_s"], n2[b + 1])
                        dve.tensor_scalar(gate_d[b][:, :], gate_e[b][:, :], -1.0, -1.0, ALU.mult, ALU.add).then_inc(S["den_s"], 1)
                        dve.wait_ge(S["den_s"], n2[b + 1])
                        dve.reciprocal(nbeta[b][:, :], gate_d[b][:, :]).then_inc(S["nbeta_s"], 1)
                    for l in lanes:
                        b, h = divmod(l, H0)
                        dve.wait_ge(S["nbeta_s"], n2[b + 1])
                        dve.wait_ge(S["gramp_s"], n4[l + 1])
                        dve.wait_ge(S["low_s"], n2[b + 1])
                        dve.scalar_tensor_tensor(out=gram[l][:, :], in0=pb[l][:, 0:P], scalar=nbeta[b][:, h:h + 1],
                                                 in1=decay_low[b][:, h, :], op0=ALU.mult, op1=ALU.mult).then_inc(S["gram_s"], 1)
                        dve.tensor_tensor(intra[l][:, :], pb[l][:, 1:P + 1], decay_low[b][:, h, :], ALU.mult).then_inc(S["intra_s"], 1)
                    dve.wait_ge(S["gram_s"], n4[LN0])
                    dve.tensor_tensor(gram0[LN0 - 1][:, :], gram[LN0 - 1][:, :], m["level0"], ALU.mult).then_inc(S["g0d_s"], 1)
                    for l in lanes:
                        if l < LN0 - 1:
                            dve.wait_ge(S["g0_s"], g0[l])
                        else:
                            dve.wait_ge(S["g0d_s"], g0d)
                        dve.tensor_tensor(inv[l][:, P:2 * P], gram0[l][:, :], ident, ALU.add).then_inc(S["inv0_s"], 1)
                    for k in range(1, LEVELS):
                        for l in lanes:
                            dve.wait_ge(prodp_s[k], n4[l + 1])
                            dve.tensor_tensor(prod[l][:, :], pa[l][:, 2 * P:3 * P], m[f"level{k}"], ALU.mult).then_inc(prod_s[k], 1)
                        for l in lanes:
                            part = slice(0, 2 * P) if k < LEVELS - 1 else slice(P, 2 * P)
                            dve.wait_ge(invp_s[k], n4[l + 1])
                            dve.tensor_tensor(inv[l][:, part], inv[l][:, part], pa[l][:, part], ALU.add).then_inc(inv_s[k], 1)
                    for c in range(2):
                        rows = slice(CH * c, CH * c + CH)
                        for l in lanes:
                            b, h = divmod(l, H0)
                            dve.wait_ge(wS_s[c], n4[l + 1])
                            dve.scalar_tensor_tensor(out=neg_r[l][rows, :], in0=pa[l][rows, 0:HD0], scalar=scal[b][rows, 2 + h:3 + h],
                                                     in1=v_tok[b][rows, h * HD0:(h + 1) * HD0], op0=ALU.mult, op1=ALU.subtract)\
                                .then_inc(negr_s[c], 1)
                        if c == 0:
                            for b in range(BL):
                                dve.tensor_scalar(x[:, tile[b], :], h_tok[b][:, :], scal[b][:, 10:11], scal[b][:, 11:12],
                                                  ALU.mult, ALU.add).then_inc(S["xh_s"], 1)
                            dve.wait_ge(S["xh_s"], n2[BL])
                            dve.sem_inc(copy_fence, 1)
                            tile_ahead(bp, j + 1)
                        for l in lanes:
                            b, h = divmod(l, H0)
                            at = 6 + 2 * c + h
                            dve.wait_ge(upd_s[c], n4[l + 1])
                            dve.scalar_tensor_tensor(out=state[l][:, :], in0=state[l][:, :], scalar=scal[b][:, at:at + 1],
                                                     in1=pa[l][:, 2 * P:3 * P], op0=ALU.mult, op1=ALU.add).then_inc(state_s[c], 1)
                    keys_ahead(bp, j + 1)
                    for b in range(BL):
                        dve.wait_ge(S["outp_s"], n2[b + 1])
                        dve.wait_ge(S["xh_s"], n2[b + 1])
                        dve.tensor_tensor(x[:, tile[b], :], x[:, tile[b], :], pa[2 * b][:, 0:D], ALU.add).then_inc(S["x_s"], 1)

        @block.tensor
        def _(pe):
            for n in names_pe:
                pe.sem_inc(S[n], 1)
            for group in (prodp_s, invp_s, wS_s, br_s, oTp_s, upd_s):
                for s in group:
                    pe.sem_inc(s, 1)
            pe.wait_ge(loaded, 16 * NLOAD)
            with pe.Fori(0, B // BL) as bp:
                with pe.Fori(0, TPB) as j:
                    n2, n4 = counts(pe, bp, j)
                    nf = front_counts(pe, bp, j)
                    for b in range(BL):
                        pe.wait_ge(S["h_s"], nf[b + 1])
                        pe.wait_ge(S["x_s"], n2[0])
                        for k in range(KD):
                            last = pe.transpose(pa[2 * b][:, k * P:(k + 1) * P], h_tok[b][:, k * P:(k + 1) * P], ident)
                        last.then_inc(S["hTp_s"], 1)
                    for b in range(BL):
                        pe.wait_ge(S["rows_s"], n2[b + 1])
                        pe.wait_ge(S["oTe_s"], n4[0])
                        for h in range(H0):
                            last = pe.transpose(pb[2 * b][:, h * P:(h + 1) * P], cum_rows[b][:, h, :], ident)
                        last.then_inc(S["rowp_s"], 1)
                    for b in range(BL):
                        pe.wait_ge(S["hT_s"], n2[b + 1])
                        pe.wait_ge(state_s[1], n4[0])
                        for k in range(KD):
                            last = pe.matmul(pa[2 * b + 1][:, 0:D + H0], h_T[b][:, k, :], w_in[:, k, :],
                                             start=(k == 0), stop=(k == KD - 1))
                        last.then_inc(S["proj_s"], 1)
                    for b in range(BL):
                        pe.wait_ge(S["rk_s"], nf[b + 1])
                        pe.wait_ge(S["hT_s"], n2[b + 1])
                        for h in range(H0):
                            last = pe.transpose(pa[2 * b][:, D + h * P:D + (h + 1) * P], rk[b][:, h, :], ident)
                        last.then_inc(S["rkTp_s"], 1)
                    for l in lanes:
                        b, h = divmod(l, H0)
                        pe.wait_ge(S["rkT_s"], n2[b + 1])
                        pe.wait_ge(S["z_s"], n2[b + 1])
                        pe.transpose(pa[l][:, 0:HD0], rk_T[b][:, h, 0:P], ident).then_inc(S["wkp_s"], 1)
                    for l in lanes:
                        b, h = divmod(l, H0)
                        pe.wait_ge(S["row_s"], n2[b + 1])
                        pe.matmul(pb[l][:, 0:P + 1], rk_T[b][:, h, 0:P], rk_T[b][:, h, 0:P + 1], start=True, stop=True)\
                            .then_inc(S["gramp_s"], 1)
                    for l in lanes:
                        pe.wait_ge(S["tail_s"], n4[l + 1])
                        pe.wait_ge(S["inv0_s"], n4[l + 1])
                        pe.transpose(pa[l][:, P:2 * P], inv[l][:, P:2 * P], ident).then_inc(S["inv1p_s"], 1)
                    for k in range(1, LEVELS):
                        for l in lanes:
                            if k == 1:
                                pe.wait_ge(S["inv1_s"], n4[l + 1])
                            else:
                                pe.wait_ge(inv_s[k - 1], n4[l + 1])
                            pe.matmul(pa[l][:, 2 * P:3 * P], gram[l][:, :], inv[l][:, 0:P], start=True, stop=True).then_inc(prodp_s[k], 1)
                        for l in lanes:
                            pe.wait_ge(prod_s[k], n4[l + 1])
                            if k < LEVELS - 1:
                                pe.matmul(pa[l][:, 0:P], inv[l][:, P:2 * P], prod[l][:, :], start=True, stop=True)
                            pe.matmul(pa[l][:, P:2 * P], prod[l][:, :], inv[l][:, P:2 * P], start=True, stop=True).then_inc(invp_s[k], 1)
                    for c in range(2):
                        rows = slice(CH * c, CH * c + CH)
                        for l in lanes:
                            b, h = divmod(l, H0)
                            if c == 0:
                                pe.wait_ge(inv_s[LEVELS - 1], n4[l + 1])
                            else:
                                pe.wait_ge(state_s[0], n4[l + 1])
                            pe.matmul(pa[l][rows, 0:HD0], rk_T[b][:, h, rows], state[l][:, :], start=True, stop=True).then_inc(wS_s[c], 1)
                        for l in lanes:
                            pe.wait_ge(negr_s[c], n4[l + 1])
                            pe.matmul(pa[l][:, P:2 * P], inv[l][rows, P:2 * P], neg_r[l][rows, :],
                                      start=True, stop=True).then_inc(br_s[c], 1)
                        for l in lanes:
                            b, h = divmod(l, H0)
                            if c == 0:
                                pe.wait_ge(S["rkd_s"], n4[l + 1])
                                pe.wait_ge(S["intra_s"], n4[l + 1])
                            pe.matmul(pb[l][:, 2 * P + CH * c:2 * P + CH * c + CH], state[l][:, :], rk_decay_T[l][:, rows],
                                      start=True, stop=False)
                            pe.wait_ge(vnew_s[c], n4[l + 1])
                            pe.matmul(pb[l][:, 2 * P + CH * c:2 * P + CH * c + CH], v_new[l][rows, :], intra[l][rows, rows],
                                      start=False, stop=True).then_inc(oTp_s[c], 1)
                            pe.matmul(pa[l][:, 2 * P:3 * P], wk_tail[l][rows, :], v_new[l][rows, :], start=True, stop=True)\
                                .then_inc(upd_s[c], 1)
                    for b in range(BL):
                        pe.wait_ge(state_s[1], n4[2 * b + 2])
                        for h in range(H0):
                            pe.wait_ge(S["oTe_s"], n4[2 * b + h + 1])
                            last = pe.matmul(pa[2 * b][:, 0:D], o_T[2 * b + h][:, :], w_out[:, h, :], start=(h == 0), stop=(h == H0 - 1))
                        last.then_inc(S["outp_s"], 1)


def quantised_ffn(nc, x, ident, small, dram):
    semaphores = []
    with ExitStack() as ctx:
        def sb(name, shape, dt=F32):
            return ctx.enter_context(nc.sbuf_tensor("ffn_" + name, shape, dt))

        def sem(name):
            s = ctx.enter_context(nc.semaphore("ffn_" + name))
            semaphores.append(s)
            return s

        w = sb("w", [P, NLIN, KD, D])
        bias = sb("bias", [P, NLIN, D])
        gamma, beta = sb("gamma", [P, NBLK, KD]), sb("beta", [P, NBLK, KD])

        with ExitStack() as c1:
            q = c1.enter_context(nc.sbuf_tensor("ffn_q", [P, NLIN, KD, D], I32))
            scales = c1.enter_context(nc.sbuf_tensor("ffn_scales", [GROUP, NLIN, D], F32))
            spread = c1.enter_context(nc.sbuf_tensor("ffn_spread", [GROUP, KD, P], F32))
            lora_a = c1.enter_context(nc.sbuf_tensor("ffn_lora_a", [RANK, NLIN, D], F32))
            lora_b = c1.enter_context(nc.sbuf_tensor("ffn_lora_b", [RANK, NLIN, D], F32))
            scale_rows = [c1.enter_context(nc.psum_tensor(f"ffn_scale_rows{i}", [P, D], F32)) for i in range(2)]
            low_rank = [c1.enter_context(nc.psum_tensor(f"ffn_low_rank{i}", [P, D], F32)) for i in range(2)]
            loaded = c1.enter_context(nc.semaphore("ffn_ffn_loaded"))
            multiplied = c1.enter_context(nc.semaphore("ffn_multiplied"))
            built = c1.enter_context(nc.semaphore("ffn_built"))
            c1.callback(clear_semaphores, nc, [loaded, multiplied, built])
            block = c1.enter_context(nc.Block())
            slices = [(i, k) for i in range(NLIN) for k in range(KD)]

            @block.sync
            def _(sp):
                for dst, src in ((q, dram["qweights"].rearrange("i (k p) o -> p i k o", p=P)), (scales, dram["scales"]),
                                 (spread, dram["spread"]), (lora_a, dram["lora_a"]), (lora_b, dram["lora_b"]),
                                 (gamma, dram["ln_gamma"]), (beta, dram["ln_beta"])):
                    sp.dma_start(dst[(slice(None),) * len(dst.shape)], src).then_inc(loaded, 16)
                sp.dma_start(bias[:, :, :], dram["biases"].rearrange("(a i) o -> a i o", a=1).broadcast_to([P, NLIN, D])).then_inc(loaded, 16)

            @block.tensor
            def _(pe):
                pe.wait_ge(loaded, 16 * 8)
                for n, (i, k) in enumerate(slices):
                    if n >= 2:
                        pe.wait_ge(built, 3 * (n - 1))
                    pe.matmul(scale_rows[n % 2][:, :], spread[:, k, :], scales[:, i, :], start=True, stop=True)
                    pe.matmul(low_rank[n % 2][:, :], lora_a[:, i, k * P:(k + 1) * P], lora_b[:, i, :], start=True, stop=True)\
                        .then_inc(multiplied, 1)

            @block.vector
            def _(dve):
                dve.wait_ge(loaded, 16 * 8)
                for n, (i, k) in enumerate(slices):
                    at = w[:, i, k, :]
                    dve.tensor_scalar(at, q[:, i, k, :], 1.0 / 7.5, -1.0, ALU.mult, ALU.add).then_inc(built, 1)
                    dve.wait_ge(multiplied, n + 1)
                    dve.wait_ge(built, 3 * n + 1)
                    dve.tensor_tensor(at, at, scale_rows[n % 2][:, :], ALU.mult).then_inc(built, 1)
                    dve.wait_ge(built, 3 * n + 2)
                    dve.tensor_tensor(at, at, low_rank[n % 2][:, :], ALU.add).then_inc(built, 1)

        lanes = range(FL)
        stats = [sb(f"stats{l}", [P, 6]) for l in lanes]
        mv = [sb(f"mv{l}", [P, 2]) for l in lanes]
        var_eps = [sb(f"var_eps{l}", [P, 1]) for l in lanes]
        rstd = [sb(f"rstd{l}", [P, 1]) for l in lanes]
        h0 = [sb(f"h0_{l}", [P, D]) for l in lanes]
        h = [sb(f"h{l}", [P, D]) for l in lanes]
        h_bias = [sb(f"h_bias{l}", [P, D]) for l in lanes]
        h_T = [sb(f"h_T{l}", [P, KD, P]) for l in lanes]
        y = [sb(f"y{l}", [P, D]) for l in lanes]
        y_norm = [sb(f"y_norm{l}", [P, D]) for l in lanes]
        act_T = [sb(f"act_T{l}", [P, KD, P]) for l in lanes]
        turn = [ctx.enter_context(nc.psum_tensor(f"ffn_turn{l}", [P, 512], F32)) for l in lanes]
        acc = [ctx.enter_context(nc.psum_tensor(f"ffn_acc{l}", [P, 512], F32)) for l in lanes]
        NORMS = NBLK + 1
        stats_s = [sem(f"stats{n}_s") for n in range(NORMS)]
        mv_s = [sem(f"mv{n}_s") for n in range(NORMS)]
        ve_s = [sem(f"ve{n}_s") for n in range(NORMS)]
        rstd_s = [sem(f"rstd{n}_s") for n in range(NORMS)]
        h_s = [sem(f"h{n}_s") for n in range(NBLK + 1)]
        y_s, yn_s = [sem(f"y{n}_s") for n in range(NBLK)], [sem(f"yn{n}_s") for n in range(NBLK)]
        hb_s = [sem(f"hb{n}_s") for n in range(NBLK)]
        hT_s, aT_s = [sem(f"hT{n}_s") for n in range(NBLK)], [sem(f"aT{n}_s") for n in range(NBLK)]
        hTp_s, ynp_s = [sem(f"hTp{n}_s") for n in range(NBLK)], [sem(f"ynp{n}_s") for n in range(NBLK)]
        mm1_s, mm2_s = [sem(f"mm1{n}_s") for n in range(NBLK)], [sem(f"mm2{n}_s") for n in range(NBLK)]
        fence = sem("fence")
        pad_done = sem("pad_done")
        x_s = sem("xffn_s")
        ctx.callback(clear_semaphores, nc, semaphores)
        block = ctx.enter_context(nc.Block())

        def value(eng, v):
            return v if isinstance(v, int) else eng.snap(v)

        def counts(eng, it):
            return [value(eng, it * FL + k + 1) for k in range(FL + 1)]

        @block.gpsimd
        def _(pool):
            for s in ve_s + rstd_s + hb_s:
                pool.sem_inc(s, 1)

            def inverse_root(it, norm):
                n = counts(pool, it)
                for l in lanes:
                    pool.wait_ge(mv_s[norm], n[l + 1])
                    pool.tensor_tensor(var_eps[l][:, :], mv[l][:, 1:2], small[:, 2:3], ALU.add).then_inc(ve_s[norm], 1)
                    pool.wait_ge(ve_s[norm], n[l + 1])
                    pool.tensor_tensor(rstd[l][:, :], var_eps[l][:, :], small[:, 0:1], ALU.pow).then_inc(rstd_s[norm], 1)

            inverse_root(0, 0)
            with pool.Fori(0, NT // FL) as it:
                n = counts(pool, it)
                for b in range(NBLK):
                    for l in lanes:
                        pool.wait_ge(h_s[b], n[l + 1])
                        if b == 0:
                            pool.wait_ge(h_s[NBLK], n[0])
                        source = h if b else h0
                        pool.tensor_tensor(h_bias[l][:, :], source[l][:, :], bias[:, 2 * b + 1, :], ALU.add).then_inc(hb_s[b], 1)
                    inverse_root(it, b + 1)
                inverse_root(it + 1, 0)

        @block.scalar
        def _(act):
            for s in hT_s + aT_s:
                act.sem_inc(s, 1)
            with act.Fori(0, NT // FL) as it:
                n = counts(act, it)
                for b in range(NBLK):
                    for l in lanes:
                        act.wait_ge(hTp_s[b], n[l + 1])
                        act.activation(h_T[l][:, :, :], turn[l][:, 0:D], ACT.Copy).then_inc(hT_s[b], 1)
                    for l in lanes:
                        act.wait_ge(ynp_s[b], n[l + 1])
                        for k in range(KD):
                            last = act.activation(act_T[l][:, k, :], turn[l][:, k * P:(k + 1) * P], ACT.Gelu,
                                                  scale=gamma[:, b, k:k + 1], bias=beta[:, b, k:k + 1])
                        last.then_inc(aT_s[b], 1)

        @block.vector
        def _(dve):
            for s in stats_s + mv_s + h_s + y_s + yn_s + [x_s]:
                dve.sem_inc(s, 1)

            def norm_of(n, l, norm, source):
                dve.bn_stats(stats[l][:, :], source).then_inc(stats_s[norm], 1)
                dve.wait_ge(stats_s[norm], n[l + 1])
                dve.sem_inc(fence, 1)
                dve.bn_aggr(mv[l][:, :], stats[l][:, :]).then_inc(mv_s[norm], 1)

            def normalise(n, l, norm, out, source, s):
                dve.wait_ge(mv_s[norm], n[l + 1])
                dve.wait_ge(rstd_s[norm], n[l + 1])
                dve.tensor_scalar(out, source, mv[l][:, 0:1], rstd[l][:, 0:1], ALU.subtract, ALU.mult).then_inc(s, 1)

            def norm_input(it):
                n = counts(dve, it)
                tile = [value(dve, it * FL + l) for l in lanes]
                for l in lanes:
                    norm_of(n, l, 0, x[:, tile[l], :])
                for l in lanes:
                    normalise(n, l, 0, h0[l][:, :], x[:, tile[l], :], h_s[0])

            dve.memset(x[:, NT:, :], 0.0).then_inc(pad_done, 1)
            dve.wait_ge(pad_done, 1)
            norm_input(0)
            with dve.Fori(0, NT // FL) as it:
                n = counts(dve, it)
                tile = [dve.snap(it * FL + l) for l in lanes]
                for b in range(NBLK):
                    for l in lanes:
                        dve.wait_ge(mm1_s[b], n[l + 1])
                        dve.tensor_tensor(y[l][:, :], acc[l][:, 0:D], bias[:, 2 * b, :], ALU.add).then_inc(y_s[b], 1)
                        dve.wait_ge(y_s[b], n[l + 1])
                        dve.sem_inc(fence, 1)
                        norm_of(n, l, b + 1, y[l][:, :])
                        if l > 0:
                            normalise(n, l - 1, b + 1, y_norm[l - 1][:, :], y[l - 1][:, :], yn_s[b])
                    normalise(n, FL - 1, b + 1, y_norm[FL - 1][:, :], y[FL - 1][:, :], yn_s[b])
                    if b == NBLK - 1:
                        norm_input(it + 1)
                    for l in lanes:
                        dve.wait_ge(mm2_s[b], n[l + 1])
                        dve.wait_ge(hb_s[b], n[l + 1])
                        dve.tensor_tensor(h[l][:, :], h_bias[l][:, :], acc[l][:, 0:D], ALU.add).then_inc(h_s[b + 1], 1)
                for l in lanes:
                    dve.wait_ge(h_s[NBLK], n[l + 1])
                    dve.tensor_tensor(x[:, tile[l], :], x[:, tile[l], :], h[l][:, :], ALU.add).then_inc(x_s, 1)

        @block.tensor
        def _(pe):
            for s in hTp_s + ynp_s + mm1_s + mm2_s:
                pe.sem_inc(s, 1)
            with pe.Fori(0, NT // FL) as it:
                n = counts(pe, it)

                def turned(l, source, s, s_done):
                    pe.wait_ge(s, n[l + 1])
                    for k in range(KD):
                        last = pe.transpose(turn[l][:, k * P:(k + 1) * P], source[l][:, k * P:(k + 1) * P], ident)
                    last.then_inc(s_done, 1)

                def product(l, source, i, s, s_done):
                    pe.wait_ge(s, n[l + 1])
                    for k in range(KD):
                        last = pe.matmul(acc[l][:, 0:D], source[l][:, k, :], w[:, i, k, :], start=(k == 0), stop=(k == KD - 1))
                    last.then_inc(s_done, 1)

                for b in range(NBLK):
                    for l in range(FL + 1):
                        if l < FL:
                            turned(l, h if b else h0, h_s[b], hTp_s[b])
                        if l > 0:
                            if b == 0:
                                pe.wait_ge(h_s[NBLK], n[0])
                            product(l - 1, h_T, 2 * b, hT_s[b], mm1_s[b])
                    for l in range(FL + 1):
                        if l < FL:
                            turned(l, y_norm, yn_s[b], ynp_s[b])
                        if l > 0:
                            product(l - 1, act_T, 2 * b + 1, aT_s[b], mm2_s[b])


def gqa_attention(nc, x, ident, small, dram):
    semaphores = []
    with ExitStack() as ctx:
        def sb(name, shape, dt=F32):
            return ctx.enter_context(nc.sbuf_tensor("gqa_" + name, shape, dt))

        def sem(name):
            s = ctx.enter_context(nc.semaphore("gqa_" + name))
            semaphores.append(s)
            return s

        lanes, slots = range(FL), range(4)
        HB = NH // 2
        QW = NH * HD
        w_qkv = sb("w_qkv", [P, KD, QW + 2 * NKV * HD])
        w_o = sb("w_o", [P, KD, D])
        cos, sin = sb("cos", [P, TPB, HD]), sb("sin", [P, TPB, HD])
        mask32 = sb("mask32", [P, 2, P])
        mask = sb("mask", [P, 2, P], BF16)
        ident_b, ident_h = sb("ident_b", [P, P], BF16), sb("ident_h", [P, P], F16)
        stats = [sb(f"stats{l}", [P, 6]) for l in lanes]
        mv = [sb(f"mv{l}", [P, 2]) for l in lanes]
        var_eps = [sb(f"var_eps{l}", [P, 1]) for l in lanes]
        rstd = [sb(f"rstd{l}", [P, 1]) for l in lanes]
        x_norm = [sb(f"x_norm{l}", [P, D]) for l in lanes]
        x_T = [sb(f"x_T{l}", [P, KD, P]) for l in lanes]
        NR_ = NH + NKV
        by_cos = [sb(f"by_cos{l}", [P, NR_, HD]) for l in lanes]
        by_sin = [sb(f"by_sin{l}", [P, NR_, HD]) for l in lanes]
        rot = [sb(f"rot{l}", [P, NR_, HD]) for l in lanes]
        q_feat = sb("q_feat", [P, TPB, NH, FEAT], F16)
        k_feat = [sb(f"k_feat{l}", [P, NKV, 2, 2 * FEAT], F16) for l in lanes]
        q_T, k_T = sb("q_T", [P, HB, T], F16), sb("k_T", [P, NKV, 2, T], F16)
        v_aug = sb("v_aug", [P, TPB, NKV, 32])
        v_group = sb("v_group", [P, TPB, 32])
        part_max = sb("part_max", [P, TPB, 4, 2])
        prob = [sb(f"prob{i}", [P, T]) for i in slots]
        o_T = sb("o_T", [P, T])
        inv_sum = sb("inv_sum", [P, TPB * 4])
        y = sb("y", [P, TPB, D])
        y_T = [sb(f"y_T{l}", [P, KD, P]) for l in lanes]
        bank = [ctx.enter_context(nc.psum_tensor(f"gqa_bank{i}", [P, 1024], F32)) for i in range(4)]
        pv, back = bank[2], bank[3]

        S = {n: sem(n) for n in (
            "fd", "fa", "fp", "stats", "mv", "ve", "rstd", "xn", "xTp", "xT", "proj", "cos", "sin", "rot", "v", "qhi", "qlo", "khi", "klo",
            "kdup", "qTp", "qT", "kTp", "kT", "score", "max", "m16", "vg", "q2p", "q2", "st", "exp", "pv", "oT", "oTp", "inv", "y",
            "yTp", "yT", "out", "x")}
        owner = {"dve": "stats mv xn cos sin v qlo klo kdup kT max m16 vg q2 oT inv y x".split(),
                 "act": "xT qhi khi qT exp yT".split(), "pool": "ve rstd rot".split(),
                 "pe": "xTp proj qTp kTp score q2p st pv oTp yTp out".split()}
        START = {"max": 2, "kT": FL, "pv": 4, "exp": 2}
        loaded, setup = sem("loaded"), sem("setup")
        ctx.callback(clear_semaphores, nc, semaphores)
        block = ctx.enter_context(nc.Block())
        PIECES = [(r, t, lo, min(lo + 512, (t + 1) * P)) for r in range(4) for t in range(TPB) for lo in range(0, (t + 1) * P, 512)]
        NS = len(PIECES)
        NC = 4 * TPB

        def first(eng, who):
            for n in owner[who]:
                eng.sem_inc(S[n], START.get(n, 1))

        def wait(eng, name, index, back_by=0):
            value = index + (START.get(name, 1) + 1 - back_by)
            eng.wait_ge(S[name], value if isinstance(value, int) else eng.snap(value))

        def fenced(eng, fence, name, index, back_by=0):
            wait(eng, name, index, back_by)
            eng.sem_inc(S[fence], 1)

        @block.sync
        def _(sp):
            for dst, src in ((w_qkv, "w_qkv"), (w_o, "w_o"), (cos, "cos"), (sin, "sin"), (mask32, "causal")):
                sp.dma_start(dst[:, :, :], dram[src]).then_inc(loaded, 16)

        @block.gpsimd
        def _(pool):
            first(pool, "pool")

            def inverse_root(at):
                for l in lanes:
                    wait(pool, "mv", at + l)
                    pool.tensor_tensor(var_eps[l][:, :], mv[l][:, 1:2], small[:, 2:3], ALU.add).then_inc(S["ve"], 1)
                    wait(pool, "ve", at + l)
                    pool.tensor_tensor(rstd[l][:, :], var_eps[l][:, :], small[:, 0:1], ALU.pow).then_inc(S["rstd"], 1)

            inverse_root(0)
            with pool.Fori(0, B) as b:
                for half in range(2):
                    at = pool.snap((b * 2 + half) * FL)
                    for l in lanes:
                        wait(pool, "cos", at + l)
                        wait(pool, "sin", at + l)
                        pool.tensor_tensor(rot[l][:, :, :], by_cos[l][:, :, :], by_sin[l][:, :, :], ALU.add).then_inc(S["rot"], 1)
                    inverse_root(at + FL)

        @block.scalar
        def _(act):
            first(act, "act")
            act.wait_ge(loaded, 16 * 5)
            act.activation(mask[:, :, :], mask32[:, :, :], ACT.Copy).then_inc(setup, 1)
            act.activation(ident_b[:, :], ident, ACT.Copy).then_inc(setup, 1)
            act.activation(ident_h[:, :], ident, ACT.Copy).then_inc(setup, 1)
            act.wait_ge(setup, 3 + NSET)
            with act.Fori(0, B) as b:
                for half in range(2):
                    at = act.snap((b * 2 + half) * FL)
                    for l in lanes:
                        wait(act, "xTp", at + l)
                        act.activation(x_T[l][:, :, :], bank[l][:, 0:D], ACT.Copy).then_inc(S["xT"], 1)
                    for l in lanes:
                        wait(act, "rot", at + l)
                        rq = rot[l][:, 0:NH, :]
                        tile = half * FL + l
                        act.activation(q_feat[:, tile, :, 0:HD], rq, ACT.Copy)
                        act.activation(q_feat[:, tile, :, HD:2 * HD], rq, ACT.Copy).then_inc(S["qhi"], 1)
                        act.activation(k_feat[l][:, :, 0, 0:HD], rot[l][:, NH:, :], ACT.Copy)
                        act.activation(k_feat[l][:, :, 0, 2 * HD:3 * HD], rot[l][:, NH:, :], ACT.Copy).then_inc(S["khi"], 1)
                    for l in lanes:
                        wait(act, "qTp", at + l)
                        act.activation(q_T[:, :, (half * FL + l) * P:(half * FL + l + 1) * P],
                                       bank[l][:, :].rearrange("p (h t) -> p h t", t=P), ACT.Copy).then_inc(S["qT"], 1)
                with act.Fori(0, NKV) as g:
                    for r in range(4):
                        for kt in range(TPB):
                            u = (b * NKV + g) * NC + (r * TPB + kt)
                            wait(act, "st", u)
                            wait(act, "pv", u, 4)
                            act.activation(prob[kt % 4][:, kt * P:T], bank[kt % 2][:, kt * P:T], ACT.Exp, scale=HD ** -0.5)\
                                .then_inc(S["exp"], 1)
                for h in range(2):
                    for l in lanes:
                        wait(act, "yTp", b * TPB + h * FL + l)
                        act.activation(y_T[l][:, :, :], bank[l][:, 0:D], ACT.Copy).then_inc(S["yT"], 1)

        @block.vector
        def _(dve):
            V = nc.vector
            first(dve, "dve")
            V.memset(x[:, NT:, :], 0.0).then_inc(setup, 1)
            V.memset(q_feat[:, :, :, 3 * HD:], 0.0).then_inc(setup, 1)
            for l in lanes:
                V.memset(k_feat[l][:, :, :, :], 0.0).then_inc(setup, 1)
            V.memset(v_aug[:, :, :, HD:], 0.0).then_inc(setup, 1)
            V.memset(part_max[:, :, :, :], -3e38).then_inc(setup, 1)
            dve.wait_ge(setup, 3 + 4 + FL)
            for l in lanes:
                V.memset(k_feat[l][:, :, 0, 3 * HD:3 * HD + 1], -1.0)
                V.memset(k_feat[l][:, :, 1, FEAT + 3 * HD:FEAT + 3 * HD + 1], -1.0).then_inc(setup, 1)
            V.memset(v_aug[:, :, :, HD:HD + 1], 1.0).then_inc(setup, 1)
            dve.wait_ge(setup, 3 + NSET)
            dve.wait_ge(loaded, 16 * 5)

            def maxima(b, g):
                group = dve.snap(b * NKV + g)
                for i, (r, t, lo, hi) in enumerate(PIECES):
                    wait(dve, "score", group * NS + i)
                    at = (i % 2) * 512
                    V.reduce_max(part_max[:, t, r, lo // 512:lo // 512 + 1], back[:, at:at + hi - lo], axis=AX_X).then_inc(S["max"], 1)
                wait(dve, "max", group * NS + (NS - 1))
                V.tensor_tensor(q_feat[:, :, bass.ds(g * 4, 4), 3 * HD], part_max[:, :, :, 0], part_max[:, :, :, 1], ALU.max)\
                    .then_inc(S["m16"], 1)
                for half in range(2):
                    fenced(dve, "fd", "q2p", group * 2 + half)
                    V.tensor_copy(q_T[:, bass.ds(g * 2, 2), half * 512:(half + 1) * 512],
                                  back[:, :].rearrange("p (h t) -> p h t", h=2)).then_inc(S["q2"], 1)

            def v_of_group(b, g):
                V.tensor_copy(v_group[:, :, :], v_aug[:, :, g, :]).then_inc(S["vg"], 1)

            def normalise(b, g):
                at = dve.snap(b * NKV + g)
                wait(dve, "pv", at * NC + (NC - 1))
                V.tensor_copy(o_T[:, :], pv[:, :]).then_inc(S["oT"], 1)
                wait(dve, "oTp", at)
                heads = back[:, :].rearrange("p (h d) -> p h d", d=32)
                V.reciprocal(inv_sum[:, :], heads[:, :, HD]).then_inc(S["inv"], 1)
                wait(dve, "inv", at)
                for t in range(TPB):
                    four = slice(4 * t, 4 * t + 4)
                    last = V.tensor_tensor(y[:, t, bass.ds(g * 4 * HD, 4 * HD)].rearrange("p (r d) -> p r d", d=HD), heads[:, four, 0:HD],
                                           inv_sum[:, four][:, :, None].broadcast_to([P, 4, HD]), ALU.mult)
                last.then_inc(S["y"], 1)

            def statistics(at):
                for l in lanes:
                    tile = at + l if isinstance(at, int) else dve.snap(at + l)
                    V.bn_stats(stats[l][:, :], x[:, tile, :]).then_inc(S["stats"], 1)
                for l in lanes:
                    fenced(dve, "fd", "stats", at + l)
                    V.bn_aggr(mv[l][:, :], stats[l][:, :]).then_inc(S["mv"], 1)

            def norm(at):
                for l in lanes:
                    tile = at + l if isinstance(at, int) else dve.snap(at + l)
                    wait(dve, "mv", at + l)
                    wait(dve, "rstd", at + l)
                    V.tensor_scalar(x_norm[l][:, :], x[:, tile, :], mv[l][:, 0:1], rstd[l][:, 0:1],
                                    ALU.subtract, ALU.mult).then_inc(S["xn"], 1)

            statistics(0)
            norm(0)
            with dve.Fori(0, B) as b:
                for half in range(2):
                    at = dve.snap((b * 2 + half) * FL)
                    for l in lanes:
                        wait(dve, "proj", at + l)
                        tile = half * FL + l
                        heads = bank[l][:, 512:512 + NR_ * HD].rearrange("p (h d) -> p h d", d=HD)
                        H2 = HD // 2
                        V.tensor_tensor(by_cos[l][:, :, :], heads, cos[:, tile, :][:, None, :].broadcast_to([P, NR_, HD]), ALU.mult)\
                            .then_inc(S["cos"], 1)
                        V.tensor_tensor(by_sin[l][:, :, 0:H2], heads[:, :, H2:], sin[:, tile, 0:H2][:, None, :].broadcast_to([P, NR_, H2]), ALU.mult)
                        V.tensor_tensor(by_sin[l][:, :, H2:], heads[:, :, 0:H2], sin[:, tile, H2:][:, None, :].broadcast_to([P, NR_, H2]), ALU.mult)\
                            .then_inc(S["sin"], 1)
                        V.tensor_copy(v_aug[:, tile, :, 0:HD],
                                      bank[l][:, 512 + NR_ * HD:512 + (NR_ + NKV) * HD].rearrange("p (h d) -> p h d", d=HD)).then_inc(S["v"], 1)
                    for l in lanes:
                        tile = half * FL + l
                        wait(dve, "qhi", at + l)
                        V.tensor_tensor(q_feat[:, tile, :, 2 * HD:3 * HD], rot[l][:, 0:NH, :], q_feat[:, tile, :, 0:HD], ALU.subtract)\
                            .then_inc(S["qlo"], 1)
                        wait(dve, "khi", at + l)
                        V.tensor_tensor(k_feat[l][:, :, 0, HD:2 * HD], rot[l][:, NH:, :], k_feat[l][:, :, 0, 0:HD], ALU.subtract)\
                            .then_inc(S["klo"], 1)
                        wait(dve, "klo", at + l)
                        V.tensor_copy(k_feat[l][:, :, 1, FEAT:FEAT + 3 * HD], k_feat[l][:, :, 0, 0:3 * HD]).then_inc(S["kdup"], 1)
                    if half == 0:
                        statistics(dve.snap((b * 2 + 1) * FL))
                    for l in lanes:
                        wait(dve, "kTp", at + l)
                        V.tensor_copy(k_T[:, :, :, :].rearrange("p g c t -> p (g c) t")[:, :, (half * FL + l) * P:(half * FL + l + 1) * P],
                                      bank[l][:, :].rearrange("p (h t) -> p h t", t=P)).then_inc(S["kT"], 1)
                    if half == 0:
                        norm(dve.snap((b * 2 + 1) * FL))
                maxima(b, 0)
                with dve.Fori(0, NKV - 1) as g:
                    v_of_group(b, g)
                    maxima(b, g + 1)
                    normalise(b, g)
                v_of_group(b, NKV - 1)
                statistics(dve.snap((b * 2 + 2) * FL))
                norm(dve.snap((b * 2 + 2) * FL))
                normalise(b, NKV - 1)
                for h in range(2):
                    for l in lanes:
                        tile = b * TPB + h * FL + l
                        wait(dve, "out", tile)
                        V.tensor_tensor(x[:, tile, :], x[:, tile, :], bank[l][:, 512:512 + D], ALU.add).then_inc(S["x"], 1)

        @block.tensor
        def _(pe):
            first(pe, "pe")
            pe.wait_ge(setup, 3 + NSET)

            def score(b, g, i):
                r, t, lo, hi = PIECES[i]
                hb = pe.snap(g * 2 + r // 2) if not isinstance(g, int) else g * 2 + r // 2
                fenced(pe, "fp", "max", (b * NKV + g) * NS + i, 2)
                at = (i % 2) * 512 - lo
                diagonal = hi == (t + 1) * P
                last = pe.matmul(back[:, at + lo:at + hi], q_T[:, hb, t * P:(t + 1) * P], k_T[:, g, r % 2, lo:hi], start=True, stop=not diagonal)
                if diagonal:
                    last = pe.matmul(back[:, at + t * P:at + hi], ident_b[:, :], mask[:, 0, :], start=False, stop=True)
                last.then_inc(S["score"], 1)

            def turn_again(b, g):
                wait(pe, "m16", b * NKV + g)
                for half in range(2):
                    if half:
                        wait(pe, "q2", (b * NKV + g) * 2)
                    for i in range(2):
                        for t in range(4):
                            flat = q_feat[:, half * 4 + t, :, :].rearrange("p h f -> p (h f)")
                            last = pe.matmul(back[:, i * 512 + t * P:i * 512 + (t + 1) * P], flat[:, bass.ds((g * 2 + i) * P, P)], ident_h[:, :],
                                             start=True, stop=True)
                    last.then_inc(S["q2p"], 1)

            def group_of(b, g, more):
                group = pe.snap(b * NKV + g)
                fenced(pe, "fp", "q2", group * 2 + 1)

                def pieces_up_to(n):
                    while more and done[0] < min(NS, -(-n * NS // (4 * 36))):
                        score(b, g + 1, done[0])
                        done[0] += 1

                def values(i, due):
                    r, kt = divmod(i, TPB)
                    fenced(pe, "fp", "exp", group * NC + i)
                    if i == 0:
                        fenced(pe, "fp", "vg", group)
                        fenced(pe, "fp", "oT", group, 1)
                    for lo in (0, 512):
                        start = max(lo, kt * P)
                        if start < lo + 512:
                            last = pe.matmul(pv[32 * r:32 * r + 32, start:lo + 512], v_group[:, kt, :], prob[kt % 4][:, start:lo + 512],
                                             start=(kt == 0), stop=(kt * P + P == lo + 512), tile_position=(0, 32 * r))
                            if start < 512:
                                pieces_up_to(due)
                    last.then_inc(S["pv"], 1)

                done = [0]
                if more:
                    wait(pe, "y", group, 1)
                for r in range(4):
                    hb = pe.snap(g * 2 + r // 2) if not isinstance(g, int) else g * 2 + r // 2
                    for kt in range(TPB):
                        i = r * TPB + kt
                        fenced(pe, "fp", "exp", group * NC + i, 2)
                        out = bank[kt % 2]
                        before = r * 36 + sum(TPB - k for k in range(kt))
                        for lo in (0, 512):
                            start = max(lo, kt * P)
                            if start < lo + 512:
                                pe.matmul(out[:, start:lo + 512], k_T[:, g, r % 2, kt * P:(kt + 1) * P], q_T[:, hb, start:lo + 512],
                                          start=True, stop=(start != kt * P))
                                if start < 512:
                                    pieces_up_to(before + 2)
                        pe.matmul(out[:, kt * P:(kt + 1) * P], ident_b[:, :], mask[:, 1, :], start=False, stop=True).then_inc(S["st"], 1)
                        pieces_up_to(before + (TPB - kt) // 2)
                        if i > 0:
                            values(i - 1, before + 3 * (TPB - kt) // 4)
                        pieces_up_to(before + TPB - kt)
                values(NC - 1, 4 * 36)
                if more:
                    turn_again(b, g + 1)
                    fenced(pe, "fp", "q2", group * 2 + 3)
                wait(pe, "oT", group)
                wait(pe, "y", group, 1)
                for t in range(TPB):
                    last = pe.transpose(back[:, t * P:(t + 1) * P], o_T[:, t * P:(t + 1) * P], ident)
                last.then_inc(S["oTp"], 1)

            with pe.Fori(0, B) as b:
                for half in range(2):
                    at = pe.snap((b * 2 + half) * FL)
                    for l in lanes:
                        wait(pe, "xn", at + l)
                        wait(pe, "kT", at + l, FL)
                        if half == 0:
                            wait(pe, "x", b * TPB, 1)
                        for k in range(KD):
                            last = pe.transpose(bank[l][:, k * P:(k + 1) * P], x_norm[l][:, k * P:(k + 1) * P], ident)
                        last.then_inc(S["xTp"], 1)
                    for l in lanes:
                        wait(pe, "xT", at + l)
                        for k in range(KD):
                            last = pe.matmul(bank[l][:, 512:512 + QW + 2 * NKV * HD], x_T[l][:, k, :], w_qkv[:, k, :],
                                             start=(k == 0), stop=(k == KD - 1))
                        last.then_inc(S["proj"], 1)
                    for l in lanes:
                        fenced(pe, "fp", "qlo", at + l)
                        fenced(pe, "fp", "v", at + l)
                        flat = q_feat[:, half * FL + l, :, :].rearrange("p h f -> p (h f)")
                        for i in range(HB):
                            last = pe.matmul(bank[l][:, i * P:(i + 1) * P], flat[:, i * P:(i + 1) * P], ident_h[:, :], start=True, stop=True)
                        last.then_inc(S["qTp"], 1)
                    for l in lanes:
                        wait(pe, "qT", at + l)
                        wait(pe, "kdup", at + l)
                        flat = k_feat[l][:, :, :, :].rearrange("p g c f -> p (g c f)")
                        for i in range(2 * NKV):
                            last = pe.matmul(bank[l][:, i * P:(i + 1) * P], flat[:, i * P:(i + 1) * P], ident_h[:, :], start=True, stop=True)
                        last.then_inc(S["kTp"], 1)
                fenced(pe, "fp", "kT", b * TPB + (TPB - 1))
                for i in range(NS):
                    score(b, 0, i)
                turn_again(b, 0)
                with pe.Fori(0, NKV - 1) as g:
                    group_of(b, g, True)
                group_of(b, NKV - 1, False)
                wait(pe, "y", b * NKV + (NKV - 1))
                for h in range(2):
                    for l in lanes:
                        if h == 1:
                            wait(pe, "x", b * TPB + l)
                        t = h * FL + l
                        for k in range(KD):
                            last = pe.transpose(bank[l][:, k * P:(k + 1) * P], y[:, t, k * P:(k + 1) * P], ident)
                        last.then_inc(S["yTp"], 1)
                    for l in lanes:
                        wait(pe, "yT", b * TPB + h * FL + l)
                        for k in range(KD):
                            last = pe.matmul(bank[l][:, 512:512 + D], y_T[l][:, k, :], w_o[:, k, :], start=(k == 0), stop=(k == KD - 1))
                        last.then_inc(S["out"], 1)


def moe_ffn(nc, x, ident, small, dram):
    with ExitStack() as ctx:
        def sb(name, shape, dt=F32):
            return ctx.enter_context(nc.sbuf_tensor("moe_" + name, shape, dt))

        def sem(name):
            return ctx.enter_context(nc.semaphore("moe_" + name))

        lanes = range(FL)
        TOK = FL * P
        parts = ("hi", "lo")
        w_gu = {s: sb(f"w_gu_{s}", [P, KD, NEXP * 2 * IP], F16) for s in parts}
        w_dn = {s: sb(f"w_dn_{s}", [P, KI, NEXP * D], F16) for s in parts}
        w_route = sb("w_route", [P, KD, NEXP])
        before = sb("before", [P, FL * NR * NR])

        with ExitStack() as c1:
            SLOTS = 6
            stage = [c1.enter_context(nc.sbuf_tensor(f"moe_stage{i}", [P, KD * 2 * IP], F32)) for i in range(SLOTS)]
            staged = [c1.enter_context(nc.semaphore(f"moe_staged{i}")) for i in range(SLOTS)]
            others = c1.enter_context(nc.semaphore("moe_route_loaded"))
            hi_done = c1.enter_context(nc.semaphore("moe_hi_done"))
            lo_done = c1.enter_context(nc.semaphore("moe_lo_done"))
            c1.callback(clear_semaphores, nc, staged + [others, hi_done, lo_done])
            block = c1.enter_context(nc.Block())
            jobs = [(e, kind) for e in range(NEXP) for kind in range(2)]

            def views(n):
                e, kind = jobs[n]
                if kind == 0:
                    st = stage[n % SLOTS][:, :].rearrange("p (k i) -> p k i", k=KD)
                    return st, [w_gu[s][:, :, e * 2 * IP:(e + 1) * 2 * IP] for s in parts], dram["w_gate_up"][e]
                st = stage[n % SLOTS][:, 0:KI * D].rearrange("p (k i) -> p k i", k=KI)
                return st, [w_dn[s][:, :, e * D:(e + 1) * D] for s in parts], dram["w_down"][e]

            @block.sync
            def _(sp):
                sp.dma_start(w_route[:, :, :], dram["w_route"]).then_inc(others, 16)
                sp.dma_start(before[:, :], dram["before"]).then_inc(others, 16)
                for n in range(len(jobs)):
                    st, _, src = views(n)
                    if n >= SLOTS:
                        sp.wait_ge(lo_done, n - SLOTS + 1)
                    sp.dma_start(st, src).then_inc(staged[n % SLOTS], 16)
                sp.wait_ge(others, 32)

            @block.scalar
            def _(act):
                for n in range(len(jobs)):
                    st, (hi, lo), _ = views(n)
                    act.wait_ge(staged[n % SLOTS], 16 * (n // SLOTS + 1))
                    act.activation(hi, st, ACT.Copy).then_inc(hi_done, 1)

            @block.vector
            def _(dve):
                for n in range(len(jobs)):
                    st, (hi, lo), _ = views(n)
                    dve.wait_ge(hi_done, n + 1)
                    dve.tensor_tensor(lo, st, hi, ALU.subtract).then_inc(lo_done, 1)

        stats = [sb(f"stats{l}", [P, 6]) for l in lanes]
        mv = [sb(f"mv{l}", [P, 2]) for l in lanes]
        var_eps = [sb(f"var_eps{l}", [P, 1]) for l in lanes]
        rstd = [sb(f"rstd{l}", [P, 1]) for l in lanes]
        res = [sb(f"res{l}", [P, D]) for l in lanes]
        x_norm = [sb(f"x_norm{l}", [P, D]) for l in lanes]
        x_T = sb("x_T", [P, KD, TOK])
        x_T_hi, x_T_lo = sb("x_T_hi", [P, KD, TOK], F16), sb("x_T_lo", [P, KD, TOK], F16)
        silu = [sb(f"silu{i}", [P, TOK]) for i in range(2)]
        hidden = [sb(f"hidden{i}", [P, TOK]) for i in range(2)]
        hid_hi = sb("hid_hi", [P, 2 * KI, TOK], F16)
        hid_lo = sb("hid_lo", [P, 2 * KI, TOK], F16)
        logit = sb("logit", [P, FL, NEXP])
        score = sb("score", [P, FL * NR])
        top = sb("top", [P, FL])
        e_arg, e_val = sb("e_arg", [P, FL, NEXP]), sb("e_val", [P, FL, NEXP])
        other = sb("other", [P, FL * NR, NR])
        above, not_below = sb("above", [P, FL * NR, NR]), sb("not_below", [P, FL * NR, NR])
        rank, chosen = sb("rank", [P, FL * NR]), sb("chosen", [P, FL * NR])
        total, inv_total = sb("total", [P, FL]), sb("inv_total", [P, FL])
        shared_d = sb("shared_d", [P, FL])
        share = [sb(f"share{i}", [P, FL, NEXP]) for i in range(1)]
        turn = [ctx.enter_context(nc.psum_tensor(f"moe_turn{k}", [P, 512], F32)) for k in range(KD)]
        gate_p = [ctx.enter_context(nc.psum_tensor(f"moe_gate_p{i}", [P, 512], F32)) for i in range(2)]
        up_p = [ctx.enter_context(nc.psum_tensor(f"moe_up_p{i}", [P, 512], F32)) for i in range(2)]
        out_p = [ctx.enter_context(nc.psum_tensor(f"moe_out_p{i}", [P, 512], F32)) for i in range(2)]

        names = {"dve": ["res_s", "stats_s", "mv_s", "xn_s", "lo_s", "hid_s", "hlo_s", "sum_s", "back_s", "fence"],
                 "act": ["xT_s", "xhi_s", "exp_s", "silu_s", "hhi_s"],
                 "pe": ["turn_s", "logit_s", "gu_s", "out_s"], "pool": ["ve_s", "rstd_s"]}
        S = {n: sem(n) for g in names.values() for n in g}
        route = sem("route")
        block = ctx.enter_context(nc.Block())
        NU = NEXP * KI

        SUM0 = FL + 1

        def buf(half, i):
            return (half * KI + i) % 2

        def first(eng, g):
            for n in names[g]:
                eng.sem_inc(S[n], 1)

        def value(eng, v):
            return v if isinstance(v, int) else eng.snap(v)

        def lane_counts(eng, f):
            return [value(eng, f * FL + k + 1) for k in range(FL + 1)]

        @block.gpsimd
        def _(pool):
            first(pool, "pool")
            with pool.Fori(0, NT // FL + 1) as it:
                n = lane_counts(pool, it)
                for l in lanes:
                    pool.wait_ge(S["mv_s"], n[l + 1])
                    pool.tensor_tensor(var_eps[l][:, :], mv[l][:, 1:2], small[:, 2:3], ALU.add).then_inc(S["ve_s"], 1)
                    pool.wait_ge(S["ve_s"], n[l + 1])
                    pool.tensor_tensor(rstd[l][:, :], var_eps[l][:, :], small[:, 0:1], ALU.pow).then_inc(S["rstd_s"], 1)

        @block.tensor
        def _(pe):
            first(pe, "pe")

            def units(it, e, half):
                for i in range(KI):
                    u = it * NU + e * KI + i
                    pe.wait_ge(S["hid_s"], pe.snap(u + 1 if isinstance(e, int) and i == 0 else u))
                    for which, bank in enumerate((gate_p[buf(half, i)], up_p[buf(half, i)])):
                        n = 0
                        for k in range(KD):
                            col = bass.ds(e * 2 * IP + which * IP + i * P, P)
                            for w_, x_ in ((w_gu["hi"], x_T_hi), (w_gu["lo"], x_T_hi), (w_gu["hi"], x_T_lo)):
                                last = pe.matmul(bank[:, :], w_[:, k, col], x_[:, k, :], start=(n == 0), stop=(n == 3 * KD - 1))
                                n += 1
                    last.then_inc(S["gu_s"], 1)

            def down(it, e, half):
                pe.wait_ge(S["hlo_s"], pe.snap(it * NU + e * KI + KI + 1))
                for l in lanes:
                    if l % 2 == 0:
                        pe.wait_ge(S["sum_s"], pe.snap(it * (NEXP * FL) + e * FL + l + SUM0 - 2))
                    n = 0
                    for i in range(KI):
                        tok = slice(l * P, (l + 1) * P)
                        col = bass.ds(e * D, D)
                        for h_, w_ in ((hid_hi, w_dn["hi"]), (hid_hi, w_dn["lo"]), (hid_lo, w_dn["hi"])):
                            last = pe.matmul(out_p[l // 2][:, (l % 2) * D:(l % 2 + 1) * D], h_[:, half * KI + i, tok], w_[:, i, col],
                                             start=(n == 0), stop=(n == 3 * KI - 1))
                            n += 1
                    last.then_inc(S["out_s"], 1)

            def turns(f):
                n = lane_counts(pe, f)
                for l in lanes:
                    pe.wait_ge(S["xn_s"], n[l + 1])
                    for k in range(KD):
                        last = pe.transpose(turn[k][:, l * P:(l + 1) * P], x_norm[l][:, k * P:(k + 1) * P], ident)
                    last.then_inc(S["turn_s"], 1)

            turns(0)
            with pe.Fori(0, NT // FL) as it:
                pe.wait_ge(S["lo_s"], pe.snap(it * KD + KD + 1))
                for l in lanes:
                    for k in range(KD):
                        last = pe.matmul(turn[0][:, l * 16:l * 16 + NEXP], x_T[:, k, l * P:(l + 1) * P], w_route[:, k, :],
                                         start=(k == 0), stop=(k == KD - 1))
                last.then_inc(S["logit_s"], 1)
                units(it, 0, 0)
                with pe.Fori(0, NEXP // 2) as pair:
                    units(it, 2 * pair + 1, 1)
                    down(it, 2 * pair, 0)
                    units(it, 2 * pair + 2, 0)
                    down(it, 2 * pair + 1, 1)
                turns(it + 1)
                down(it, NEXP - 1, 0)

        @block.scalar
        def _(act):
            first(act, "act")

            def units(it, e, half):
                for i in range(KI):
                    u = act.snap(it * NU + e * KI + i + 2)
                    act.wait_ge(S["gu_s"], u)
                    act.activation(silu[buf(half, i)][:, :], gate_p[buf(half, i)][:, :], ACT.Silu).then_inc(S["silu_s"], 1)
                    act.wait_ge(S["hid_s"], u)
                    act.activation(hid_hi[:, half * KI + i, :], hidden[buf(half, i)][:, :], ACT.Copy).then_inc(S["hhi_s"], 1)

            def evacuate(f):
                act.wait_ge(S["turn_s"], lane_counts(act, f)[FL])
                for k in range(KD):
                    act.activation(x_T_hi[:, k, :], turn[k][:, :], ACT.Copy).then_inc(S["xhi_s"], 1)
                for k in range(KD):
                    act.activation(x_T[:, k, :], turn[k][:, :], ACT.Copy).then_inc(S["xT_s"], 1)

            evacuate(0)
            with act.Fori(0, NT // FL) as it:
                units(it, 0, 0)
                act.wait_ge(route, act.snap(it * ROUTE + 3))
                act.activation(e_val[:, :, :], e_arg[:, :, :], ACT.Exp).then_inc(S["exp_s"], 1)
                with act.Fori(0, NEXP // 2) as pair:
                    units(it, 2 * pair + 1, 1)
                    units(it, 2 * pair + 2, 0)
                evacuate(it + 1)

        @block.vector
        def _(dve):
            first(dve, "dve")
            dve.sem_inc(S["sum_s"], SUM0 - 1)
            V = nc.vector

            def units(it, e, half):
                for i in range(KI):
                    u = dve.snap(it * NU + e * KI + i + 2)
                    dve.wait_ge(S["silu_s"], u)
                    dve.tensor_tensor(hidden[buf(half, i)][:, :], silu[buf(half, i)][:, :], up_p[buf(half, i)][:, :], ALU.mult).then_inc(S["hid_s"], 1)
                    dve.wait_ge(S["hhi_s"], u)
                    dve.tensor_tensor(hid_lo[:, half * KI + i, :], hidden[buf(half, i)][:, :], hid_hi[:, half * KI + i, :], ALU.subtract)\
                        .then_inc(S["hlo_s"], 1)

            def down(it, e):
                for l in lanes:
                    base = it * (NEXP * FL) + e * FL + l
                    if l % 2 == 0:
                        dve.wait_ge(S["out_s"], dve.snap(base + 3))
                    dve.wait_ge(S["sum_s"], dve.snap(base + 1 + SUM0 - FL))
                    dve.scalar_tensor_tensor(out=res[l][:, :], in0=out_p[l // 2][:, (l % 2) * D:(l % 2 + 1) * D], scalar=share[0][:, l, bass.ds(e, 1)],
                                             in1=res[l][:, :], op0=ALU.mult, op1=ALU.add).then_inc(S["sum_s"], 1)

            def norm(f):
                n = lane_counts(dve, f)
                for l in lanes:
                    dve.bn_stats(stats[l][:, :], x[:, value(dve, f * FL + l), :]).then_inc(S["stats_s"], 1)
                for l in lanes:
                    dve.wait_ge(S["stats_s"], n[l + 1])
                    dve.sem_inc(S["fence"], 1)
                    dve.bn_aggr(mv[l][:, :], stats[l][:, :]).then_inc(S["mv_s"], 1)
                for l in lanes:
                    dve.wait_ge(S["mv_s"], n[l + 1])
                    dve.wait_ge(S["rstd_s"], n[l + 1])
                    dve.tensor_scalar(x_norm[l][:, :], x[:, value(dve, f * FL + l), :], mv[l][:, 0:1], rstd[l][:, 0:1],
                                      ALU.subtract, ALU.mult).then_inc(S["xn_s"], 1)

            def low_parts(f):
                for k in range(KD):
                    dve.wait_ge(S["xT_s"], value(dve, f * KD + k + 2))
                    dve.tensor_tensor(x_T_lo[:, k, :], turn[k][:, :], x_T_hi[:, k, :], ALU.subtract).then_inc(S["lo_s"], 1)

            dve.memset(x[:, NT:, :], 0.0).then_inc(S["res_s"], 1)
            dve.wait_ge(S["res_s"], 2)
            norm(0)
            low_parts(0)
            with dve.Fori(0, NT // FL) as it:
                n = lane_counts(dve, it)
                dve.wait_ge(S["back_s"], n[0])
                dve.sem_inc(S["fence"], 1)
                for l in lanes:
                    dve.tensor_copy(res[l][:, :], x[:, dve.snap(it * FL + l), :]).then_inc(S["res_s"], 1)
                norm(it + 1)
                units(it, 0, 0)
                link = Chain(dve, route, dve.snap(it * ROUTE), ROUTE)
                dve.wait_ge(S["logit_s"], dve.snap(it + 2))
                link(V.tensor_copy(logit[:, :, :], turn[0][:, 0:FL * 16].rearrange("p (t e) -> p t e", t=FL)[:, :, 0:NEXP]))
                V.tensor_copy(score[:, :].rearrange("p (t e) -> p t e", t=FL), logit[:, :, 0:NR])
                V.tensor_scalar(e_arg[:, :, NR], logit[:, :, NR], -80.0, -1.0, ALU.max, ALU.mult)
                link(V.reduce_max(top[:, :], logit[:, :, 0:NR], axis=AX_X))
                link(V.tensor_tensor(e_arg[:, :, 0:NR], logit[:, :, 0:NR], top[:, :, None].broadcast_to([P, FL, NR]), ALU.subtract))
                for l in lanes:
                    ins = V.tensor_copy(other[:, l * NR:(l + 1) * NR, :],
                                        score[:, l * NR:(l + 1) * NR][:, None, :].broadcast_to([P, NR, NR]))
                link(ins)
                mine = score[:, :, None].broadcast_to([P, FL * NR, NR])
                V.tensor_tensor(above[:, :, :], other[:, :, :], mine, ALU.is_gt)
                link(V.tensor_tensor(not_below[:, :, :], other[:, :, :], mine, ALU.is_ge))
                link(V.tensor_tensor(not_below[:, :, :], not_below[:, :, :], above[:, :, :], ALU.subtract))
                link(V.tensor_tensor(not_below[:, :, :], not_below[:, :, :], before[:, :].rearrange("p (e j) -> p e j", j=NR), ALU.mult))
                link(V.tensor_tensor(above[:, :, :], above[:, :, :], not_below[:, :, :], ALU.add))
                link(V.reduce_sum(rank[:, :], above[:, :, :], axis=AX_X))
                link(V.tensor_scalar(chosen[:, :], rank[:, :], float(TOPK), None, ALU.is_lt))
                dve.wait_ge(S["exp_s"], dve.snap(it + 2))
                V.tensor_scalar(shared_d[:, :], e_val[:, :, NR], 1.0, None, ALU.add)
                link(V.tensor_tensor(share[0][:, :, 0:NR], e_val[:, :, 0:NR], chosen[:, :].rearrange("p (t e) -> p t e", t=FL), ALU.mult))
                V.reciprocal(share[0][:, :, NR], shared_d[:, :])
                link(V.reduce_sum(total[:, :], share[0][:, :, 0:NR], axis=AX_X))
                link(V.reciprocal(inv_total[:, :], total[:, :]))
                link(V.tensor_tensor(share[0][:, :, 0:NR], share[0][:, :, 0:NR], inv_total[:, :, None].broadcast_to([P, FL, NR]), ALU.mult))
                link.close()

                dve.wait_ge(S["res_s"], dve.snap(it * FL + FL + 2))
                dve.sem_inc(S["fence"], 1)
                with dve.Fori(0, NEXP // 2) as pair:
                    units(it, 2 * pair + 1, 1)
                    down(it, 2 * pair)
                    units(it, 2 * pair + 2, 0)
                    down(it, 2 * pair + 1)
                low_parts(it + 1)
                down(it, NEXP - 1)
                for l in lanes:
                    dve.wait_ge(S["sum_s"], dve.snap(it * (NEXP * FL) + (NEXP - 1) * FL + l + 1 + SUM0))
                    dve.sem_inc(S["fence"], 1)
                    dve.tensor_copy(x[:, dve.snap(it * FL + l), :], res[l][:, :]).then_inc(S["back_s"], 1)


def cap_array():
    r, c = np.arange(P)[:, None], np.arange(P)[None, :]
    return np.where((r < c) & (r // CH == c // CH), 3e38, -1e30).astype(np.float32)


def last_row_arrays():
    out = np.zeros((2, P, P), np.float32)
    for c in range(2):
        out[c, (c + 1) * CH - 1] = 1.0
    return out


def layouts(a):
    out = {
        "x": a["L0_attn_out"].reshape(B * T, D),
        "masks": mask_arrays(),
        "w_write": a["L0_attn_W_write"].T,
        "w_alpha_rows": a["L0_attn_W_alpha"],
        "cap": cap_array(),
        "last_row": last_row_arrays(),
        "w_beta": a["L0_attn_W_beta"].T,
        "w_read": a["L0_attn_W_read"].T,
        "a_log": a["L0_attn_A_log"],
        "dt_bias": a["L0_attn_dt_bias"],
        "small": np.repeat(np.array([[-0.5, -0.5, EPS, EPS, 0.5]], np.float32), P, 0),
    }
    group_of = np.arange(D) // GROUP
    out.update({
        "qweights": a["L0_ffn_qweights"].transpose(0, 2, 1),
        "scales": a["L0_ffn_scales"].transpose(2, 0, 1),
        "spread": (np.arange(D // GROUP)[:, None] == group_of[None, :]).astype(np.float32).reshape(D // GROUP, KD, P),
        "biases": a["L0_ffn_biases"],
        "lora_a": a["L0_ffn_lora_a"].transpose(1, 0, 2),
        "lora_b": a["L0_ffn_lora_b"].transpose(2, 0, 1),
        "ln_gamma": a["L0_ffn_ln_gamma"].reshape(NBLK, KD, P).transpose(2, 0, 1),
        "ln_beta": a["L0_ffn_ln_beta"].reshape(NBLK, KD, P).transpose(2, 0, 1),
    })

    half = HD // 2
    inv_freq = (1.0 / np.power(10000.0, np.arange(half) / half)).astype(np.float32)
    angle = (np.arange(T, dtype=np.float32)[:, None] * inv_freq[None, :]).astype(np.float32).astype(np.float64)
    sines = np.concatenate([-np.sin(angle), np.sin(angle)], 1)
    cosines = np.concatenate([np.cos(angle)] * 2, 1)

    def by_tile(v):
        return v.astype(np.float32).reshape(TPB, P, HD).transpose(1, 0, 2)

    def slices(w):
        return w.reshape(KD, P, -1).transpose(1, 0, 2)

    later = (np.arange(P)[None, :] > np.arange(P)[:, None])
    out.update({
        "w_qkv": slices(np.concatenate([a["L1_attn_Wq"], a["L1_attn_Wk"], a["L1_attn_Wv"]], 1)),
        "w_o": slices(a["L1_attn_Wo"]),
        "cos": by_tile(cosines),
        "sin": by_tile(sines),
        "causal": np.stack([np.where(later, -1e30, 0), np.where(later.T, -1e30, 0)], 1).astype(np.float32),
    })

    def padded(w, axis):
        pad = [(0, 0)] * w.ndim
        pad[axis] = (0, IP - w.shape[axis])
        return np.pad(w, pad)

    gate, up, dn = (np.concatenate([a["L1_ffn_w_" + n], a["L1_ffn_sw_" + n][None]], 0) for n in ("gate", "up", "down"))
    both = np.concatenate([padded(gate, 2), padded(up, 2)], 2)
    earlier = (np.arange(NR)[None, :] < np.arange(NR)[:, None]).astype(np.float32).reshape(1, -1)
    out.update({
        "w_gate_up": both.reshape(NEXP, KD, P, 2 * IP).transpose(0, 2, 1, 3),
        "w_down": padded(dn, 1).reshape(NEXP, KI, P, D).transpose(0, 2, 1, 3),
        "w_route": np.concatenate([a["L1_ffn_gate_w"], a["L1_ffn_shared_gate_w"]], 0).T.reshape(KD, P, NEXP).transpose(1, 0, 2),
        "before": np.repeat(np.tile(earlier, (1, FL)), P, 0),
    })
    return out


def store(nc, x, out_dram):
    with ExitStack() as ctx:
        stored = ctx.enter_context(nc.semaphore("stored"))
        block = ctx.enter_context(nc.Block())

        @block.sync
        def _(sp):
            for b in range(B):
                sp.dma_start(out_dram[b * T:(b + 1) * T, :].rearrange("(t p) d -> p t d", p=P),
                             x[:, b * TPB:(b + 1) * TPB, :]).then_inc(stored, 16)
            sp.wait_ge(stored, 16 * B)


def load_constants(nc, masks, small, dram, x=None):
    with ExitStack() as ctx:
        constants_loaded = ctx.enter_context(nc.semaphore("constants_loaded"))
        ctx.callback(clear_semaphores, nc, [constants_loaded])
        block = ctx.enter_context(nc.Block())

        @block.sync
        def _(sp):
            sp.dma_start(masks[:, :, :], dram["masks"]).then_inc(constants_loaded, 16)
            sp.dma_start(small[:, :], dram["small"]).then_inc(constants_loaded, 16)
            if x is not None:
                sp.dma_start(x[:, 0:NT, :], dram["x"].rearrange("(t p) d -> p t d", p=P)).then_inc(constants_loaded, 16)
            sp.wait_ge(constants_loaded, 48 if x is not None else 32)


def build_program(nc, dram, out_dram, stages):
    with ExitStack() as ctx:
        x = ctx.enter_context(nc.sbuf_tensor("x", [P, NT + FL, D], F32))
        masks = ctx.enter_context(nc.sbuf_tensor("masks", [P, len(MASKS), P], F32))
        small = ctx.enter_context(nc.sbuf_tensor("small", [P, 5], F32))
        ident = masks[:, 0, :]
        if 1 in stages:
            with ExitStack() as c2:
                cums = c2.enter_context(nc.sbuf_tensor("cums", [P, NT, NCUM], F32))
                load_constants(nc, masks, small, dram)
                first_norm(nc, x, small, dram, cums)
                decay_sums(nc, x, ident, small, dram, cums)
                delta_attention(nc, x, ident, masks, small, dram, cums)
        else:
            load_constants(nc, masks, small, dram, x)
        if 2 in stages:
            quantised_ffn(nc, x, ident, small, dram)
        if 3 in stages:
            gqa_attention(nc, x, ident, small, dram)
        if 4 in stages:
            moe_ffn(nc, x, ident, small, dram)
        store(nc, x, out_dram)


STAGES = (1, 2, 3, 4)


def kernel(**inputs):
    import concourse.bacc as bacc
    from concourse.bass_utils import run_bass_kernel_spmd as run

    a = {k: np.asarray(v) for k, v in inputs.items()}
    arrays = layouts(a)
    nc = bacc.Bacc("TRN2", target_bir_lowering=False, num_devices=1)
    dram, feed = {}, {}
    for name, value in arrays.items():
        value = np.ascontiguousarray(value)
        feed["in_" + name] = value
        dram[name] = nc.dram_tensor("in_" + name, value.shape, mybir.dt.from_np(value.dtype), kind="ExternalInput").ap()
    out = nc.dram_tensor("out", (B * T, D), F32, kind="ExternalOutput").ap()
    build_program(nc, dram, out, STAGES)
    got = run(nc, [feed], core_ids=[0]).results[0]["out"]
    return got.reshape(B, T, D)
```
